# Optimizing a Trainium2 kernel written in Bass

```python
import numpy as np
import jax
import jax.numpy as jnp

def _softmax(x, axis=-1):
    return jax.nn.softmax(x, axis=axis)

def _gelu(x):
    return jax.nn.gelu(x, approximate=True)

def _silu(x):
    return jax.nn.silu(x)

def _sigmoid(x):
    return jax.nn.sigmoid(x)

def _layernorm(x, axis=-1, eps=1e-05):
    m = jnp.mean(x, axis=axis, keepdims=True)
    v = jnp.var(x, axis=axis, keepdims=True)
    return (x - m) / jnp.sqrt(v + eps)

def _scatter_add(tgt, idx, src, axis=0):
    return tgt.at[idx].add(src)

def _segment_sum(src, seg, n):
    return jax.ops.segment_sum(src, seg, n)
kernel_name = 'mk_recurrent_d1_jaxref_r2_6e5b17'

def setup_inputs(seed: int=0):
    np.random.seed(seed)
    _w = jnp.asarray

    def _L0_attn_setup():
        import jax, jax.numpy as jnp
        import numpy as np
        D_MODEL = 512
        D_STATE = 128
        HEADDIM = 64
        EXPAND = 2
        CHUNK = 64
        D_CONV = 4
        D_INNER = EXPAND * D_MODEL
        NHEADS = D_INNER // HEADDIM
        D_IN_PROJ = 2 * D_INNER + 2 * D_STATE + NHEADS
        CONV_CH = D_INNER + 2 * D_STATE
        EPS = 1e-05

        def segsum(x):
            T = x.shape[-1]
            m1 = jnp.tril(jnp.ones((T, T), bool), -1)
            xr = jnp.where(m1, x[..., :, None], 0.0)
            s = jnp.cumsum(xr, axis=-2)
            m0 = jnp.tril(jnp.ones((T, T), bool), 0)
            return jnp.where(m0, s, -jnp.inf)

        def ssd(x, A, B, C, chunk):
            b, L, h, p = x.shape
            c = L // chunk
            x = x.reshape(b, c, chunk, h, p)
            A = A.reshape(b, c, chunk, h).transpose(0, 3, 1, 2)
            B = B.reshape(b, c, chunk, -1)
            C = C.reshape(b, c, chunk, -1)
            A_cum = jnp.cumsum(A, axis=-1)
            Lm = jnp.exp(segsum(A))
            Y_diag = jnp.einsum('bcln,bcsn,bhcls,bcshp->bclhp', C, B, Lm, x)
            decay_states = jnp.exp(A_cum[:, :, :, -1:] - A_cum)
            states = jnp.einsum('bcln,bhcl,bclhp->bchpn', B, decay_states, x)
            init = jnp.zeros_like(states[:, :1])
            states = jnp.concatenate([init, states], axis=1)
            Ac_last = jnp.pad(A_cum[:, :, :, -1], ((0, 0), (0, 0), (1, 0)))
            decay_chunk = jnp.exp(segsum(Ac_last))
            new_states = jnp.einsum('bhzc,bchpn->bzhpn', decay_chunk, states)
            states = new_states[:, :-1]
            sdo = jnp.exp(A_cum)
            Y_off = jnp.einsum('bcln,bchpn,bhcl->bclhp', C, states, sdo)
            return (Y_diag + Y_off).reshape(b, L, h, p)
        key = jax.random.key(seed)
        ks = jax.random.split(key, 8)
        return {'u': jax.random.normal(ks[0], (2, 2048, D_MODEL), jnp.float32), 'W_in': jax.random.normal(ks[1], (D_MODEL, D_IN_PROJ), jnp.float32) * 0.02, 'conv_w': jax.random.normal(ks[2], (CONV_CH, D_CONV), jnp.float32) * 0.3, 'conv_b': jax.random.normal(ks[3], (CONV_CH,), jnp.float32) * 0.1, 'dt_bias': jax.random.normal(ks[4], (NHEADS,), jnp.float32), 'A_log': jax.random.normal(ks[5], (NHEADS,), jnp.float32) * 0.5, 'D': jax.random.normal(ks[6], (NHEADS,), jnp.float32), 'norm_w': jnp.ones((D_INNER,), jnp.float32), 'W_out': jax.random.normal(ks[7], (D_INNER, D_MODEL), jnp.float32) * 0.02}
    _L0_attn_in = _L0_attn_setup()

    def _L0_ffn_setup():
        import jax, jax.numpy as jnp
        import numpy as np
        DIM = 512

        def _reference_tuple_inner(x, W_r, W_k, W_v, mu_r, mu_k):
            B, T, C = x.shape
            x_prev = jnp.concatenate([jnp.zeros((B, 1, C), x.dtype), x[:, :-1, :]], axis=1)
            xr = mu_r * x + (1.0 - mu_r) * x_prev
            xk = mu_k * x + (1.0 - mu_k) * x_prev
            r = jax.nn.sigmoid(jnp.einsum('btc,dc->btd', xr, W_r))
            k = jnp.einsum('btc,dc->btd', xk, W_k)
            k_act = jnp.square(jax.nn.relu(k))
            out = r * jnp.einsum('btc,dc->btd', k_act, W_v)
            new_state = x[:, -1, :]
            return (out, new_state)
        key = jax.random.key(seed)
        ks = jax.random.split(key, 6)
        B, T, C = (8, 1024, DIM)
        x = jax.random.normal(ks[0], (B, T, C), dtype=jnp.float32)
        s = 1.0 / np.sqrt(C)
        W_r = jax.random.uniform(ks[1], (C, C), jnp.float32, -s, s)
        W_k = jax.random.uniform(ks[2], (C, C), jnp.float32, -s, s)
        W_v = jax.random.uniform(ks[3], (C, C), jnp.float32, -s, s)
        mu_r = jax.random.uniform(ks[4], (C,), jnp.float32)
        mu_k = jax.random.uniform(ks[5], (C,), jnp.float32)
        return {'x': x, 'W_r': W_r, 'W_k': W_k, 'W_v': W_v, 'mu_r': mu_r, 'mu_k': mu_k}
    _L0_ffn_in = _L0_ffn_setup()
    _d = {'L0_attn_u': _L0_attn_in['u'], 'L0_attn_W_in': _L0_attn_in['W_in'], 'L0_attn_conv_w': _L0_attn_in['conv_w'], 'L0_attn_conv_b': _L0_attn_in['conv_b'], 'L0_attn_dt_bias': _L0_attn_in['dt_bias'], 'L0_attn_A_log': _L0_attn_in['A_log'], 'L0_attn_D': _L0_attn_in['D'], 'L0_attn_norm_w': _L0_attn_in['norm_w'], 'L0_attn_W_out': _L0_attn_in['W_out'], 'L0_ffn_W_r': _L0_ffn_in['W_r'], 'L0_ffn_W_k': _L0_ffn_in['W_k'], 'L0_ffn_W_v': _L0_ffn_in['W_v'], 'L0_ffn_mu_r': _L0_ffn_in['mu_r'], 'L0_ffn_mu_k': _L0_ffn_in['mu_k']}
    _x0 = _d['L0_attn_u']
    _d['L0_attn_u'] = jax.random.normal(jax.random.fold_in(jax.random.key(seed), 1), (2, 4096, 512), dtype=_x0.dtype)
    del _x0
    return _d

def reference(L0_attn_u, L0_attn_W_in, L0_attn_conv_w, L0_attn_conv_b, L0_attn_dt_bias, L0_attn_A_log, L0_attn_D, L0_attn_norm_w, L0_attn_W_out, L0_ffn_W_r, L0_ffn_W_k, L0_ffn_W_v, L0_ffn_mu_r, L0_ffn_mu_k):

    def _L0_attn_ref(u, W_in, conv_w, conv_b, dt_bias, A_log, D, norm_w, W_out):
        import jax, jax.numpy as jnp
        import numpy as np
        D_MODEL = 512
        D_STATE = 128
        HEADDIM = 64
        EXPAND = 2
        CHUNK = 64
        D_CONV = 4
        D_INNER = EXPAND * D_MODEL
        NHEADS = D_INNER // HEADDIM
        D_IN_PROJ = 2 * D_INNER + 2 * D_STATE + NHEADS
        CONV_CH = D_INNER + 2 * D_STATE
        EPS = 1e-05

        def segsum(x):
            T = x.shape[-1]
            m1 = jnp.tril(jnp.ones((T, T), bool), -1)
            xr = jnp.where(m1, x[..., :, None], 0.0)
            s = jnp.cumsum(xr, axis=-2)
            m0 = jnp.tril(jnp.ones((T, T), bool), 0)
            return jnp.where(m0, s, -jnp.inf)

        def ssd(x, A, B, C, chunk):
            b, L, h, p = x.shape
            c = L // chunk
            x = x.reshape(b, c, chunk, h, p)
            A = A.reshape(b, c, chunk, h).transpose(0, 3, 1, 2)
            B = B.reshape(b, c, chunk, -1)
            C = C.reshape(b, c, chunk, -1)
            A_cum = jnp.cumsum(A, axis=-1)
            Lm = jnp.exp(segsum(A))
            Y_diag = jnp.einsum('bcln,bcsn,bhcls,bcshp->bclhp', C, B, Lm, x)
            decay_states = jnp.exp(A_cum[:, :, :, -1:] - A_cum)
            states = jnp.einsum('bcln,bhcl,bclhp->bchpn', B, decay_states, x)
            init = jnp.zeros_like(states[:, :1])
            states = jnp.concatenate([init, states], axis=1)
            Ac_last = jnp.pad(A_cum[:, :, :, -1], ((0, 0), (0, 0), (1, 0)))
            decay_chunk = jnp.exp(segsum(Ac_last))
            new_states = jnp.einsum('bhzc,bchpn->bzhpn', decay_chunk, states)
            states = new_states[:, :-1]
            sdo = jnp.exp(A_cum)
            Y_off = jnp.einsum('bcln,bchpn,bhcl->bclhp', C, states, sdo)
            return (Y_diag + Y_off).reshape(b, L, h, p)
        b, L, _ = u.shape
        zxbcdt = u @ W_in
        z = zxbcdt[..., :D_INNER]
        xBC = zxbcdt[..., D_INNER:D_INNER + CONV_CH]
        dt = jax.nn.softplus(zxbcdt[..., -NHEADS:] + dt_bias)
        xc = jnp.pad(xBC.transpose(0, 2, 1), ((0, 0), (0, 0), (D_CONV - 1, 0)))
        xc = jax.lax.conv_general_dilated(xc, conv_w[:, None, :], (1,), 'VALID', feature_group_count=CONV_CH, dimension_numbers=('NCH', 'OIH', 'NCH')) + conv_b[None, :, None]
        xBC = jax.nn.silu(xc.transpose(0, 2, 1))
        x = xBC[..., :D_INNER].reshape(b, L, NHEADS, HEADDIM)
        B = xBC[..., D_INNER:D_INNER + D_STATE]
        C = xBC[..., D_INNER + D_STATE:]
        A = -jnp.exp(A_log)
        y = ssd(x * dt[..., None], A * dt, B, C, CHUNK)
        y = y + x * D[:, None]
        y = y.reshape(b, L, D_INNER)
        y = y * jax.nn.silu(z)
        y = y * jax.lax.rsqrt(jnp.mean(y * y, axis=-1, keepdims=True) + EPS) * norm_w
        return y @ W_out

    def _L0_ffn_ref(x, W_r, W_k, W_v, mu_r, mu_k):
        import jax, jax.numpy as jnp
        import numpy as np
        DIM = 512

        def _reference_tuple_inner(x, W_r, W_k, W_v, mu_r, mu_k):
            B, T, C = x.shape
            x_prev = jnp.concatenate([jnp.zeros((B, 1, C), x.dtype), x[:, :-1, :]], axis=1)
            xr = mu_r * x + (1.0 - mu_r) * x_prev
            xk = mu_k * x + (1.0 - mu_k) * x_prev
            r = jax.nn.sigmoid(jnp.einsum('btc,dc->btd', xr, W_r))
            k = jnp.einsum('btc,dc->btd', xk, W_k)
            k_act = jnp.square(jax.nn.relu(k))
            out = r * jnp.einsum('btc,dc->btd', k_act, W_v)
            new_state = x[:, -1, :]
            return (out, new_state)
        return _reference_tuple_inner(x, W_r, W_k, W_v, mu_r, mu_k)[0]
    x = L0_attn_u
    xn = _layernorm(x, axis=-1)
    s = _L0_attn_ref(xn, L0_attn_W_in, L0_attn_conv_w, L0_attn_conv_b, L0_attn_dt_bias, L0_attn_A_log, L0_attn_D, L0_attn_norm_w, L0_attn_W_out)
    g = _silu(_L0_ffn_ref(xn, L0_ffn_W_r, L0_ffn_W_k, L0_ffn_W_v, L0_ffn_mu_r, L0_ffn_mu_k))
    x = x + s * g
    return x

_drawn_inputs = setup_inputs


def setup_inputs(seed=0):
    import zlib

    import numpy as np

    out = dict(_drawn_inputs(seed))
    spreads = {'L0_attn_norm_w': (1.0, 0.6)}
    factors = {'L0_attn_conv_b': 5.623,
     'L0_attn_dt_bias': 8.0,
     'L0_attn_A_log': 8.0,
     'L0_ffn_W_r': 8.0,
     'L0_ffn_mu_r': 8.0,
     'L0_ffn_mu_k': 3.721,
     'L0_attn_D': 6.586}
    for name, (base, spread) in spreads.items():
        noise = np.random.default_rng([zlib.crc32(name.encode()), seed]).standard_normal(out[name].shape)
        drawn = base * np.exp(spread * noise) if base else spread * noise
        out[name] = jnp.asarray(drawn.astype(out[name].dtype))
    for name, factor in factors.items():
        out[name] = (out[name] * factor).astype(out[name].dtype)
    return out
```

```python
import concourse.bass as bass
from concourse import mybir
from contextlib import ExitStack

F32 = mybir.dt.float32
F32R = mybir.dt.float32r
ALU = mybir.AluOpType
ACT = mybir.ActivationFunctionType
P = 128
DM = 512
KD = DM // P
LN_EPS = 1e-5


def apart(eng, passed):
    eng.sem_inc(passed)


def column(ap):
    return ap.rearrange("(k p) -> p k", p=P)


def ffn_phase(nc, u_rows, w_r, w_k, w_v, mu_r, mu_k, gate_rows, ident, ln_scale, ln_shift, n_tok, n_batch):
    T = 512
    C = T // P
    N = n_tok // T
    N_PER_BATCH = N // n_batch

    ctx = ExitStack()
    with ctx:
        def sb(name, shape, dt=F32):
            return ctx.enter_context(nc.sbuf_tensor("f_" + name, shape, dt))

        def ps(name):
            return ctx.enter_context(nc.psum_tensor("f_" + name, [P, 512], F32))

        def sem(name):
            return ctx.enter_context(nc.semaphore("f_" + name))

        w_hi = {n: sb(f"w{n}_hi", [P, KD, DM], F32R) for n in "rkv"}
        w_lo = {n: sb(f"w{n}_lo", [P, KD, DM], F32R) for n in "rkv"}
        mu = {"r": sb("mu_r", [P, KD]), "k": sb("mu_k", [P, KD])}
        keep = sb("keep", [P, N])
        keep_now = sb("keep_now", [P, 1])
        minus_half = sb("minus_half", [P, C])
        minus_one = sb("minus_one", [P, C])
        eps = sb("eps", [P, C])

        u = sb("u", [P, C, DM])
        bn = sb("bn", [P, C, 6])
        mv = sb("mv", [P, C, 2])
        ve = sb("ve", [P, C])
        scale = sb("scale", [P, C])
        mean_scaled = sb("mean_scaled", [P, C])
        shift = sb("shift", [P, C])
        xn = sb("xn", [P, C, DM])
        xt = sb("xt", [P, KD, T + 1])
        dt_ = sb("dt", [P, KD, T])
        mixed = sb("mixed", [P, 2 * KD, T])
        x_hi = {n: sb(f"x{n}_hi", [P, KD, T], F32R) for n in "rk"}
        x_lo = {n: sb(f"x{n}_lo", [P, KD, T], F32R) for n in "rk"}
        kr = sb("kr", [P, KD, T])
        ka = sb("ka", [P, KD, T])
        ka_hi = sb("ka_hi", [P, KD, T], F32R)
        ka_lo = sb("ka_lo", [P, KD, T], F32R)
        tr = sb("tr", [P, C, DM])
        f2 = sb("f2", [P, C, DM])
        tg = sb("tg", [P, C, DM])
        g4 = sb("g4", [P, C, DM])

        ps_t = [ps("ps_t0"), ps("ps_t1")]
        ps_k = [ps("ps_k0"), ps("ps_k1")]
        ps_r = [ps("ps_r0"), ps("ps_r1")]
        ps_v = [ps("ps_v0"), ps("ps_v1")]

        w_loaded = {n: sem(f"w{n}_loaded") for n in "rkv"}
        mu_loaded = sem("mu_loaded")
        consts_set = sem("consts_set")
        w_turned = sem("w_turned")
        w_hi_set = sem("w_hi_set")
        w_lo_set = sem("w_lo_set")
        u_loaded = sem("u_loaded")
        bn_done = sem("bn_done")
        mv_done = sem("mv_done")
        pool_step = sem("pool_step")
        ln_done = sem("ln_done")
        xn_done = sem("xn_done")
        turned = sem("turned")
        xt_done = sem("xt_done")
        keep_set = sem("keep_set")
        edge_done = sem("edge_done")
        diff_done = sem("diff_done")
        mixed_done = sem("mixed_done")
        hi_done = sem("hi_done")
        lo_done = sem("lo_done")
        k_done = sem("k_done")
        kr_done = sem("kr_done")
        ka_done = sem("ka_done")
        kahi_done = sem("kahi_done")
        kalo_done = sem("kalo_done")
        r_done = sem("r_done")
        tr_done = sem("tr_done")
        v_done = sem("v_done")
        f2_done = sem("f2_done")
        tg_done = sem("tg_done")
        g4_done = sem("g4_done")
        g_stored = sem("g_stored")
        passed = sem("passed")
        dve_passed = sem("dve_passed")

        w_raw = {"r": mixed[:, 0:KD, :], "k": mixed[:, KD:2 * KD, :], "v": xn[:, :, :]}
        W_SRC = {"r": w_r, "k": w_k, "v": w_v}

        def u_tile(n):
            return u_rows[bass.ds(n * T, T), :].rearrange("(c p) d -> p c d", p=P)

        def g_tile(n):
            return gate_rows[bass.ds(n * T, T), :].rearrange("(c p) d -> p c d", p=P)

        block = ctx.enter_context(nc.Block())

        @block.sync
        def _(sp):
            for n in "rkv":
                sp.dma_start(w_raw[n], W_SRC[n].rearrange("(o p) c -> p o c", p=P)).then_inc(w_loaded[n], 16)
            sp.dma_start(u[:, :, :], u_tile(0)).then_inc(u_loaded, 16)
            sp.dma_start(mu["r"][:, :], column(mu_r), allow_slow_non_contiguous=True).then_inc(mu_loaded, 16)
            sp.dma_start(mu["k"][:, :], column(mu_k), allow_slow_non_contiguous=True).then_inc(mu_loaded, 16)
            sp.wait_ge(xn_done, C)
            sp.dma_start(u[:, :, :], u_tile(1)).then_inc(u_loaded, 16)
            with sp.Fori(0, N - 2) as n:
                sp.wait_ge(xn_done, (n + 2) * C)
                sp.dma_start(u[:, :, :], u_tile(n + 2)).then_inc(u_loaded, 16)
                sp.wait_ge(g4_done, (n + 1) * C)
                sp.dma_start(g_tile(n), g4[:, :, :]).then_inc(g_stored, 16)
            for n in (N - 2, N - 1):
                sp.wait_ge(g4_done, (n + 1) * C)
                sp.dma_start(g_tile(n), g4[:, :, :]).then_inc(g_stored, 16)
            sp.wait_ge(g_stored, 16 * N)

        @block.gpsimd
        def _(pool):
            pool.memset(keep[:, :], 1.0).then_inc(pool_step, 1)
            pool.memset(minus_half[:, :], -0.5).then_inc(consts_set, 1)
            pool.memset(minus_one[:, :], -1.0).then_inc(consts_set, 1)
            pool.memset(eps[:, :], LN_EPS).then_inc(consts_set, 1)
            pool.memset(xt[:, :, T:T + 1], 0.0).then_inc(consts_set, 1)
            pool.wait_ge(pool_step, 1)
            for b in range(1, n_batch):
                pool.memset(keep[:, b * N_PER_BATCH:b * N_PER_BATCH + 1], 0.0).then_inc(consts_set, 1)
            pool.wait_ge(consts_set, 3 + n_batch)

            STEPS = 4

            def norm(n, first_tile=False):
                first = 1 + n * STEPS
                pool.wait_ge(mv_done, n + 1)
                nc.gpsimd.tensor_tensor(ve[:, :], mv[:, :, 1], eps[:, :], ALU.add).then_inc(pool_step, 1)
                pool.wait_ge(pool_step, first + 1)
                if not first_tile:
                    pool.wait_ge(xn_done, n * C)
                nc.gpsimd.tensor_tensor(scale[:, :], ve[:, :], minus_half[:, :], ALU.pow).then_inc(pool_step, 1)
                pool.wait_ge(pool_step, first + 2)
                nc.gpsimd.tensor_tensor(mean_scaled[:, :], mv[:, :, 0], scale[:, :], ALU.mult).then_inc(pool_step, 1)
                pool.wait_ge(pool_step, first + 3)
                nc.gpsimd.tensor_tensor(shift[:, :], mean_scaled[:, :], minus_one[:, :], ALU.mult)\
                    .then_inc(pool_step, 1)
                pool.wait_ge(pool_step, first + 4)
                apart(pool, passed)
                nc.gpsimd.tensor_copy(ln_scale[:, bass.ds(n * C, C)], scale[:, :]).then_inc(ln_done, 1)
                nc.gpsimd.tensor_copy(ln_shift[:, bass.ds(n * C, C)], shift[:, :]).then_inc(ln_done, 1)

            def edge_and_diff(n, first_tile=False):
                if not first_tile:
                    pool.wait_ge(edge_done, n)
                    pool.wait_ge(mixed_done, n * 2 * KD)
                    apart(pool, passed)
                nc.gpsimd.tensor_copy(keep_now[:, :], keep[:, bass.ds(n, 1)]).then_inc(keep_set, 1)
                pool.wait_ge(keep_set, n + 1)
                nc.gpsimd.tensor_tensor(xt[:, :, 0:1], xt[:, :, T:T + 1],
                                        keep_now[:, :].unsqueeze(1).to_broadcast([P, KD, 1]), ALU.mult)\
                    .then_inc(edge_done, 1)
                pool.wait_ge(edge_done, n + 1)
                for k in range(KD):
                    pool.wait_ge(xt_done, n * KD + k + 1)
                    nc.gpsimd.tensor_tensor(dt_[:, k, :], xt[:, k, 1:T + 1], xt[:, k, 0:T], ALU.subtract)\
                        .then_inc(diff_done, 1)

            norm(0, first_tile=True)
            edge_and_diff(0, first_tile=True)
            with pool.Fori(0, N - 1) as n:
                norm(n + 1)
                edge_and_diff(n + 1)

        @block.scalar
        def _(act):
            for i, w in enumerate("rkv"):
                for k in range(KD):
                    act.wait_ge(w_turned, i * KD + k + 1)
                    nc.scalar.activation(w_hi[w][:, k, :], ps_t[k % 2][:, :], ACT.Copy).then_inc(w_hi_set, 1)

            def normalise(n, first_tile=False):
                act.wait_ge(ln_done, 2 * (n + 1))
                act.wait_ge(u_loaded, 16 * (n + 1))
                if not first_tile:
                    act.wait_ge(turned, n * KD)
                else:
                    act.wait_ge(w_turned, 3 * KD)
                for c in range(C):
                    nc.scalar.activation(xn[:, c, :], u[:, c, :], ACT.Identity, bias=shift[:, c:c + 1],
                                         scale=scale[:, c:c + 1]).then_inc(xn_done, 1)

            def columns(n):
                act.wait_ge(edge_done, n + 1)
                for k in range(KD):
                    act.wait_ge(turned, n * KD + k + 1)
                    nc.scalar.activation(xt[:, k, 1:T + 1], ps_t[k % 2][:, :], ACT.Copy).then_inc(xt_done, 1)

            def high(n, w, first_tile=False):
                base = KD * "kr".index(w)
                if not first_tile:
                    act.wait_ge(k_done if w == "k" else r_done, n * KD)
                for k in range(KD):
                    act.wait_ge(mixed_done, n * 2 * KD + base + k + 1)
                    nc.scalar.activation(x_hi[w][:, k, :], mixed[:, base + k, :], ACT.Copy).then_inc(hi_done, 1)

            def tanh_gate(n, c):
                act.wait_ge(f2_done, n * C + c + 1)
                nc.scalar.activation(tg[:, c, :], f2[:, c, :], ACT.Tanh, scale=0.25).then_inc(tg_done, 1)

            def body(n, first_tile, last_tile):
                for m in range(KD + 1):
                    if m < KD:
                        act.wait_ge(k_done, n * KD + m + 1)
                        if not first_tile and m == 0:
                            act.wait_ge(ka_done, n * KD)
                        nc.scalar.activation(kr[:, m, :], ps_k[m % 2][:, :], ACT.Relu).then_inc(kr_done, 1)
                    if m >= 1:
                        act.wait_ge(ka_done, n * KD + m)
                        if not first_tile and m == 1:
                            act.wait_ge(v_done, n * C)
                        nc.scalar.activation(ka_hi[:, m - 1, :], ka[:, m - 1, :], ACT.Copy).then_inc(kahi_done, 1)
                if not last_tile:
                    normalise(n + 1)
                if not first_tile:
                    act.wait_ge(f2_done, n * C)
                for c in range(C):
                    act.wait_ge(r_done, n * C + c + 1)
                    nc.scalar.activation(tr[:, c, :], ps_r[c % 2][:, :], ACT.Tanh, scale=0.5).then_inc(tr_done, 1)
                if not last_tile:
                    columns(n + 1)
                    high(n + 1, "k")
                if not first_tile:
                    act.wait_ge(g4_done, n * C)
                tanh_gate(n, 0)
                tanh_gate(n, 1)
                if not last_tile:
                    high(n + 1, "r")
                tanh_gate(n, 2)
                tanh_gate(n, 3)

            normalise(0, first_tile=True)
            columns(0)
            high(0, "k", first_tile=True)
            high(0, "r", first_tile=True)
            body(0, True, False)
            with act.Fori(1, N - 1) as n:
                body(n, False, False)
            body(N - 1, False, True)

        @block.vector
        def _(dve):
            for i, w in enumerate("rkv"):
                for k in range(KD):
                    dve.wait_ge(w_hi_set, i * KD + k + 1)
                    nc.vector.tensor_tensor(w_lo[w][:, k, :], ps_t[k % 2][:, :], w_hi[w][:, k, :].bitcast(F32),
                                            ALU.subtract).then_inc(w_lo_set, 1)

            def statistics(n, first_tile=False):
                dve.wait_ge(u_loaded, 16 * (n + 1))
                for c in range(C):
                    nc.vector.bn_stats(bn[:, c, :], u[:, c, :]).then_inc(bn_done, 1)
                dve.wait_ge(bn_done, (n + 1) * C)
                if not first_tile:
                    dve.wait_ge(ln_done, 2 * n)
                    apart(dve, dve_passed)
                for c in range(C):
                    last = nc.vector.bn_aggr(mv[:, c, :], bn[:, c, :])
                last.then_inc(mv_done, 1)

            def mix(n, w, first_tile=False):
                base = KD * "kr".index(w)

                def low(k):
                    dve.wait_ge(hi_done, n * 2 * KD + base + k + 1)
                    nc.vector.tensor_tensor(x_lo[w][:, k, :], mixed[:, base + k, :],
                                            x_hi[w][:, k, :].bitcast(F32), ALU.subtract).then_inc(lo_done, 1)

                if not first_tile:
                    dve.wait_ge(lo_done, n * 2 * KD - KD + base)
                    dve.wait_ge(k_done if w == "k" else r_done, n * KD)
                for k in range(KD):
                    dve.wait_ge(diff_done, n * KD + k + 1)
                    nc.vector.scalar_tensor_tensor(mixed[:, base + k, :], dt_[:, k, :], mu[w][:, k:k + 1],
                                                   xt[:, k, 0:T], ALU.mult, ALU.add).then_inc(mixed_done, 1)
                    if k >= 1:
                        low(k - 1)
                low(KD - 1)

            def squares(n, first_tile):
                def low(m):
                    dve.wait_ge(kahi_done, n * KD + m + 1)
                    nc.vector.tensor_tensor(ka_lo[:, m, :], ka[:, m, :], ka_hi[:, m, :].bitcast(F32),
                                            ALU.subtract).then_inc(kalo_done, 1)
                if not first_tile:
                    dve.wait_ge(kalo_done, n * KD)
                    dve.wait_ge(v_done, n * C)
                for m in range(KD):
                    dve.wait_ge(kr_done, n * KD + m + 1)
                    nc.vector.tensor_tensor(ka[:, m, :], kr[:, m, :], kr[:, m, :], ALU.mult).then_inc(ka_done, 1)
                    if m >= 1:
                        low(m - 1)
                low(KD - 1)

            def gated(n, c):
                dve.wait_ge(v_done, n * C + c + 1)
                dve.wait_ge(tr_done, n * C + c + 1)
                nc.vector.scalar_tensor_tensor(f2[:, c, :], tr[:, c, :], 1.0, ps_v[c % 2][:, :], ALU.add,
                                               ALU.mult).then_inc(f2_done, 1)

            def silu_gate(n, c):
                dve.wait_ge(tg_done, n * C + c + 1)
                nc.vector.scalar_tensor_tensor(g4[:, c, :], tg[:, c, :], 1.0, f2[:, c, :], ALU.add,
                                               ALU.mult).then_inc(g4_done, 1)

            def body(n, first_tile, last_tile):
                if not last_tile:
                    statistics(n + 1)
                squares(n, first_tile)
                if not last_tile:
                    mix(n + 1, "k")
                if not first_tile:
                    dve.wait_ge(g4_done, n * C)
                gated(n, 0)
                gated(n, 1)
                if not first_tile:
                    dve.wait_ge(g_stored, 16 * n)
                silu_gate(n, 0)
                silu_gate(n, 1)
                if not last_tile:
                    mix(n + 1, "r")
                gated(n, 2)
                gated(n, 3)
                silu_gate(n, 2)
                silu_gate(n, 3)

            dve.wait_ge(mu_loaded, 32)
            statistics(0, first_tile=True)
            mix(0, "k", first_tile=True)
            mix(0, "r", first_tile=True)
            body(0, True, False)
            with dve.Fori(1, N - 1) as n:
                body(n, False, False)
            body(N - 1, False, True)

        @block.tensor
        def _(pe):
            for i, w in enumerate("rkv"):
                pe.wait_ge(w_loaded[w], 16)
                for k in range(KD):
                    q = i * KD + k
                    if q >= 2:
                        pe.wait_ge(w_lo_set, q - 1)
                    for o in range(KD):
                        last = nc.tensor.transpose(ps_t[k % 2][:, o * P:(o + 1) * P],
                                                   w_raw[w][:, o, k * P:(k + 1) * P], ident[:, :])
                    last.then_inc(w_turned, 1)

            def turn(n, first_tile=False):
                pe.wait_ge(xn_done, (n + 1) * C)
                for k in range(KD):
                    if first_tile and k < 2:
                        pe.wait_ge(w_lo_set, 3 * KD)
                    else:
                        pe.wait_ge(xt_done, n * KD + k - 1)
                    for c in range(C):
                        last = nc.tensor.transpose(ps_t[k % 2][:, c * P:(c + 1) * P], xn[:, c, k * P:(k + 1) * P],
                                                   ident[:, :])
                    last.then_inc(turned, 1)

            def product(out, lhs_hi, lhs_lo, rhs_hi, rhs_lo):
                pairs = [(lhs_hi, rhs_hi), (lhs_hi, rhs_lo), (lhs_lo, rhs_hi)]
                for k in range(KD):
                    for j, (a, b) in enumerate(pairs):
                        last = nc.tensor.matmul(out, a(k), b(k), start=(k == 0 and j == 0),
                                                stop=(k == KD - 1 and j == 2))
                return last

            def body(n, first_tile, last_tile):
                pe.wait_ge(lo_done, n * 2 * KD + KD)
                for m in range(KD):
                    if not (first_tile and m < 2):
                        pe.wait_ge(kr_done, n * KD + m - 1)
                    product(ps_k[m % 2][:, :],
                            lambda k: w_hi["k"][:, k, m * P:(m + 1) * P], lambda k: w_lo["k"][:, k, m * P:(m + 1) * P],
                            lambda k: x_hi["k"][:, k, :], lambda k: x_lo["k"][:, k, :]).then_inc(k_done, 1)
                pe.wait_ge(lo_done, (n + 1) * 2 * KD)
                for c in range(C):
                    if not (first_tile and c < 2):
                        pe.wait_ge(tr_done, n * C + c - 1)
                    product(ps_r[c % 2][:, :],
                            lambda k: x_hi["r"][:, k, c * P:(c + 1) * P], lambda k: x_lo["r"][:, k, c * P:(c + 1) * P],
                            lambda k: w_hi["r"][:, k, :], lambda k: w_lo["r"][:, k, :]).then_inc(r_done, 1)
                if not last_tile:
                    turn(n + 1)
                pe.wait_ge(kalo_done, (n + 1) * KD)
                for c in range(C):
                    if not (first_tile and c < 2):
                        pe.wait_ge(f2_done, n * C + c - 1)
                    product(ps_v[c % 2][:, :],
                            lambda k: ka_hi[:, k, c * P:(c + 1) * P], lambda k: ka_lo[:, k, c * P:(c + 1) * P],
                            lambda k: w_hi["v"][:, k, :], lambda k: w_lo["v"][:, k, :]).then_inc(v_done, 1)

            turn(0, first_tile=True)
            body(0, True, False)
            with pe.Fori(1, N - 1) as n:
                body(n, False, False)
            body(N - 1, False, True)


D_INNER, D_STATE, N_HEAD, HEAD, N_TAP = 1024, 128, 16, 64, 4
RMS_EPS = 1e-5
W_X = D_INNER
W_DT = 2 * D_INNER + 2 * D_STATE
W_ALL = W_DT + N_HEAD


def ssm_phase(nc, u_rows, w_in, conv_w, conv_b, dt_bias, a_log, d_skip, norm_w, w_out, gate_rows, out_rows,
              ident, ln_scale, ln_shift, n_tok, n_batch):
    C = 2
    T = C * P
    N = n_tok // T
    N_PER_BATCH = N // n_batch
    XT = D_INNER // P
    NT = XT + 2
    B_TILE, C_TILE = XT, XT + 1
    ORDER = [B_TILE, C_TILE] + list(range(XT))
    HALF = N_HEAD // 2
    LO = 32

    ctx = ExitStack()
    with ctx:
        def sb(name, shape, dt=F32):
            return ctx.enter_context(nc.sbuf_tensor("s_" + name, shape, dt))

        def ps(name):
            return ctx.enter_context(nc.psum_tensor("s_" + name, [P, 512], F32))

        def sem(name):
            return ctx.enter_context(nc.semaphore("s_" + name))

        w_hi = sb("w_hi", [P, KD, W_ALL], F32R)
        w_lo = sb("w_lo", [P, KD, W_ALL], F32R)
        wo_hi = sb("wo_hi", [P, XT, DM], F32R)
        wo_lo = sb("wo_lo", [P, XT, DM], F32R)
        tri = sb("tri", [P, P])
        pick = sb("pick", [LO + N_HEAD, N_HEAD], F32R)
        ones_row = sb("ones_row", [1, P])
        taps = sb("taps", [P, NT, N_TAP])
        tap_bias = sb("tap_bias", [P, NT])
        dtb = sb("dtb", [N_HEAD, 1])
        head_rows = sb("head_rows", [1, 2 * N_HEAD])
        head_params = sb("head_params", [P, 2 * N_HEAD])
        norm_cols = sb("norm_cols", [P, XT])
        keep = sb("keep", [P, N])
        keep_now = sb("keep_now", [P, 1])
        minus_half = sb("minus_half", [P, 1])
        ones = sb("ones", [P, 1])

        u = sb("u", [P, C, DM])
        residual = sb("residual", [P, C, DM])
        gate = sb("gate", [P, C, DM])
        scale = sb("scale", [P, C])
        shift = sb("shift", [P, C])
        xn = sb("xn", [P, DM])
        x_hi = sb("x_hi", [P, KD, T], F32R)
        x_lo = sb("x_lo", [P, KD, T], F32R)
        raw = sb("raw", [P, 2, T + N_TAP - 1])
        edges = sb("edges", [P, NT, N_TAP - 1])
        acc = sb("acc", [P, 2, T])
        act_x = sb("act_x", [P, 2, T])
        bt = sb("bt", [P, T])
        ct = sb("ct", [P, T])
        b_tok = sb("b_tok", [P, C, D_STATE])
        x_tok = sb("x_tok", [P, C, D_INNER])
        xd = sb("xd", [P, C, D_INNER])
        xdd = sb("xdd", [P, C, D_INNER])
        sp = sb("sp", [P, 6, C * N_HEAD])
        dtv = sb("dtv", [P, C, N_HEAD])
        a_dup = sb("a_dup", [P, C, LO + N_HEAD])
        cum_rows = sb("cum_rows", [N_HEAD, T])
        dt_raw = cum_rows
        cum_parts = sb("cum_parts", [LO + N_HEAD, T], F32R)
        cum = sb("cum", [P, C, N_HEAD])
        grow = sb("grow", [P, C, N_HEAD])
        chunk_decay = sb("chunk_decay", [P, C, N_HEAD])
        tail = sb("tail", [P, C, N_HEAD])
        tail_decay = sb("tail_decay", [P, C, N_HEAD])
        lm = sb("lm", [P, N_HEAD, C, P])
        gm = sb("gm", [P, C, P])
        gz = sb("gz", [P, C, D_INNER])
        part = sb("part", [P, 2, 512])
        state = sb("state", [P, D_INNER])
        ssq = sb("ssq", [P, C])
        rms = sb("rms", [P, C, 2])
        y_hi = sb("y_hi", [P, XT, P], F32R)
        y_lo = sb("y_lo", [P, XT, P], F32R)

        turn_ps = [ps("turn0"), ps("turn1")]
        proj_ps = [ps("proj0"), ps("proj1")]
        cum_ps = ps("cum_ps")
        off_ps = ps("off_ps")
        diag_ps = ps("diag_ps")
        state_ps = ps("state_ps")
        small = turn_ps[0]
        dt_ps = small[0:N_HEAD, 0:T]
        dtt_ps = small[:, 256:288]
        cumr_ps = small[0:LO + N_HEAD, 0:T]
        cumt_ps = small[:, 288:320]
        last_ps = small[:, 320:352]
        pair_ps = turn_ps[1][:, 0:T]

        names = """w0_loaded w1_loaded state_kept keep_set w_hi_set w_lo_set wo_hi_set taps_halved wo_lo_set wo_loaded wo_scaled params_loaded consts pool_step head_ps heads_exp heads_set
            u_loaded rest_loaded out_stored norm_set xn_done turned xhi_done xlo_done
            dt_done dtraw_done dtt_done sp_act sp_step dt_set a_set cumr_done cumrows_done cumhi_done cumlo_done
            cumt_done cum_set grow_set last_done chunk_set tail_set taild_set
            proj_done edge_in raw_done edge_out acc_done tap_done tanh_done conv_done
            pair_done pair_copied xd_done xdd_done skip_done gm_done
            cumb_done relu_done exp_done lm_done z_done tz_done gz_done
            off_done st_done diag_done decayed state_set part_off part_sum sum_done y_done sq_done rms_step
            y_turned yhi_done ylo_done out_done o_mult o_done
            pool_passed pe_passed sp_passed""".split()
        S = {n: sem(n) for n in names}

        def rows(t, n):
            return t[bass.ds(n * T, T), :].rearrange("(c p) d -> p c d", p=P)

        def heads(ap):
            return ap.unsqueeze(-1).to_broadcast([P, ap.shape[-1], HEAD])

        STAGE = [lm[:, :, :, :].rearrange("p h c l -> p (h c l)"),
                 x_tok[:, :, :].rearrange("p c d -> p (c d)")]
        STAGE2 = [xd[:, :, :].rearrange("p c d -> p (c d)"), xdd[:, :, :].rearrange("p c d -> p (c d)")]

        block = ctx.enter_context(nc.Block())

        @block.sync
        def _(sp_):
            wv = w_in.rearrange("(k p) n -> k p n", p=P)
            WH = W_ALL // 2
            for k in range(KD):
                for h in range(2):
                    q = 2 * k + h
                    if q >= 2:
                        sp_.wait_ge(S["w_lo_set"], q - 1)
                    sp_.dma_start(STAGE2[h][:, 0:WH], wv[k, :, h * WH:(h + 1) * WH]).then_inc(S[f"w{h}_loaded"], 16)
            sp_.dma_start(STAGE[0][:, 0:XT * DM].rearrange("p (j d) -> p j d", d=DM),
                          w_out.rearrange("(j p) d -> p j d", p=P)).then_inc(S["wo_loaded"], 16)
            slow = dict(allow_slow_non_contiguous=True)
            sp_.dma_start(taps[:, :, :], conv_w.rearrange("(j p) t -> p j t", p=P)).then_inc(S["params_loaded"], 16)
            sp_.dma_start(tap_bias[:, :], column(conv_b), **slow).then_inc(S["params_loaded"], 16)
            sp_.dma_start(norm_cols[:, :], column(norm_w), **slow).then_inc(S["params_loaded"], 16)
            sp_.dma_start(dtb[:, :], dt_bias.rearrange("(h a) -> h a", a=1)).then_inc(S["params_loaded"], 16)
            sp_.dma_start(head_rows[:, 0:N_HEAD], a_log.rearrange("(a h) -> a h", a=1)).then_inc(S["params_loaded"], 16)
            sp_.dma_start(head_rows[:, N_HEAD:], d_skip.rearrange("(a h) -> a h", a=1)).then_inc(S["params_loaded"], 16)
            sp_.dma_start(u[:, :, :], rows(u_rows, 0)).then_inc(S["u_loaded"], 16)

            def body(n, first_tile, last_tile):
                if not last_tile:
                    sp_.wait_ge(S["xn_done"], (n + 1) * C)
                    sp_.dma_start(u[:, :, :], rows(u_rows, n + 1)).then_inc(S["u_loaded"], 16)
                if not first_tile:
                    sp_.wait_ge(S["out_stored"], 16 * n)
                    apart(sp_, S["sp_passed"])
                    sp_.wait_ge(S["o_done"], C * n)
                sp_.dma_start(gate[:, :, :], rows(gate_rows, n)).then_inc(S["rest_loaded"], 16)
                sp_.dma_start(residual[:, :, :], rows(u_rows, n)).then_inc(S["rest_loaded"], 16)
                sp_.wait_ge(S["o_done"], C * (n + 1))
                sp_.dma_start(rows(out_rows, n), gate[:, :, :]).then_inc(S["out_stored"], 16)

            body(0, True, False)
            with sp_.Fori(1, N - 1) as n:
                body(n, False, False)
            body(N - 1, False, True)
            sp_.wait_ge(S["out_stored"], 16 * N)

        @block.gpsimd
        def _(pool):
            pool.memset(tri[:, :], 1.0).then_inc(S["pool_step"], 1)
            pool.memset(part[0:LO + N_HEAD, 0, 0:N_HEAD], 0.0).then_inc(S["pool_step"], 1)
            pool.memset(keep[:, :], 1.0).then_inc(S["pool_step"], 1)
            pool.memset(ones_row[:, :], 1.0).then_inc(S["consts"], 1)
            pool.memset(minus_half[:, :], -0.5).then_inc(S["consts"], 1)
            pool.memset(ones[:, :], 1.0).then_inc(S["consts"], 1)
            pool.memset(a_dup[:, :, :], 0.0).then_inc(S["consts"], 1)
            pool.memset(state[:, :], 0.0).then_inc(S["consts"], 1)
            pool.memset(edges[:, :, :], 0.0).then_inc(S["consts"], 1)
            pool.wait_ge(S["pool_step"], 3)
            pool.affine_select(out=tri[:, :], in_=tri[:, :], compare_op=ALU.is_ge, fill=0.0, base=0,
                               pattern=[[1, P]], channel_multiplier=-1).then_inc(S["consts"], 1)
            select = part[0:LO + N_HEAD, 0, 0:N_HEAD]
            for i, start in enumerate((0, LO)):
                pool.affine_select(out=select, in_=select, compare_op=ALU.not_equal, fill=1.0, base=-start,
                                   pattern=[[-1, N_HEAD]], channel_multiplier=1).then_inc(S["pool_step"], 1)
                pool.wait_ge(S["pool_step"], 4 + i)
            nc.gpsimd.tensor_copy(pick[:, :], select).then_inc(S["consts"], 1)
            for b in range(1, n_batch):
                pool.memset(keep[:, b * N_PER_BATCH:b * N_PER_BATCH + 1], 0.0).then_inc(S["consts"], 1)
            pool.wait_ge(S["consts"], 7 + n_batch)

            def norm(n, first_tile=False):
                if not first_tile:
                    pool.wait_ge(S["xn_done"], n * C)
                    apart(pool, S["pool_passed"])
                nc.gpsimd.tensor_copy(scale[:, :], ln_scale[:, bass.ds(n * C, C)]).then_inc(S["norm_set"], 1)
                nc.gpsimd.tensor_copy(shift[:, :], ln_shift[:, bass.ds(n * C, C)]).then_inc(S["norm_set"], 1)

            def edge_before(n, q, first_tile):
                j = ORDER[q]
                if q >= 2:
                    pool.wait_ge(S["tap_done"], (n * NT + q - 1) * 3)
                    pool.wait_ge(S["edge_out"], n * NT + q - 1)
                elif not first_tile:
                    pool.wait_ge(S["tap_done"], n * NT * 3)
                    pool.wait_ge(S["edge_out"], n * NT)
                nc.gpsimd.tensor_tensor(raw[:, q % 2, 0:N_TAP - 1], edges[:, j, :],
                                        keep_now[:, :].to_broadcast([P, N_TAP - 1]), ALU.mult)\
                    .then_inc(S["edge_in"], 1)

            def edge_after(n, q):
                pool.wait_ge(S["raw_done"], n * NT + q + 1)
                pool.wait_ge(S["edge_in"], n * NT + q + 1)
                nc.gpsimd.tensor_tensor(edges[:, ORDER[q], :], raw[:, q % 2, T:T + N_TAP - 1],
                                        ones[:, :].to_broadcast([P, N_TAP - 1]), ALU.mult)\
                    .then_inc(S["edge_out"], 1)

            def x_products(n, j, first_tile):
                cols = slice(j * P, (j + 1) * P)
                hs = slice(2 * j, 2 * j + 2)
                pool.wait_ge(S["xd_done"], n * XT + j + 1)
                if j == 0:
                    pool.wait_ge(S["taild_set"], n + 1)
                    if not first_tile:
                        pool.wait_ge(S["st_done"], 4 * n)
                for c in range(C):
                    nc.gpsimd.tensor_tensor(xdd[:, c, cols].rearrange("p (h d) -> p h d", d=HEAD),
                                            xd[:, c, cols].rearrange("p (h d) -> p h d", d=HEAD),
                                            heads(tail_decay[:, c, hs]), ALU.mult).then_inc(S["xdd_done"], 1)
                for c in range(C):
                    v = x_tok[:, c, cols].rearrange("p (h d) -> p h d", d=HEAD)
                    nc.gpsimd.tensor_tensor(v, v, heads(head_params[:, N_HEAD + 2 * j:N_HEAD + 2 * j + 2]),
                                            ALU.mult).then_inc(S["skip_done"], 1)

            def decay_state(n, c, first_tile):
                for h in range(2):
                    pool.wait_ge(S["off_done"], n * 4 + c * 2 + h + 1)
                    if c:
                        pool.wait_ge(S["state_set"], n * 4 + h + 1)
                    elif not first_tile:
                        pool.wait_ge(S["state_kept"], n)
                    v = state[:, h * 512:(h + 1) * 512].rearrange("p (h d) -> p h d", d=HEAD)
                    nc.gpsimd.tensor_tensor(v, v, heads(chunk_decay[:, c, h * HALF:(h + 1) * HALF]), ALU.mult)\
                        .then_inc(S["decayed"], 1)

            def add_and_gate(n, c):
                for h in range(2):
                    cols = slice(h * 512, (h + 1) * 512)
                    pool.wait_ge(S["part_sum"], n * 4 + c * 2 + h + 1)
                    nc.gpsimd.tensor_tensor(x_tok[:, c, cols], x_tok[:, c, cols], part[:, h, :], ALU.add)\
                        .then_inc(S["sum_done"], 1)
                    pool.wait_ge(S["sum_done"], n * 4 + c * 2 + h + 1)
                    pool.wait_ge(S["gz_done"], n * 4 + c * 2 + h + 1)
                    nc.gpsimd.tensor_tensor(x_tok[:, c, cols], x_tok[:, c, cols], gz[:, c, cols], ALU.mult)\
                        .then_inc(S["y_done"], 1)

            def rms_factor(n, c):
                pool.wait_ge(S["sq_done"], n * C + c + 1)
                apart(pool, S["pool_passed"])
                nc.gpsimd.tensor_scalar(rms[:, c, 0:1], ssq[:, c:c + 1], 64.0 / (4 * D_INNER), 64 * RMS_EPS,
                                        ALU.mult, ALU.add).then_inc(S["rms_step"], 1)
                pool.wait_ge(S["rms_step"], n * 4 + c * 2 + 1)
                nc.gpsimd.tensor_tensor(rms[:, c, 1:2], rms[:, c, 0:1], minus_half[:, :], ALU.pow)\
                    .then_inc(S["rms_step"], 1)

            def body(n, first_tile, last_tile):
                if not first_tile:
                    pool.wait_ge(S["edge_in"], n * NT)
                    apart(pool, S["pool_passed"])
                nc.gpsimd.tensor_copy(keep_now[:, :], keep[:, bass.ds(n, 1)]).then_inc(S["keep_set"], 1)
                pool.wait_ge(S["keep_set"], n + 1)
                if not first_tile:
                    pool.wait_ge(S["state_set"], 4 * n)
                    apart(pool, S["pool_passed"])
                    nc.gpsimd.tensor_scalar(state[:, :], state[:, :], keep_now[:, :], None, ALU.mult)\
                        .then_inc(S["state_kept"], 1)
                for q in range(NT + 1):
                    if q < NT:
                        edge_before(n, q, first_tile)
                    if q >= 1:
                        edge_after(n, q - 1)
                    if q >= 7:
                        x_products(n, q - 7, first_tile)
                if not last_tile:
                    norm(n + 1)
                for j in range(NT - 6, XT):
                    x_products(n, j, first_tile)
                pool.wait_ge(S["chunk_set"], n + 1)
                pool.wait_ge(S["skip_done"], (n + 1) * XT * C)
                if not first_tile:
                    pool.wait_ge(S["o_mult"], C * n)
                decay_state(n, 0, first_tile)
                add_and_gate(n, 0)
                decay_state(n, 1, first_tile)
                rms_factor(n, 0)
                add_and_gate(n, 1)
                rms_factor(n, 1)

            norm(0, first_tile=True)
            body(0, True, False)
            with pool.Fori(1, N - 1) as n:
                body(n, False, False)
            body(N - 1, False, True)

        @block.scalar
        def _(act):
            WH = W_ALL // 2
            for q in range(2 * KD):
                k, h = q // 2, q % 2
                act.wait_ge(S[f"w{h}_loaded"], 16 * (k + 1))
                nc.scalar.activation(w_hi[:, k, h * WH:(h + 1) * WH], STAGE2[h][:, 0:WH], ACT.Copy)\
                    .then_inc(S["w_hi_set"], 1)
            for j in range(XT):
                act.wait_ge(S["wo_scaled"], j + 1)
                nc.scalar.activation(wo_hi[:, j, :], STAGE[0][:, j * DM:(j + 1) * DM], ACT.Copy)\
                    .then_inc(S["wo_hi_set"], 1)
            act.wait_ge(S["head_ps"], 1)
            nc.scalar.activation(head_params[:, 0:N_HEAD], cum_ps[:, 0:N_HEAD], ACT.Exp).then_inc(S["heads_exp"], 1)
            nc.scalar.activation(head_params[:, N_HEAD:], cum_ps[:, N_HEAD:2 * N_HEAD], ACT.Copy)\
                .then_inc(S["heads_set"], 1)

            def normalise(n, c, first_tile=False):
                act.wait_ge(S["norm_set"], 2 * (n + 1))
                act.wait_ge(S["u_loaded"], 16 * (n + 1))
                if c == 1:
                    act.wait_ge(S["turned"], n * C + 1)
                elif not first_tile:
                    act.wait_ge(S["turned"], n * C)
                nc.scalar.activation(xn[:, :], u[:, c, :], ACT.Identity, bias=shift[:, c:c + 1],
                                     scale=scale[:, c:c + 1]).then_inc(S["xn_done"], 1)

            def high(n, c):
                act.wait_ge(S["turned"], n * C + c + 1)
                nc.scalar.activation(x_hi[:, :, c * P:(c + 1) * P],
                                     turn_ps[c][:, :].rearrange("p (k t) -> p k t", t=P), ACT.Copy)\
                    .then_inc(S["xhi_done"], 1)

            def conv_in(n, q, first_tile):
                j = ORDER[q]
                act.wait_ge(S["proj_done"], n * NT + q + 1)
                act.wait_ge(S["edge_in"], n * NT + q + 1)
                nc.scalar.activation(raw[:, q % 2, N_TAP - 1:], proj_ps[q % 2][:, 0:T], ACT.Copy)\
                    .then_inc(S["raw_done"], 1)
                if q >= 2 or not first_tile:
                    act.wait_ge(S["conv_done"], n * NT + max(q - 1, 0))
                nc.scalar.activation(acc[:, q % 2, :], proj_ps[q % 2][:, 0:T], ACT.Identity,
                                     bias=tap_bias[:, j:j + 1], scale=taps[:, j, N_TAP - 1:N_TAP])\
                    .then_inc(S["acc_done"], 1)

            def conv_tanh(n, q, first_tile):
                act.wait_ge(S["tap_done"], (n * NT + q + 1) * 3)
                if q >= 4:
                    act.wait_ge(S["pair_done"], n * (XT + 2) + q - 1)
                elif q >= 2:
                    act.wait_ge(S["conv_done"], n * NT + q - 1)
                elif not first_tile:
                    act.wait_ge(S["pair_done"], n * (XT + 2))
                nc.scalar.activation(act_x[:, q % 2, :], acc[:, q % 2, :], ACT.Tanh).then_inc(S["tanh_done"], 1)

            def x_copy(n, j, first_tile):
                act.wait_ge(S["pair_done"], n * (XT + 2) + j + 3)
                if j == 0 and not first_tile:
                    act.wait_ge(S["y_turned"], 4 * n)
                    act.wait_ge(S["sq_done"], C * n)
                nc.scalar.activation(x_tok[:, :, j * P:(j + 1) * P],
                                     pair_ps.rearrange("p (c d) -> p c d", d=P), ACT.Copy)\
                    .then_inc(S["pair_copied"], 1)

            def decay_heads(n, first, first_tile):
                for h in (first, first + 1):
                    act.wait_ge(S["cumb_done"], n * N_HEAD + first + 2)
                    if h == 0 and not first_tile:
                        act.wait_ge(S["diag_done"], 4 * n)
                    for c in range(C):
                        nc.scalar.activation(lm[:, h, c, :], cum_ps[:, (h % 2) * T + c * P:(h % 2) * T + (c + 1) * P],
                                             ACT.Relu, bias=cum[:, c, h:h + 1], scale=-1.0)\
                            .then_inc(S["relu_done"], 1)
                act.wait_ge(S["relu_done"], (n * N_HEAD + first + 2) * C)
                v = lm[:, first:first + 2, :, :].rearrange("p h c l -> p (h c l)")
                nc.scalar.activation(v, v, ACT.Exp, scale=-1.0).then_inc(S["exp_done"], 1)

            def z_tanh(n, i, first_tile):
                c, h = i // 2, i % 2
                act.wait_ge(S["z_done"], n * 4 + i + 1)
                if not first_tile and i == 0:
                    act.wait_ge(S["y_done"], 4 * n)
                nc.scalar.activation(gz[:, c, h * 512:(h + 1) * 512], proj_ps[h][:, :], ACT.Tanh, scale=0.5)\
                    .then_inc(S["tz_done"], 1)

            def body(n, first_tile, last_tile):
                act.wait_ge(S["dt_done"], n + 1)
                if not first_tile:
                    act.wait_ge(S["cumt_done"], n)
                nc.scalar.activation(dt_raw[:, :], dt_ps, ACT.Identity, bias=dtb[:, 0:1]).then_inc(S["dtraw_done"], 1)
                conv_in(n, 0, first_tile)
                conv_in(n, 1, first_tile)
                act.wait_ge(S["dtt_done"], n + 1)
                if not first_tile:
                    act.wait_ge(S["dt_set"], n)
                nc.scalar.activation(sp[:, 0, :], dtt_ps, ACT.Abs).then_inc(S["sp_act"], 1)
                act.wait_ge(S["sp_act"], 2 * n + 1)
                nc.scalar.activation(sp[:, 1, :], sp[:, 0, :], ACT.Exp, scale=-1.0).then_inc(S["sp_act"], 1)
                conv_tanh(n, 0, first_tile)
                conv_in(n, 2, first_tile)
                conv_tanh(n, 1, first_tile)
                act.wait_ge(S["pair_done"], n * (XT + 2) + 1)
                if not first_tile:
                    act.wait_ge(S["st_done"], 4 * n)
                nc.scalar.activation(b_tok[:, :, :], pair_ps.rearrange("p (c d) -> p c d", d=P), ACT.Copy)\
                    .then_inc(S["pair_copied"], 1)
                conv_in(n, 3, first_tile)
                conv_tanh(n, 2, first_tile)
                act.wait_ge(S["cumr_done"], n + 1)
                if not first_tile:
                    act.wait_ge(S["cumb_done"], n * N_HEAD)
                    act.wait_ge(S["cumt_done"], n)
                nc.scalar.activation(cum_parts[:, :], cumr_ps, ACT.Copy).then_inc(S["cumhi_done"], 1)
                nc.scalar.activation(cum_rows[:, :], small[0:N_HEAD, 0:T], ACT.Copy).then_inc(S["cumrows_done"], 1)
                conv_in(n, 4, first_tile)
                conv_tanh(n, 3, first_tile)
                x_copy(n, 0, first_tile)
                act.wait_ge(S["cumt_done"], n + 1)
                if not first_tile:
                    act.wait_ge(S["relu_done"], n * N_HEAD * C)
                    act.wait_ge(S["tail_set"], 2 * n)
                nc.scalar.activation(cum[:, :, :].rearrange("p c h -> p (c h)"), cumt_ps, ACT.Copy)\
                    .then_inc(S["cum_set"], 1)
                if not first_tile:
                    act.wait_ge(S["part_off"], 4 * n)
                nc.scalar.activation(grow[:, :, :].rearrange("p c h -> p (c h)"), cumt_ps, ACT.Exp)\
                    .then_inc(S["grow_set"], 1)
                conv_in(n, 5, first_tile)
                conv_tanh(n, 4, first_tile)
                x_copy(n, 1, first_tile)
                act.wait_ge(S["last_done"], n + 1)
                if not first_tile:
                    act.wait_ge(S["decayed"], 4 * n)
                nc.scalar.activation(chunk_decay[:, :, :].rearrange("p c h -> p (c h)"), last_ps, ACT.Exp)\
                    .then_inc(S["chunk_set"], 1)
                conv_in(n, 6, first_tile)
                conv_tanh(n, 5, first_tile)
                act.wait_ge(S["tail_set"], 2 * (n + 1))
                if not first_tile:
                    act.wait_ge(S["xdd_done"], n * XT * C)
                nc.scalar.activation(tail_decay[:, :, :], tail[:, :, :], ACT.Exp, scale=-1.0)\
                    .then_inc(S["taild_set"], 1)
                decay_heads(n, 0, first_tile)
                x_copy(n, 2, first_tile)
                conv_in(n, 7, first_tile)
                conv_tanh(n, 6, first_tile)
                decay_heads(n, 2, first_tile)
                x_copy(n, 3, first_tile)
                conv_in(n, 8, first_tile)
                conv_tanh(n, 7, first_tile)
                decay_heads(n, 4, first_tile)
                x_copy(n, 4, first_tile)
                conv_in(n, 9, first_tile)
                conv_tanh(n, 8, first_tile)
                decay_heads(n, 6, first_tile)
                x_copy(n, 5, first_tile)
                conv_tanh(n, 9, first_tile)
                z_tanh(n, 0, first_tile)
                decay_heads(n, 8, first_tile)
                x_copy(n, 6, first_tile)
                z_tanh(n, 1, first_tile)
                decay_heads(n, 10, first_tile)
                x_copy(n, 7, first_tile)
                z_tanh(n, 2, first_tile)
                decay_heads(n, 12, first_tile)
                z_tanh(n, 3, first_tile)
                decay_heads(n, 14, first_tile)
                if not last_tile:
                    normalise(n + 1, 0)
                    normalise(n + 1, 1)
                    high(n + 1, 0)
                    high(n + 1, 1)
                for c in range(C):
                    act.wait_ge(S["y_done"], n * 4 + 2 * c + 2)
                    act.wait_ge(S["diag_done"], n * 4 + 2 * c + 2)
                    act.wait_ge(S["xdd_done"], (n + 1) * XT * C)
                    if not first_tile:
                        act.wait_ge(S["rms_step"], 4 * n)
                    nc.scalar.activation(xd[:, c, :], x_tok[:, c, :], ACT.Square, accum_out=ssq[:, c:c + 1])\
                        .then_inc(S["sq_done"], 1)
                    for r in range(2):
                        act.wait_ge(S["y_turned"], n * 4 + 2 * c + r + 1)
                        if r == 0 and (c == 1 or not first_tile):
                            act.wait_ge(S["out_done"], n * C + c)
                        nc.scalar.activation(y_hi[:, 4 * r:4 * r + 4, :],
                                             turn_ps[r][:, :].rearrange("p (j t) -> p j t", t=P), ACT.Copy)\
                            .then_inc(S["yhi_done"], 1)

            act.wait_ge(S["taps_halved"], 2)
            normalise(0, 0, first_tile=True)
            normalise(0, 1, first_tile=True)
            high(0, 0)
            high(0, 1)
            body(0, True, False)
            with act.Fori(1, N - 1) as n:
                body(n, False, False)
            body(N - 1, False, True)

        @block.vector
        def _(dve):
            WH = W_ALL // 2
            for q in range(2 * KD):
                k, h = q // 2, q % 2
                dve.wait_ge(S["w_hi_set"], q + 1)
                nc.vector.tensor_tensor(w_lo[:, k, h * WH:(h + 1) * WH], STAGE2[h][:, 0:WH],
                                        w_hi[:, k, h * WH:(h + 1) * WH].bitcast(F32), ALU.subtract)\
                    .then_inc(S["w_lo_set"], 1)
            dve.wait_ge(S["wo_loaded"], 16)
            dve.wait_ge(S["params_loaded"], 16 * 6)
            nc.vector.tensor_scalar(taps[:, :, :], taps[:, :, :], 0.5, None, ALU.mult).then_inc(S["taps_halved"], 1)
            nc.vector.tensor_scalar(tap_bias[:, :], tap_bias[:, :], 0.5, None, ALU.mult).then_inc(S["taps_halved"], 1)
            for j in range(XT):
                w = STAGE[0][:, j * DM:(j + 1) * DM]
                nc.vector.tensor_scalar(w, w, norm_cols[:, j:j + 1], None, ALU.mult).then_inc(S["wo_scaled"], 1)
                dve.wait_ge(S["wo_hi_set"], j + 1)
                nc.vector.tensor_tensor(wo_lo[:, j, :], w, wo_hi[:, j, :].bitcast(F32), ALU.subtract)\
                    .then_inc(S["wo_lo_set"], 1)
            dve.wait_ge(S["heads_exp"], 1)
            nc.vector.tensor_scalar(head_params[:, 0:N_HEAD], head_params[:, 0:N_HEAD], -1.0, None, ALU.mult)\
                .then_inc(S["heads_set"], 1)
            dve.wait_ge(S["heads_set"], 2)
            dve.wait_ge(S["taps_halved"], 2)
            dve.wait_ge(S["consts"], 7 + n_batch)

            def low(n, c):
                dve.wait_ge(S["xhi_done"], n * C + c + 1)
                v = slice(c * P, (c + 1) * P)
                nc.vector.tensor_tensor(x_lo[:, :, v], turn_ps[c][:, :].rearrange("p (k t) -> p k t", t=P),
                                        x_hi[:, :, v].bitcast(F32), ALU.subtract).then_inc(S["xlo_done"], 1)

            def conv_taps(n, q):
                j = ORDER[q]
                dve.wait_ge(S["acc_done"], n * NT + q + 1)
                for i, t in enumerate((2, 1, 0)):
                    if i:
                        dve.wait_ge(S["tap_done"], (n * NT + q) * 3 + i)
                    nc.vector.scalar_tensor_tensor(acc[:, q % 2, :], raw[:, q % 2, t:t + T], taps[:, j, t:t + 1],
                                                   acc[:, q % 2, :], ALU.mult, ALU.add).then_inc(S["tap_done"], 1)

            def conv_out(n, q, first_tile):
                dve.wait_ge(S["tanh_done"], n * NT + q + 1)
                if q < 2 and not first_tile:
                    dve.wait_ge(S["off_done"], 4 * n)
                out = (bt, ct)[q][:, :] if q < 2 else act_x[:, q % 2, :]
                nc.vector.scalar_tensor_tensor(out, act_x[:, q % 2, :], 1.0, acc[:, q % 2, :], ALU.add, ALU.mult)\
                    .then_inc(S["conv_done"], 1)

            def x_dt(n, j, first_tile):
                dve.wait_ge(S["pair_copied"], n * (XT + 1) + j + 2)
                if j == 0 and not first_tile:
                    dve.wait_ge(S["sq_done"], C * n)
                src = x_tok[:, :, j * P:(j + 1) * P].rearrange("p c (h d) -> p c h d", d=HEAD)
                out = xd[:, :, j * P:(j + 1) * P].rearrange("p c (h d) -> p c h d", d=HEAD)
                w = dtv[:, :, 2 * j:2 * j + 2].unsqueeze(-1).to_broadcast([P, C, 2, HEAD])
                nc.vector.tensor_tensor(out, src, w, ALU.mult).then_inc(S["xd_done"], 1)

            def softplus(n):
                base = [n * 14]

                def step(ins):
                    base[0] = base[0] + 1
                    ins.then_inc(S["sp_step"], 1)
                    dve.wait_ge(S["sp_step"], base[0])

                e, s, s2, r, q = (sp[:, i, :] for i in (1, 2, 3, 4, 5))
                dve.wait_ge(S["sp_act"], 2 * (n + 1))
                step(nc.vector.tensor_scalar(r, e, 2.0, None, ALU.add))
                step(nc.vector.reciprocal(q, r))
                step(nc.vector.tensor_tensor(s, e, q, ALU.mult))
                step(nc.vector.tensor_tensor(s2, s, s, ALU.mult))
                step(nc.vector.tensor_scalar(q, s2, 1.0 / 17, None, ALU.mult))
                for odd in (15, 13, 11, 9, 7, 5, 3):
                    step(nc.vector.scalar_tensor_tensor(q, q, 1.0 / odd, s2, ALU.add, ALU.mult))
                step(nc.vector.scalar_tensor_tensor(q, q, 1.0, s, ALU.add, ALU.mult))
                step(nc.vector.tensor_scalar(r, dtt_ps, 0.0, None, ALU.max))
                nc.vector.scalar_tensor_tensor(dtv[:, :, :].rearrange("p c h -> p (c h)"), q, 2.0, r, ALU.mult,
                                               ALU.add).then_inc(S["dt_set"], 1)
                dve.wait_ge(S["dt_set"], n + 1)
                for start in (0, LO):
                    nc.vector.tensor_tensor(a_dup[:, :, start:start + N_HEAD], dtv[:, :, :],
                                            head_params[:, 0:N_HEAD].unsqueeze(1).to_broadcast([P, C, N_HEAD]),
                                            ALU.mult).then_inc(S["a_set"], 1)

            def body(n, first_tile, last_tile):
                conv_taps(n, 0)
                conv_taps(n, 1)
                conv_out(n, 0, first_tile)
                conv_taps(n, 2)
                conv_out(n, 1, first_tile)
                if not first_tile:
                    dve.wait_ge(S["xd_done"], n * XT)
                    dve.wait_ge(S["cumr_done"], n)
                softplus(n)
                conv_taps(n, 3)
                conv_out(n, 2, first_tile)
                dve.wait_ge(S["pair_done"], n * (XT + 2) + 2)
                if not first_tile:
                    dve.wait_ge(S["lm_done"], 4 * n)
                nc.vector.tensor_tensor(gm[:, :, :], pair_ps.rearrange("p (c l) -> p c l", l=P),
                                        tri[:, :].unsqueeze(1).to_broadcast([P, C, P]), ALU.mult)\
                    .then_inc(S["gm_done"], 1)
                dve.wait_ge(S["cumhi_done"], n + 1)
                dve.wait_ge(S["cumrows_done"], n + 1)
                nc.vector.tensor_tensor(cum_parts[LO:LO + N_HEAD, :], small[LO:LO + N_HEAD, 0:T],
                                        cum_parts[LO:LO + N_HEAD, :].bitcast(F32), ALU.subtract)\
                    .then_inc(S["cumlo_done"], 1)
                conv_taps(n, 4)
                conv_out(n, 3, first_tile)
                x_dt(n, 0, first_tile)
                conv_taps(n, 5)
                conv_out(n, 4, first_tile)
                x_dt(n, 1, first_tile)
                dve.wait_ge(S["chunk_set"], n + 1)
                if not first_tile:
                    dve.wait_ge(S["taild_set"], n)
                flat = tail[:, :, :].rearrange("p c h -> p (c h)")
                nc.vector.tensor_tensor(flat, cum[:, :, :].rearrange("p c h -> p (c h)"), last_ps, ALU.subtract)\
                    .then_inc(S["tail_set"], 1)
                dve.wait_ge(S["tail_set"], 2 * n + 1)
                nc.vector.tensor_scalar(flat, flat, 0.0, None, ALU.max).then_inc(S["tail_set"], 1)
                for q in range(6, NT):
                    conv_taps(n, q)
                    conv_out(n, q - 1, first_tile)
                    x_dt(n, q - 4, first_tile)
                conv_out(n, NT - 1, first_tile)

                def z_gate(i):
                    c, h = i // 2, i % 2
                    dve.wait_ge(S["tz_done"], n * 4 + i + 1)
                    v = gz[:, c, h * 512:(h + 1) * 512]
                    nc.vector.scalar_tensor_tensor(v, v, 1.0, proj_ps[h][:, :], ALU.add, ALU.mult)\
                        .then_inc(S["gz_done"], 1)

                def mask(c, h):
                    dve.wait_ge(S["exp_done"], n * HALF + (h + 1) * HALF // 2)
                    v = lm[:, h * HALF:(h + 1) * HALF, c, :]
                    nc.vector.tensor_tensor(v, v, gm[:, c:c + 1, :].to_broadcast([P, HALF, P]), ALU.mult)\
                        .then_inc(S["lm_done"], 1)

                z_gate(0)
                x_dt(n, 6, first_tile)
                z_gate(1)
                x_dt(n, 7, first_tile)
                dve.wait_ge(S["gm_done"], n + 1)
                mask(0, 0)
                mask(1, 0)
                z_gate(2)
                z_gate(3)
                mask(0, 1)
                mask(1, 1)
                for c in range(C):
                    for h in range(2):
                        i = n * 4 + 2 * c + h
                        dve.wait_ge(S["off_done"], i + 1)
                        if c or not first_tile:
                            dve.wait_ge(S["sum_done"], i - 1)
                        v = part[:, h, :].rearrange("p (h d) -> p h d", d=HEAD)
                        nc.vector.tensor_tensor(v, off_ps[:, :].rearrange("p (h d) -> p h d", d=HEAD),
                                                heads(grow[:, c, h * HALF:(h + 1) * HALF]), ALU.mult)\
                            .then_inc(S["part_off"], 1)
                        dve.wait_ge(S["part_off"], i + 1)
                        dve.wait_ge(S["diag_done"], i + 1)
                        nc.vector.tensor_tensor(part[:, h, :], part[:, h, :], diag_ps[:, :], ALU.add)\
                            .then_inc(S["part_sum"], 1)
                        dve.wait_ge(S["st_done"], i + 1)
                        dve.wait_ge(S["decayed"], i + 1)
                        v = state[:, h * 512:(h + 1) * 512]
                        nc.vector.tensor_tensor(v, v, state_ps[:, :], ALU.add).then_inc(S["state_set"], 1)
                if not last_tile:
                    low(n + 1, 0)
                    low(n + 1, 1)

                for c in range(C):
                    for r in range(2):
                        dve.wait_ge(S["yhi_done"], n * 4 + 2 * c + r + 1)
                        if c and r == 0:
                            dve.wait_ge(S["out_done"], n * C + c)
                        nc.vector.tensor_tensor(y_lo[:, 4 * r:4 * r + 4, :],
                                                turn_ps[r][:, :].rearrange("p (j t) -> p j t", t=P),
                                                y_hi[:, 4 * r:4 * r + 4, :].bitcast(F32), ALU.subtract)\
                            .then_inc(S["ylo_done"], 1)
                    dve.wait_ge(S["rest_loaded"], 32 * (n + 1))
                    dve.wait_ge(S["out_done"], n * C + c + 1)
                    dve.wait_ge(S["rms_step"], n * 4 + 2 * c + 2)
                    nc.vector.scalar_tensor_tensor(gate[:, c, :], proj_ps[c][:, :], rms[:, c, 1:2], gate[:, c, :],
                                                   ALU.mult, ALU.mult).then_inc(S["o_mult"], 1)
                    dve.wait_ge(S["o_mult"], n * C + c + 1)
                    nc.vector.tensor_tensor(gate[:, c, :], gate[:, c, :], residual[:, c, :], ALU.add)\
                        .then_inc(S["o_done"], 1)

            low(0, 0)
            low(0, 1)
            body(0, True, False)
            with dve.Fori(1, N - 1) as n:
                body(n, False, False)
            body(N - 1, False, True)

        @block.tensor
        def _(pe):
            pe.wait_ge(S["params_loaded"], 16 * 6)
            pe.wait_ge(S["consts"], 7 + n_batch)
            nc.tensor.matmul(cum_ps[:, 0:2 * N_HEAD], ones_row[:, :], head_rows[:, :], start=True, stop=True)\
                .then_inc(S["head_ps"], 1)
            pe.wait_ge(S["heads_set"], 2)
            pe.wait_ge(S["w_lo_set"], 2 * KD)
            pe.wait_ge(S["wo_lo_set"], XT)

            def turn(n, c, first_tile=False):
                pe.wait_ge(S["xn_done"], n * C + c + 1)
                if c == 0 and not first_tile:
                    pe.wait_ge(S["chunk_set"], n)
                    pe.wait_ge(S["tail_set"], 2 * n)
                    pe.wait_ge(S["pair_copied"], n * (XT + 1))
                    pe.wait_ge(S["xd_done"], n * XT)
                for k in range(KD):
                    last = nc.tensor.transpose(turn_ps[c][:, k * P:(k + 1) * P], xn[:, k * P:(k + 1) * P],
                                               ident[:, :])
                last.then_inc(S["turned"], 1)

            def product(out, blocks, lhs_hi, lhs_lo, rhs_hi, rhs_lo):
                pairs = [(lhs_hi, rhs_hi), (lhs_hi, rhs_lo), (lhs_lo, rhs_hi)]
                for k in range(blocks):
                    for j, (a, b) in enumerate(pairs):
                        last = nc.tensor.matmul(out, a(k), b(k), start=(k == 0 and j == 0),
                                                stop=(k == blocks - 1 and j == 2))
                return last

            def by_channel(out, lo, width):
                return product(out, KD, lambda k: w_hi[:, k, lo:lo + width], lambda k: w_lo[:, k, lo:lo + width],
                               lambda k: x_hi[:, k, :], lambda k: x_lo[:, k, :])

            def project(n, q, first_tile):
                if q >= 2:
                    pe.wait_ge(S["acc_done"], n * NT + q - 1)
                elif not first_tile:
                    pe.wait_ge(S["o_mult"], n * C)
                by_channel(proj_ps[q % 2][:, 0:T], W_X + ORDER[q] * P, P).then_inc(S["proj_done"], 1)

            def pair(n, i, src, first_tile):
                for c in range(C):
                    last = nc.tensor.transpose(pair_ps[:, c * P:(c + 1) * P], src[:, c * P:(c + 1) * P],
                                               ident[:, :])
                last.then_inc(S["pair_done"], 1)

            def x_pair(n, j, first_tile):
                pe.wait_ge(S["conv_done"], n * NT + j + 3)
                if j == 0:
                    pe.wait_ge(S["gm_done"], n + 1)
                else:
                    pe.wait_ge(S["pair_copied"], n * (XT + 1) + j + 1)
                pair(n, j, act_x[:, j % 2, :], first_tile)

            def spread(n, first):
                if first:
                    pe.wait_ge(S["relu_done"], (n * N_HEAD + first) * C)
                for h in (first, first + 1):
                    nc.tensor.matmul(cum_ps[:, (h % 2) * T:(h % 2 + 1) * T],
                                     pick[:, h:h + 1].to_broadcast([LO + N_HEAD, P]), cum_parts[:, :],
                                     start=True, stop=True).then_inc(S["cumb_done"], 1)

            def z_part(n, i):
                c, h = i // 2, i % 2
                if i < 2:
                    pe.wait_ge(S["acc_done"], (n + 1) * NT)
                else:
                    pe.wait_ge(S["gz_done"], n * 4 + i - 1)
                v = slice(c * P, (c + 1) * P)
                cols = slice(h * 512, (h + 1) * 512)
                product(proj_ps[h][:, :], KD, lambda k: x_hi[:, k, v], lambda k: x_lo[:, k, v],
                        lambda k: w_hi[:, k, cols], lambda k: w_lo[:, k, cols]).then_inc(S["z_done"], 1)

            def chunk(n, c, first_tile):
                tok = slice(c * P, (c + 1) * P)
                for h in range(2):
                    i = n * 4 + 2 * c + h
                    cols = slice(h * 512, (h + 1) * 512)
                    if c:
                        pe.wait_ge(S["state_set"], i - 1)
                    elif not first_tile:
                        pe.wait_ge(S["state_kept"], n)
                    if not (first_tile and c == 0 and h == 0):
                        pe.wait_ge(S["part_off"], i)
                    nc.tensor.matmul(off_ps[:, :], ct[:, tok], state[:, cols], start=True, stop=True)\
                        .then_inc(S["off_done"], 1)
                    if c == 0 and h == 0:
                        pe.wait_ge(S["xdd_done"], (n + 1) * XT * C)
                    if not (first_tile and c == 0 and h == 0):
                        pe.wait_ge(S["state_set"], i)
                    nc.tensor.matmul(state_ps[:, :], b_tok[:, c, :], xdd[:, c, cols], start=True, stop=True)\
                        .then_inc(S["st_done"], 1)
                    pe.wait_ge(S["lm_done"], n * 4 + 2 * h + c + 1)
                    if not (first_tile and c == 0 and h == 0):
                        pe.wait_ge(S["part_sum"], i)
                    for m in range(HALF - 1, -1, -1):
                        lead = 32 if m else 0
                        lo = m * HEAD - lead
                        hi = (m + 1) * HEAD
                        last = nc.tensor.matmul(diag_ps[:, lo:hi], lm[:, h * HALF + m, c, :],
                                                xd[:, c, h * 512 + lo:h * 512 + hi], start=True, stop=True)
                    last.then_inc(S["diag_done"], 1)

            def output(n, c, last_tile):
                pe.wait_ge(S["y_done"], n * 4 + 2 * c + 2)
                for r in range(2):
                    if c == 0 and not last_tile:
                        pe.wait_ge(S["xlo_done"], (n + 1) * C + r + 1)
                    elif c == 0 and r == 0:
                        pe.wait_ge(S["chunk_set"], n + 1)
                        pe.wait_ge(S["tail_set"], 2 * (n + 1))
                        pe.wait_ge(S["pair_copied"], (n + 1) * (XT + 1))
                        pe.wait_ge(S["xd_done"], (n + 1) * XT)
                    elif c == 1:
                        pe.wait_ge(S["ylo_done"], n * 4 + r + 1)
                    for j in range(4):
                        lo = (4 * r + j) * P
                        last = nc.tensor.transpose(turn_ps[r][:, j * P:(j + 1) * P], x_tok[:, c, lo:lo + P],
                                                   ident[:, :])
                    last.then_inc(S["y_turned"], 1)
                pe.wait_ge(S["gz_done"], 4 * (n + 1))
                pe.wait_ge(S["ylo_done"], n * 4 + 2 * c + 2)
                product(proj_ps[c][:, :], XT, lambda j: y_hi[:, j, :], lambda j: y_lo[:, j, :],
                        lambda j: wo_hi[:, j, :], lambda j: wo_lo[:, j, :]).then_inc(S["out_done"], 1)

            def body(n, first_tile, last_tile):
                pe.wait_ge(S["xlo_done"], (n + 1) * C)
                if not first_tile:
                    pe.wait_ge(S["ylo_done"], n * 4)
                by_channel(dt_ps, W_DT, N_HEAD).then_inc(S["dt_done"], 1)
                project(n, 0, first_tile)
                project(n, 1, first_tile)
                pe.wait_ge(S["dtraw_done"], n + 1)
                apart(pe, S["pe_passed"])
                for c in range(C):
                    last = nc.tensor.transpose(small[:, 256 + c * N_HEAD:256 + (c + 1) * N_HEAD],
                                               dt_raw[:, c * P:(c + 1) * P], ident[0:N_HEAD, 0:N_HEAD])
                last.then_inc(S["dtt_done"], 1)
                project(n, 2, first_tile)
                pe.wait_ge(S["conv_done"], n * NT + 1)
                pair(n, 0, bt, first_tile)
                project(n, 3, first_tile)
                pe.wait_ge(S["a_set"], 2 * (n + 1))
                for c in range(C):
                    last = nc.tensor.matmul(small[0:LO + N_HEAD, c * P:(c + 1) * P], a_dup[:, c, :], tri[:, :],
                                            start=True, stop=True)
                last.then_inc(S["cumr_done"], 1)
                pe.wait_ge(S["conv_done"], n * NT + 2)
                pe.wait_ge(S["pair_copied"], n * (XT + 1) + 1)
                for c in range(C):
                    tok = slice(c * P, (c + 1) * P)
                    last = nc.tensor.matmul(pair_ps[:, tok], bt[:, tok], ct[:, tok], start=True, stop=True)
                last.then_inc(S["pair_done"], 1)
                project(n, 4, first_tile)
                x_pair(n, 0, first_tile)
                pe.wait_ge(S["cumrows_done"], n + 1)
                pe.wait_ge(S["cumlo_done"], n + 1)
                apart(pe, S["pe_passed"])
                for c in range(C):
                    last = nc.tensor.transpose(small[:, 288 + c * N_HEAD:288 + (c + 1) * N_HEAD],
                                               cum_rows[:, c * P:(c + 1) * P], ident[0:N_HEAD, 0:N_HEAD])
                last.then_inc(S["cumt_done"], 1)
                project(n, 5, first_tile)
                x_pair(n, 1, first_tile)
                pe.wait_ge(S["cum_set"], n + 1)
                pe.wait_ge(S["grow_set"], n + 1)
                nc.tensor.matmul(last_ps, ident[:, P - 1:P].to_broadcast([P, P]), cum[:, :, :].rearrange("p c h -> p (c h)"),
                                 start=True, stop=True).then_inc(S["last_done"], 1)
                project(n, 6, first_tile)
                spread(n, 0)
                x_pair(n, 2, first_tile)
                for i in range(3):
                    project(n, 7 + i, first_tile)
                    spread(n, 2 + 2 * i)
                    x_pair(n, 3 + i, first_tile)
                z_part(n, 0)
                spread(n, 8)
                x_pair(n, 6, first_tile)
                z_part(n, 1)
                spread(n, 10)
                x_pair(n, 7, first_tile)
                z_part(n, 2)
                spread(n, 12)
                z_part(n, 3)
                spread(n, 14)
                chunk(n, 0, first_tile)
                if not last_tile:
                    turn(n + 1, 0)
                    turn(n + 1, 1)
                chunk(n, 1, first_tile)
                output(n, 0, last_tile)
                output(n, 1, last_tile)

            turn(0, 0, first_tile=True)
            turn(0, 1, first_tile=True)
            body(0, True, False)
            with pe.Fori(1, N - 1) as n:
                body(n, False, False)
            body(N - 1, False, True)


def build_program(nc, u, w_in, conv_w, conv_b, dt_bias, a_log, d_skip, norm_w, w_out, w_r, w_k, w_v, mu_r, mu_k, out):
    n_batch, length, _ = u.shape
    n_tok = n_batch * length
    u_rows = u.rearrange("b l d -> (b l) d")
    out_rows = out.rearrange("b l d -> (b l) d")
    gate_rows = nc.dram_tensor("gate_rows", (n_tok, DM), F32, kind="Internal").ap()
    ctx = ExitStack()
    with ctx:
        ident = ctx.enter_context(nc.sbuf_tensor("ident", [P, P], F32))
        ln_scale = ctx.enter_context(nc.sbuf_tensor("ln_scale", [P, n_tok // P], F32))
        ln_shift = ctx.enter_context(nc.sbuf_tensor("ln_shift", [P, n_tok // P], F32))
        ident_step = ctx.enter_context(nc.semaphore("ident_step"))
        with nc.Block() as block:
            @block.gpsimd
            def _(pool):
                pool.memset(ident[:, :], 0.0).then_inc(ident_step, 1)
                pool.wait_ge(ident_step, 1)
                pool.affine_select(out=ident[:, :], in_=ident[:, :], compare_op=ALU.not_equal, fill=1.0, base=0,
                                   pattern=[[-1, P]], channel_multiplier=1).then_inc(ident_step, 1)
                pool.wait_ge(ident_step, 2)
        ffn_phase(nc, u_rows, w_r, w_k, w_v, mu_r, mu_k, gate_rows, ident, ln_scale, ln_shift, n_tok, n_batch)
        ssm_phase(nc, u_rows, w_in, conv_w, conv_b, dt_bias, a_log, d_skip, norm_w, w_out, gate_rows, out_rows,
                  ident, ln_scale, ln_shift, n_tok, n_batch)


INPUTS = ["L0_attn_u", "L0_attn_W_in", "L0_attn_conv_w", "L0_attn_conv_b", "L0_attn_dt_bias", "L0_attn_A_log",
          "L0_attn_D", "L0_attn_norm_w", "L0_attn_W_out", "L0_ffn_W_r", "L0_ffn_W_k", "L0_ffn_W_v", "L0_ffn_mu_r",
          "L0_ffn_mu_k"]


def kernel(**inputs):
    import numpy as np
    import concourse.bacc as bacc
    from concourse.bass_utils import run_bass_kernel_spmd

    nc = bacc.Bacc("TRN2", target_bir_lowering=False, num_devices=1)
    arrays, args = {}, []
    for name in INPUTS:
        a = np.ascontiguousarray(inputs[name])
        arrays[f"in_{name}"] = a
        args.append(nc.dram_tensor(f"in_{name}", a.shape, mybir.dt.from_np(a.dtype), kind="ExternalInput").ap())
    shape = arrays["in_L0_attn_u"].shape
    args.append(nc.dram_tensor("out", shape, F32, kind="ExternalOutput").ap())
    build_program(nc, *args)
    result = run_bass_kernel_spmd(nc, [arrays], core_ids=[0])
    return result.results[0]["out"]
```

```python
import concourse.bass as bass
from concourse import mybir
from contextlib import ExitStack

F32 = mybir.dt.float32
F32R = mybir.dt.float32r
ALU = mybir.AluOpType
ACT = mybir.ActivationFunctionType
P = 128
DM = 512
KD = DM // P
LN_EPS = 1e-5


def apart(eng, passed):
    eng.sem_inc(passed)


def column(ap):
    return ap.rearrange("(k p) -> p k", p=P)


def ffn_phase(nc, u_rows, w_r, w_k, w_v, mu_r, mu_k, gate_rows, ident, ln_scale, ln_shift, n_tok, n_batch):
    T = 512
    C = T // P
    N = n_tok // T
    N_PER_BATCH = N // n_batch

    ctx = ExitStack()
    with ctx:
        def sb(name, shape, dt=F32):
            return ctx.enter_context(nc.sbuf_tensor("f_" + name, shape, dt))

        def ps(name):
            return ctx.enter_context(nc.psum_tensor("f_" + name, [P, 512], F32))

        def sem(name):
            return ctx.enter_context(nc.semaphore("f_" + name))

        w_hi = {n: sb(f"w{n}_hi", [P, KD, DM], F32R) for n in "rkv"}
        w_lo = {n: sb(f"w{n}_lo", [P, KD, DM], F32R) for n in "rkv"}
        mu = {"r": sb("mu_r", [P, KD]), "k": sb("mu_k", [P, KD])}
        keep = sb("keep", [P, N])
        keep_now = sb("keep_now", [P, 1])
        minus_half = sb("minus_half", [P, C])
        minus_one = sb("minus_one", [P, C])
        eps = sb("eps", [P, C])

        u = sb("u", [P, C, DM])
        bn = sb("bn", [P, C, 6])
        mv = sb("mv", [P, C, 2])
        ve = sb("ve", [P, C])
        scale = sb("scale", [P, C])
        mean_scaled = sb("mean_scaled", [P, C])
        shift = sb("shift", [P, C])
        xn = sb("xn", [P, C, DM])
        xt = sb("xt", [P, KD, T + 1])
        dt_ = sb("dt", [P, KD, T])
        mixed = sb("mixed", [P, 2 * KD, T])
        x_hi = {n: sb(f"x{n}_hi", [P, KD, T], F32R) for n in "rk"}
        x_lo = {n: sb(f"x{n}_lo", [P, KD, T], F32R) for n in "rk"}
        kr = sb("kr", [P, KD, T])
        ka = sb("ka", [P, KD, T])
        ka_hi = sb("ka_hi", [P, KD, T], F32R)
        ka_lo = sb("ka_lo", [P, KD, T], F32R)
        tr = sb("tr", [P, C, DM])
        f2 = sb("f2", [P, C, DM])
        tg = sb("tg", [P, C, DM])
        g4 = sb("g4", [P, C, DM])

        ps_t = [ps("ps_t0"), ps("ps_t1")]
        ps_k = [ps("ps_k0"), ps("ps_k1")]
        ps_r = [ps("ps_r0"), ps("ps_r1")]
        ps_v = [ps("ps_v0"), ps("ps_v1")]

        w_loaded = {n: sem(f"w{n}_loaded") for n in "rkv"}
        mu_loaded = sem("mu_loaded")
        consts_set = sem("consts_set")
        w_turned = sem("w_turned")
        w_hi_set = sem("w_hi_set")
        w_lo_set = sem("w_lo_set")
        u_loaded = sem("u_loaded")
        bn_done = sem("bn_done")
        mv_done = sem("mv_done")
        pool_step = sem("pool_step")
        ln_done = sem("ln_done")
        xn_done = sem("xn_done")
        turned = sem("turned")
        xt_done = sem("xt_done")
        keep_set = sem("keep_set")
        edge_done = sem("edge_done")
        diff_done = sem("diff_done")
        mixed_done = sem("mixed_done")
        hi_done = sem("hi_done")
        lo_done = sem("lo_done")
        k_done = sem("k_done")
        kr_done = sem("kr_done")
        ka_done = sem("ka_done")
        kahi_done = sem("kahi_done")
        kalo_done = sem("kalo_done")
        r_done = sem("r_done")
        tr_done = sem("tr_done")
        v_done = sem("v_done")
        f2_done = sem("f2_done")
        tg_done = sem("tg_done")
        g4_done = sem("g4_done")
        g_stored = sem("g_stored")
        passed = sem("passed")
        dve_passed = sem("dve_passed")

        w_raw = {"r": mixed[:, 0:KD, :], "k": mixed[:, KD:2 * KD, :], "v": xn[:, :, :]}
        W_SRC = {"r": w_r, "k": w_k, "v": w_v}

        def u_tile(n):
            return u_rows[bass.ds(n * T, T), :].rearrange("(c p) d -> p c d", p=P)

        def g_tile(n):
            return gate_rows[bass.ds(n * T, T), :].rearrange("(c p) d -> p c d", p=P)

        block = ctx.enter_context(nc.Block())

        @block.sync
        def _(sp):
            for n in "rkv":
                sp.dma_start(w_raw[n], W_SRC[n].rearrange("(o p) c -> p o c", p=P)).then_inc(w_loaded[n], 16)
            sp.dma_start(u[:, :, :], u_tile(0)).then_inc(u_loaded, 16)
            sp.dma_start(mu["r"][:, :], column(mu_r), allow_slow_non_contiguous=True).then_inc(mu_loaded, 16)
            sp.dma_start(mu["k"][:, :], column(mu_k), allow_slow_non_contiguous=True).then_inc(mu_loaded, 16)
            sp.wait_ge(xn_done, C)
            sp.dma_start(u[:, :, :], u_tile(1)).then_inc(u_loaded, 16)
            with sp.Fori(0, N - 2) as n:
                sp.wait_ge(xn_done, (n + 2) * C)
                sp.dma_start(u[:, :, :], u_tile(n + 2)).then_inc(u_loaded, 16)
                sp.wait_ge(g4_done, (n + 1) * C)
                sp.dma_start(g_tile(n), g4[:, :, :]).then_inc(g_stored, 16)
            for n in (N - 2, N - 1):
                sp.wait_ge(g4_done, (n + 1) * C)
                sp.dma_start(g_tile(n), g4[:, :, :]).then_inc(g_stored, 16)
            sp.wait_ge(g_stored, 16 * N)

        @block.gpsimd
        def _(pool):
            pool.memset(keep[:, :], 1.0).then_inc(pool_step, 1)
            pool.memset(minus_half[:, :], -0.5).then_inc(consts_set, 1)
            pool.memset(minus_one[:, :], -1.0).then_inc(consts_set, 1)
            pool.memset(eps[:, :], LN_EPS).then_inc(consts_set, 1)
            pool.memset(xt[:, :, T:T + 1], 0.0).then_inc(consts_set, 1)
            pool.wait_ge(pool_step, 1)
            for b in range(1, n_batch):
                pool.memset(keep[:, b * N_PER_BATCH:b * N_PER_BATCH + 1], 0.0).then_inc(consts_set, 1)
            pool.wait_ge(consts_set, 3 + n_batch)

            STEPS = 4

            def norm(n, first_tile=False):
                first = 1 + n * STEPS
                pool.wait_ge(mv_done, n + 1)
                nc.gpsimd.tensor_tensor(ve[:, :], mv[:, :, 1], eps[:, :], ALU.add).then_inc(pool_step, 1)
                pool.wait_ge(pool_step, first + 1)
                if not first_tile:
                    pool.wait_ge(xn_done, n * C)
                nc.gpsimd.tensor_tensor(scale[:, :], ve[:, :], minus_half[:, :], ALU.pow).then_inc(pool_step, 1)
                pool.wait_ge(pool_step, first + 2)
                nc.gpsimd.tensor_tensor(mean_scaled[:, :], mv[:, :, 0], scale[:, :], ALU.mult).then_inc(pool_step, 1)
                pool.wait_ge(pool_step, first + 3)
                nc.gpsimd.tensor_tensor(shift[:, :], mean_scaled[:, :], minus_one[:, :], ALU.mult)\
                    .then_inc(pool_step, 1)
                pool.wait_ge(pool_step, first + 4)
                apart(pool, passed)
                nc.gpsimd.tensor_copy(ln_scale[:, bass.ds(n * C, C)], scale[:, :]).then_inc(ln_done, 1)
                nc.gpsimd.tensor_copy(ln_shift[:, bass.ds(n * C, C)], shift[:, :]).then_inc(ln_done, 1)

            def edge_and_diff(n, first_tile=False):
                if not first_tile:
                    pool.wait_ge(edge_done, n)
                    pool.wait_ge(mixed_done, n * 2 * KD)
                    apart(pool, passed)
                nc.gpsimd.tensor_copy(keep_now[:, :], keep[:, bass.ds(n, 1)]).then_inc(keep_set, 1)
                pool.wait_ge(keep_set, n + 1)
                nc.gpsimd.tensor_tensor(xt[:, :, 0:1], xt[:, :, T:T + 1],
                                        keep_now[:, :].unsqueeze(1).to_broadcast([P, KD, 1]), ALU.mult)\
                    .then_inc(edge_done, 1)
                pool.wait_ge(edge_done, n + 1)
                for k in range(KD):
                    pool.wait_ge(xt_done, n * KD + k + 1)
                    nc.gpsimd.tensor_tensor(dt_[:, k, :], xt[:, k, 1:T + 1], xt[:, k, 0:T], ALU.subtract)\
                        .then_inc(diff_done, 1)

            norm(0, first_tile=True)
            edge_and_diff(0, first_tile=True)
            with pool.Fori(0, N - 1) as n:
                norm(n + 1)
                edge_and_diff(n + 1)

        @block.scalar
        def _(act):
            for i, w in enumerate("rkv"):
                for k in range(KD):
                    act.wait_ge(w_turned, i * KD + k + 1)
                    nc.scalar.activation(w_hi[w][:, k, :], ps_t[k % 2][:, :], ACT.Copy).then_inc(w_hi_set, 1)

            def normalise(n, first_tile=False):
                act.wait_ge(ln_done, 2 * (n + 1))
                act.wait_ge(u_loaded, 16 * (n + 1))
                if not first_tile:
                    act.wait_ge(turned, n * KD)
                else:
                    act.wait_ge(w_turned, 3 * KD)
                for c in range(C):
                    nc.scalar.activation(xn[:, c, :], u[:, c, :], ACT.Identity, bias=shift[:, c:c + 1],
                                         scale=scale[:, c:c + 1]).then_inc(xn_done, 1)

            def columns(n):
                act.wait_ge(edge_done, n + 1)
                for k in range(KD):
                    act.wait_ge(turned, n * KD + k + 1)
                    nc.scalar.activation(xt[:, k, 1:T + 1], ps_t[k % 2][:, :], ACT.Copy).then_inc(xt_done, 1)

            def high(n, w, first_tile=False):
                base = KD * "kr".index(w)
                if not first_tile:
                    act.wait_ge(k_done if w == "k" else r_done, n * KD)
                for k in range(KD):
                    act.wait_ge(mixed_done, n * 2 * KD + base + k + 1)
                    nc.scalar.activation(x_hi[w][:, k, :], mixed[:, base + k, :], ACT.Copy).then_inc(hi_done, 1)

            def tanh_gate(n, c):
                act.wait_ge(f2_done, n * C + c + 1)
                nc.scalar.activation(tg[:, c, :], f2[:, c, :], ACT.Tanh, scale=0.25).then_inc(tg_done, 1)

            def body(n, first_tile, last_tile):
                for m in range(KD + 1):
                    if m < KD:
                        act.wait_ge(k_done, n * KD + m + 1)
                        if not first_tile and m == 0:
                            act.wait_ge(ka_done, n * KD)
                        nc.scalar.activation(kr[:, m, :], ps_k[m % 2][:, :], ACT.Relu).then_inc(kr_done, 1)
                    if m >= 1:
                        act.wait_ge(ka_done, n * KD + m)
                        if not first_tile and m == 1:
                            act.wait_ge(v_done, n * C)
                        nc.scalar.activation(ka_hi[:, m - 1, :], ka[:, m - 1, :], ACT.Copy).then_inc(kahi_done, 1)
                if not last_tile:
                    normalise(n + 1)
                if not first_tile:
                    act.wait_ge(f2_done, n * C)
                for c in range(C):
                    act.wait_ge(r_done, n * C + c + 1)
                    nc.scalar.activation(tr[:, c, :], ps_r[c % 2][:, :], ACT.Tanh, scale=0.5).then_inc(tr_done, 1)
                if not last_tile:
                    columns(n + 1)
                    high(n + 1, "k")
                if not first_tile:
                    act.wait_ge(g4_done, n * C)
                tanh_gate(n, 0)
                tanh_gate(n, 1)
                if not last_tile:
                    high(n + 1, "r")
                tanh_gate(n, 2)
                tanh_gate(n, 3)

            normalise(0, first_tile=True)
            columns(0)
            high(0, "k", first_tile=True)
            high(0, "r", first_tile=True)
            body(0, True, False)
            with act.Fori(1, N - 1) as n:
                body(n, False, False)
            body(N - 1, False, True)

        @block.vector
        def _(dve):
            for i, w in enumerate("rkv"):
                for k in range(KD):
                    dve.wait_ge(w_hi_set, i * KD + k + 1)
                    nc.vector.tensor_tensor(w_lo[w][:, k, :], ps_t[k % 2][:, :], w_hi[w][:, k, :].bitcast(F32),
                                            ALU.subtract).then_inc(w_lo_set, 1)

            def statistics(n, first_tile=False):
                dve.wait_ge(u_loaded, 16 * (n + 1))
                for c in range(C):
                    nc.vector.bn_stats(bn[:, c, :], u[:, c, :]).then_inc(bn_done, 1)
                dve.wait_ge(bn_done, (n + 1) * C)
                if not first_tile:
                    dve.wait_ge(ln_done, 2 * n)
                    apart(dve, dve_passed)
                for c in range(C):
                    last = nc.vector.bn_aggr(mv[:, c, :], bn[:, c, :])
                last.then_inc(mv_done, 1)

            def mix(n, w, first_tile=False):
                base = KD * "kr".index(w)

                def low(k):
                    dve.wait_ge(hi_done, n * 2 * KD + base + k + 1)
                    nc.vector.tensor_tensor(x_lo[w][:, k, :], mixed[:, base + k, :],
                                            x_hi[w][:, k, :].bitcast(F32), ALU.subtract).then_inc(lo_done, 1)

                if not first_tile:
                    dve.wait_ge(lo_done, n * 2 * KD - KD + base)
                    dve.wait_ge(k_done if w == "k" else r_done, n * KD)
                for k in range(KD):
                    dve.wait_ge(diff_done, n * KD + k + 1)
                    nc.vector.scalar_tensor_tensor(mixed[:, base + k, :], dt_[:, k, :], mu[w][:, k:k + 1],
                                                   xt[:, k, 0:T], ALU.mult, ALU.add).then_inc(mixed_done, 1)
                    if k >= 1:
                        low(k - 1)
                low(KD - 1)

            def squares(n, first_tile):
                def low(m):
                    dve.wait_ge(kahi_done, n * KD + m + 1)
                    nc.vector.tensor_tensor(ka_lo[:, m, :], ka[:, m, :], ka_hi[:, m, :].bitcast(F32),
                                            ALU.subtract).then_inc(kalo_done, 1)
                if not first_tile:
                    dve.wait_ge(kalo_done, n * KD)
                    dve.wait_ge(v_done, n * C)
                for m in range(KD):
                    dve.wait_ge(kr_done, n * KD + m + 1)
                    nc.vector.tensor_tensor(ka[:, m, :], kr[:, m, :], kr[:, m, :], ALU.mult).then_inc(ka_done, 1)
                    if m >= 1:
                        low(m - 1)
                low(KD - 1)

            def gated(n, c):
                dve.wait_ge(v_done, n * C + c + 1)
                dve.wait_ge(tr_done, n * C + c + 1)
                nc.vector.scalar_tensor_tensor(f2[:, c, :], tr[:, c, :], 1.0, ps_v[c % 2][:, :], ALU.add,
                                               ALU.mult).then_inc(f2_done, 1)

            def silu_gate(n, c):
                dve.wait_ge(tg_done, n * C + c + 1)
                nc.vector.scalar_tensor_tensor(g4[:, c, :], tg[:, c, :], 1.0, f2[:, c, :], ALU.add,
                                               ALU.mult).then_inc(g4_done, 1)

            def body(n, first_tile, last_tile):
                if not last_tile:
                    statistics(n + 1)
                squares(n, first_tile)
                if not last_tile:
                    mix(n + 1, "k")
                if not first_tile:
                    dve.wait_ge(g4_done, n * C)
                gated(n, 0)
                gated(n, 1)
                if not first_tile:
                    dve.wait_ge(g_stored, 16 * n)
                silu_gate(n, 0)
                silu_gate(n, 1)
                if not last_tile:
                    mix(n + 1, "r")
                gated(n, 2)
                gated(n, 3)
                silu_gate(n, 2)
                silu_gate(n, 3)

            dve.wait_ge(mu_loaded, 32)
            statistics(0, first_tile=True)
            mix(0, "k", first_tile=True)
            mix(0, "r", first_tile=True)
            body(0, True, False)
            with dve.Fori(1, N - 1) as n:
                body(n, False, False)
            body(N - 1, False, True)

        @block.tensor
        def _(pe):
            for i, w in enumerate("rkv"):
                pe.wait_ge(w_loaded[w], 16)
                for k in range(KD):
                    q = i * KD + k
                    if q >= 2:
                        pe.wait_ge(w_lo_set, q - 1)
                    for o in range(KD):
                        last = nc.tensor.transpose(ps_t[k % 2][:, o * P:(o + 1) * P],
                                                   w_raw[w][:, o, k * P:(k + 1) * P], ident[:, :])
                    last.then_inc(w_turned, 1)

            def turn(n, first_tile=False):
                pe.wait_ge(xn_done, (n + 1) * C)
                for k in range(KD):
                    if first_tile and k < 2:
                        pe.wait_ge(w_lo_set, 3 * KD)
                    else:
                        pe.wait_ge(xt_done, n * KD + k - 1)
                    for c in range(C):
                        last = nc.tensor.transpose(ps_t[k % 2][:, c * P:(c + 1) * P], xn[:, c, k * P:(k + 1) * P],
                                                   ident[:, :])
                    last.then_inc(turned, 1)

            def product(out, lhs_hi, lhs_lo, rhs_hi, rhs_lo):
                pairs = [(lhs_hi, rhs_hi), (lhs_hi, rhs_lo), (lhs_lo, rhs_hi)]
                for k in range(KD):
                    for j, (a, b) in enumerate(pairs):
                        last = nc.tensor.matmul(out, a(k), b(k), start=(k == 0 and j == 0),
                                                stop=(k == KD - 1 and j == 2))
                return last

            def body(n, first_tile, last_tile):
                pe.wait_ge(lo_done, n * 2 * KD + KD)
                for m in range(KD):
                    if not (first_tile and m < 2):
                        pe.wait_ge(kr_done, n * KD + m - 1)
                    product(ps_k[m % 2][:, :],
                            lambda k: w_hi["k"][:, k, m * P:(m + 1) * P], lambda k: w_lo["k"][:, k, m * P:(m + 1) * P],
                            lambda k: x_hi["k"][:, k, :], lambda k: x_lo["k"][:, k, :]).then_inc(k_done, 1)
                pe.wait_ge(lo_done, (n + 1) * 2 * KD)
                for c in range(C):
                    if not (first_tile and c < 2):
                        pe.wait_ge(tr_done, n * C + c - 1)
                    product(ps_r[c % 2][:, :],
                            lambda k: x_hi["r"][:, k, c * P:(c + 1) * P], lambda k: x_lo["r"][:, k, c * P:(c + 1) * P],
                            lambda k: w_hi["r"][:, k, :], lambda k: w_lo["r"][:, k, :]).then_inc(r_done, 1)
                if not last_tile:
                    turn(n + 1)
                pe.wait_ge(kalo_done, (n + 1) * KD)
                for c in range(C):
                    if not (first_tile and c < 2):
                        pe.wait_ge(f2_done, n * C + c - 1)
                    product(ps_v[c % 2][:, :],
                            lambda k: ka_hi[:, k, c * P:(c + 1) * P], lambda k: ka_lo[:, k, c * P:(c + 1) * P],
                            lambda k: w_hi["v"][:, k, :], lambda k: w_lo["v"][:, k, :]).then_inc(v_done, 1)

            turn(0, first_tile=True)
            body(0, True, False)
            with pe.Fori(1, N - 1) as n:
                body(n, False, False)
            body(N - 1, False, True)


D_INNER, D_STATE, N_HEAD, HEAD, N_TAP = 1024, 128, 16, 64, 4
RMS_EPS = 1e-5
W_X = D_INNER
W_DT = 2 * D_INNER + 2 * D_STATE
W_ALL = W_DT + N_HEAD


def ssm_phase(nc, u_rows, w_in, conv_w, conv_b, dt_bias, a_log, d_skip, norm_w, w_out, gate_rows, out_rows,
              ident, ln_scale, ln_shift, n_tok, n_batch):
    C = 2
    T = C * P
    N = n_tok // T
    N_PER_BATCH = N // n_batch
    XT = D_INNER // P
    NT = XT + 2
    B_TILE, C_TILE = XT, XT + 1
    ORDER = [B_TILE, C_TILE] + list(range(XT))
    HALF = N_HEAD // 2
    LO = 32

    ctx = ExitStack()
    with ctx:
        def sb(name, shape, dt=F32):
            return ctx.enter_context(nc.sbuf_tensor("s_" + name, shape, dt))

        def ps(name):
            return ctx.enter_context(nc.psum_tensor("s_" + name, [P, 512], F32))

        def sem(name):
            return ctx.enter_context(nc.semaphore("s_" + name))

        w_hi = sb("w_hi", [P, KD, W_ALL], F32R)
        w_lo = sb("w_lo", [P, KD, W_ALL], F32R)
        wo_hi = sb("wo_hi", [P, XT, DM], F32R)
        wo_lo = sb("wo_lo", [P, XT, DM], F32R)
        tri = sb("tri", [P, P])
        pick = sb("pick", [LO + N_HEAD, N_HEAD], F32R)
        ones_row = sb("ones_row", [1, P])
        taps = sb("taps", [P, NT, N_TAP])
        tap_bias = sb("tap_bias", [P, NT])
        dtb = sb("dtb", [N_HEAD, 1])
        head_rows = sb("head_rows", [1, 2 * N_HEAD])
        head_params = sb("head_params", [P, 2 * N_HEAD])
        norm_cols = sb("norm_cols", [P, XT])
        keep = sb("keep", [P, N])
        keep_now = sb("keep_now", [P, 1])
        minus_half = sb("minus_half", [P, 1])
        ones = sb("ones", [P, 1])

        u = sb("u", [P, C, DM])
        residual = sb("residual", [P, C, DM])
        gate = sb("gate", [P, C, DM])
        scale = sb("scale", [P, C])
        shift = sb("shift", [P, C])
        xn = sb("xn", [P, DM])
        x_hi = sb("x_hi", [P, KD, T], F32R)
        x_lo = sb("x_lo", [P, KD, T], F32R)
        raw = sb("raw", [P, 2, T + N_TAP - 1])
        edges = sb("edges", [P, NT, N_TAP - 1])
        acc = sb("acc", [P, 2, T])
        act_x = sb("act_x", [P, 2, T])
        bt = sb("bt", [P, T])
        ct = sb("ct", [P, T])
        b_tok = sb("b_tok", [P, C, D_STATE])
        x_tok = sb("x_tok", [P, C, D_INNER])
        xd = sb("xd", [P, C, D_INNER])
        xdd = sb("xdd", [P, C, D_INNER])
        sp = sb("sp", [P, 6, C * N_HEAD])
        dtv = sb("dtv", [P, C, N_HEAD])
        a_dup = sb("a_dup", [P, C, LO + N_HEAD])
        cum_rows = sb("cum_rows", [N_HEAD, T])
        dt_raw = cum_rows
        cum_parts = sb("cum_parts", [LO + N_HEAD, T], F32R)
        cum = sb("cum", [P, C, N_HEAD])
        grow = sb("grow", [P, C, N_HEAD])
        chunk_decay = sb("chunk_decay", [P, C, N_HEAD])
        tail = sb("tail", [P, C, N_HEAD])
        tail_decay = sb("tail_decay", [P, C, N_HEAD])
        lm = sb("lm", [P, N_HEAD, C, P])
        gm = sb("gm", [P, C, P])
        gz = sb("gz", [P, C, D_INNER])
        part = sb("part", [P, 2, 512])
        state = sb("state", [P, D_INNER])
        ssq = sb("ssq", [P, C])
        rms = sb("rms", [P, C, 2])
        y_hi = sb("y_hi", [P, XT, P], F32R)
        y_lo = sb("y_lo", [P, XT, P], F32R)

        turn_ps = [ps("turn0"), ps("turn1")]
        proj_ps = [ps("proj0"), ps("proj1")]
        cum_ps = ps("cum_ps")
        off_ps = ps("off_ps")
        diag_ps = ps("diag_ps")
        state_ps = ps("state_ps")
        small = cum_ps
        dt_ps = small[0:N_HEAD, 0:T]
        dtt_ps = small[:, 256:288]
        cumr_ps = small[0:LO + N_HEAD, 0:T]
        cumt_ps = small[:, 288:320]
        last_ps = small[:, 320:352]
        pair_ps = [turn_ps[0][:, 0:T], turn_ps[1][:, 0:T]]
        z_ps = [state_ps, off_ps, proj_ps[0], proj_ps[1]]
        out_ps = [off_ps, diag_ps]
        CH = [(0, 0), (1, 0), (0, 1), (1, 1)]

        names = """w0_loaded w1_loaded grow_kept chunk_kept keep_set w_hi_set w_lo_set wo_hi_set taps_halved wo_lo_set wo_loaded wo_scaled params_loaded consts pool_step head_ps heads_exp heads_set
            u_loaded rest_loaded out_stored norm_set xn_done turned xhi_done xlo_done
            dt_done dtraw_done dtt_done sp_act sp_step dt_set a_set cumr_done cumrows_done cumhi_done cumlo_done
            cumt_done cum_set grow_set last_done chunk_set tail_set taild_set
            proj_done edge_in raw_done edge_out acc_done tap_done tanh_done conv_done
            pair_done pair_copied xd_done xdd_done skip_done gm_done
            cumb_done relu_done exp_done lm_done z_done tz_done gz_done
            off_done st_done diag_done decayed state_set part_off part_sum sum_done y_done sq_done rms_step
            y_turned yhi_done ylo_done out_done o_mult o_done
            pool_passed pe_passed sp_passed""".split()
        S = {n: sem(n) for n in names}

        def rows(t, n):
            return t[bass.ds(n * T, T), :].rearrange("(c p) d -> p c d", p=P)

        def heads(ap):
            return ap.unsqueeze(-1).to_broadcast([P, ap.shape[-1], HEAD])

        STAGE = [lm[:, :, :, :].rearrange("p h c l -> p (h c l)"),
                 x_tok[:, :, :].rearrange("p c d -> p (c d)")]
        STAGE2 = [xd[:, :, :].rearrange("p c d -> p (c d)"), xdd[:, :, :].rearrange("p c d -> p (c d)")]

        block = ctx.enter_context(nc.Block())

        @block.sync
        def _(sp_):
            wv = w_in.rearrange("(k p) n -> k p n", p=P)
            WH = W_ALL // 2
            for k in range(KD):
                for h in range(2):
                    q = 2 * k + h
                    if q >= 2:
                        sp_.wait_ge(S["w_lo_set"], q - 1)
                    sp_.dma_start(STAGE2[h][:, 0:WH], wv[k, :, h * WH:(h + 1) * WH]).then_inc(S[f"w{h}_loaded"], 16)
            sp_.dma_start(STAGE[0][:, 0:XT * DM].rearrange("p (j d) -> p j d", d=DM),
                          w_out.rearrange("(j p) d -> p j d", p=P)).then_inc(S["wo_loaded"], 16)
            slow = dict(allow_slow_non_contiguous=True)
            sp_.dma_start(taps[:, :, :], conv_w.rearrange("(j p) t -> p j t", p=P)).then_inc(S["params_loaded"], 16)
            sp_.dma_start(tap_bias[:, :], column(conv_b), **slow).then_inc(S["params_loaded"], 16)
            sp_.dma_start(norm_cols[:, :], column(norm_w), **slow).then_inc(S["params_loaded"], 16)
            sp_.dma_start(dtb[:, :], dt_bias.rearrange("(h a) -> h a", a=1)).then_inc(S["params_loaded"], 16)
            sp_.dma_start(head_rows[:, 0:N_HEAD], a_log.rearrange("(a h) -> a h", a=1)).then_inc(S["params_loaded"], 16)
            sp_.dma_start(head_rows[:, N_HEAD:], d_skip.rearrange("(a h) -> a h", a=1)).then_inc(S["params_loaded"], 16)
            sp_.dma_start(u[:, :, :], rows(u_rows, 0)).then_inc(S["u_loaded"], 16)

            def body(n, first_tile, last_tile):
                if not last_tile:
                    sp_.wait_ge(S["xn_done"], (n + 1) * C)
                    sp_.dma_start(u[:, :, :], rows(u_rows, n + 1)).then_inc(S["u_loaded"], 16)
                if not first_tile:
                    sp_.wait_ge(S["o_done"], C * n)
                    sp_.dma_start(rows(out_rows, n - 1), gate[:, :, :]).then_inc(S["out_stored"], 16)
                    sp_.wait_ge(S["out_stored"], 16 * n)
                sp_.dma_start(gate[:, :, :], rows(gate_rows, n)).then_inc(S["rest_loaded"], 16)
                sp_.dma_start(residual[:, :, :], rows(u_rows, n)).then_inc(S["rest_loaded"], 16)

            body(0, True, False)
            with sp_.Fori(1, N - 1) as n:
                body(n, False, False)
            body(N - 1, False, True)
            sp_.wait_ge(S["o_done"], C * N)
            sp_.dma_start(rows(out_rows, N - 1), gate[:, :, :]).then_inc(S["out_stored"], 16)
            sp_.wait_ge(S["out_stored"], 16 * N)

        @block.gpsimd
        def _(pool):
            pool.memset(tri[:, :], 1.0).then_inc(S["pool_step"], 1)
            pool.memset(part[0:LO + N_HEAD, 0, 0:N_HEAD], 0.0).then_inc(S["pool_step"], 1)
            pool.memset(keep[:, :], 1.0).then_inc(S["pool_step"], 1)
            pool.memset(ones_row[:, :], 1.0).then_inc(S["consts"], 1)
            pool.memset(minus_half[:, :], -0.5).then_inc(S["consts"], 1)
            pool.memset(ones[:, :], 1.0).then_inc(S["consts"], 1)
            pool.memset(a_dup[:, :, :], 0.0).then_inc(S["consts"], 1)
            pool.memset(state[:, :], 0.0).then_inc(S["consts"], 1)
            pool.memset(edges[:, :, :], 0.0).then_inc(S["consts"], 1)
            pool.wait_ge(S["pool_step"], 3)
            pool.affine_select(out=tri[:, :], in_=tri[:, :], compare_op=ALU.is_ge, fill=0.0, base=0,
                               pattern=[[1, P]], channel_multiplier=-1).then_inc(S["consts"], 1)
            select = part[0:LO + N_HEAD, 0, 0:N_HEAD]
            for i, start in enumerate((0, LO)):
                pool.affine_select(out=select, in_=select, compare_op=ALU.not_equal, fill=1.0, base=-start,
                                   pattern=[[-1, N_HEAD]], channel_multiplier=1).then_inc(S["pool_step"], 1)
                pool.wait_ge(S["pool_step"], 4 + i)
            nc.gpsimd.tensor_copy(pick[:, :], select).then_inc(S["consts"], 1)
            for b in range(1, n_batch):
                pool.memset(keep[:, b * N_PER_BATCH:b * N_PER_BATCH + 1], 0.0).then_inc(S["consts"], 1)
            pool.wait_ge(S["consts"], 7 + n_batch)

            def norm(n, first_tile=False):
                if not first_tile:
                    pool.wait_ge(S["xn_done"], n * C)
                    apart(pool, S["pool_passed"])
                nc.gpsimd.tensor_copy(scale[:, :], ln_scale[:, bass.ds(n * C, C)]).then_inc(S["norm_set"], 1)
                nc.gpsimd.tensor_copy(shift[:, :], ln_shift[:, bass.ds(n * C, C)]).then_inc(S["norm_set"], 1)

            def edge_before(n, q, first_tile):
                j = ORDER[q]
                if q >= 2:
                    pool.wait_ge(S["tap_done"], (n * NT + q - 1) * 3)
                    pool.wait_ge(S["edge_out"], n * NT + q - 1)
                elif not first_tile:
                    pool.wait_ge(S["tap_done"], n * NT * 3)
                    pool.wait_ge(S["edge_out"], n * NT)
                nc.gpsimd.tensor_tensor(raw[:, q % 2, 0:N_TAP - 1], edges[:, j, :],
                                        keep_now[:, :].to_broadcast([P, N_TAP - 1]), ALU.mult)\
                    .then_inc(S["edge_in"], 1)

            def edge_after(n, q):
                pool.wait_ge(S["raw_done"], n * NT + q + 1)
                pool.wait_ge(S["edge_in"], n * NT + q + 1)
                nc.gpsimd.tensor_tensor(edges[:, ORDER[q], :], raw[:, q % 2, T:T + N_TAP - 1],
                                        ones[:, :].to_broadcast([P, N_TAP - 1]), ALU.mult)\
                    .then_inc(S["edge_out"], 1)

            def to_end(n, j, first_tile):
                cols = slice(j * P, (j + 1) * P)
                pool.wait_ge(S["xd_done"], n * XT + j + 1)
                if j == 0:
                    pool.wait_ge(S["taild_set"], n + 1)
                    if not first_tile:
                        pool.wait_ge(S["st_done"], 4 * n)
                for c in range(C):
                    nc.gpsimd.tensor_tensor(xdd[:, c, cols].rearrange("p (h d) -> p h d", d=HEAD),
                                            xd[:, c, cols].rearrange("p (h d) -> p h d", d=HEAD),
                                            heads(tail_decay[:, c, 2 * j:2 * j + 2]), ALU.mult)\
                        .then_inc(S["xdd_done"], 1)

            def skip(n, j):
                pool.wait_ge(S["xd_done"], n * XT + j + 1)
                for c in range(C):
                    v = x_tok[:, c, j * P:(j + 1) * P].rearrange("p (h d) -> p h d", d=HEAD)
                    nc.gpsimd.tensor_tensor(v, v, heads(head_params[:, N_HEAD + 2 * j:N_HEAD + 2 * j + 2]),
                                            ALU.mult).then_inc(S["skip_done"], 1)

            def keep_decays(n):
                pool.wait_ge(S["keep_set"], n + 1)
                pool.wait_ge(S["grow_set"], n + 1)
                k = keep_now[:, :].to_broadcast([P, N_HEAD])
                nc.gpsimd.tensor_tensor(grow[:, 0, :], grow[:, 0, :], k, ALU.mult).then_inc(S["grow_kept"], 1)
                pool.wait_ge(S["chunk_set"], n + 1)
                nc.gpsimd.tensor_tensor(chunk_decay[:, 0, :], chunk_decay[:, 0, :], k, ALU.mult)\
                    .then_inc(S["chunk_kept"], 1)

            def decay_state(n, i):
                c, h = CH[i]
                pool.wait_ge(S["off_done"], n * 4 + i + 1)
                if c:
                    pool.wait_ge(S["state_set"], n * 4 + i)
                else:
                    pool.wait_ge(S["chunk_kept"], n + 1)
                v = state[:, h * 512:(h + 1) * 512].rearrange("p (h d) -> p h d", d=HEAD)
                nc.gpsimd.tensor_tensor(v, v, heads(chunk_decay[:, c, h * HALF:(h + 1) * HALF]), ALU.mult)\
                    .then_inc(S["decayed"], 1)

            def add_and_gate(n, i):
                c, h = CH[i]
                cols = slice(h * 512, (h + 1) * 512)
                pool.wait_ge(S["skip_done"], n * XT * C + (h + 1) * XT)
                pool.wait_ge(S["part_sum"], n * 4 + i + 1)
                nc.gpsimd.tensor_tensor(x_tok[:, c, cols], x_tok[:, c, cols], part[:, i % 2, :], ALU.add)\
                    .then_inc(S["sum_done"], 1)
                pool.wait_ge(S["sum_done"], n * 4 + i + 1)
                pool.wait_ge(S["gz_done"], n * 4 + i + 1)
                nc.gpsimd.tensor_tensor(x_tok[:, c, cols], x_tok[:, c, cols], gz[:, c, cols], ALU.mult)\
                    .then_inc(S["y_done"], 1)

            def rms_factor(n, c):
                pool.wait_ge(S["sq_done"], n * C + c + 1)
                apart(pool, S["pool_passed"])
                nc.gpsimd.tensor_scalar(rms[:, c, 0:1], ssq[:, c:c + 1], 64.0 / (4 * D_INNER), 64 * RMS_EPS,
                                        ALU.mult, ALU.add).then_inc(S["rms_step"], 1)
                pool.wait_ge(S["rms_step"], n * 4 + c * 2 + 1)
                nc.gpsimd.tensor_tensor(rms[:, c, 1:2], rms[:, c, 0:1], minus_half[:, :], ALU.pow)\
                    .then_inc(S["rms_step"], 1)

            def add_residual(n, c):
                pool.wait_ge(S["o_mult"], n * C + c + 1)
                nc.gpsimd.tensor_tensor(gate[:, c, :], gate[:, c, :], residual[:, c, :], ALU.add)\
                    .then_inc(S["o_done"], 1)

            def body(n, first_tile, last_tile):
                if not first_tile:
                    pool.wait_ge(S["edge_in"], n * NT)
                    pool.wait_ge(S["chunk_kept"], n)
                    apart(pool, S["pool_passed"])
                nc.gpsimd.tensor_copy(keep_now[:, :], keep[:, bass.ds(n, 1)]).then_inc(S["keep_set"], 1)
                pool.wait_ge(S["keep_set"], n + 1)

                def edge(q):
                    if q < NT:
                        edge_before(n, q, first_tile)

                edge(0)
                edge(1)
                if not first_tile:
                    add_and_gate(n - 1, 3)
                edge_after(n, 0)
                edge(2)
                if not first_tile:
                    rms_factor(n - 1, 0)
                edge_after(n, 1)
                edge(3)
                if not first_tile:
                    rms_factor(n - 1, 1)
                keep_decays(n)
                edge_after(n, 2)
                edge(4)
                if not first_tile:
                    add_residual(n - 1, 0)
                edge_after(n, 3)
                edge(5)
                edge_after(n, 4)
                edge(6)
                for q in range(5, 10):
                    edge_after(n, q)
                    edge(q + 2)
                    to_end(n, q - 5, first_tile)
                    if q == 8:
                        decay_state(n, 0)
                    if q < 9:
                        skip(n, q - 5)
                    if q == 6 and not last_tile:
                        norm(n + 1)
                    if q == 7 and not first_tile:
                        add_residual(n - 1, 1)
                to_end(n, 5, first_tile)
                decay_state(n, 1)
                add_and_gate(n, 0)
                to_end(n, 6, first_tile)
                skip(n, 4)
                to_end(n, 7, first_tile)
                decay_state(n, 2)
                skip(n, 5)
                add_and_gate(n, 1)
                skip(n, 6)
                skip(n, 7)
                add_and_gate(n, 2)
                decay_state(n, 3)

            norm(0, first_tile=True)
            body(0, True, False)
            with pool.Fori(1, N - 1) as n:
                body(n, False, False)
            body(N - 1, False, True)
            add_and_gate(N - 1, 3)
            for c in range(C):
                rms_factor(N - 1, c)
                add_residual(N - 1, c)

        @block.scalar
        def _(act):
            WH = W_ALL // 2
            for q in range(2 * KD):
                k, h = q // 2, q % 2
                act.wait_ge(S[f"w{h}_loaded"], 16 * (k + 1))
                nc.scalar.activation(w_hi[:, k, h * WH:(h + 1) * WH], STAGE2[h][:, 0:WH], ACT.Copy)\
                    .then_inc(S["w_hi_set"], 1)
            for j in range(XT):
                act.wait_ge(S["wo_scaled"], j + 1)
                nc.scalar.activation(wo_hi[:, j, :], STAGE[0][:, j * DM:(j + 1) * DM], ACT.Copy)\
                    .then_inc(S["wo_hi_set"], 1)
            act.wait_ge(S["head_ps"], 1)
            nc.scalar.activation(head_params[:, 0:N_HEAD], cum_ps[:, 0:N_HEAD], ACT.Exp).then_inc(S["heads_exp"], 1)
            nc.scalar.activation(head_params[:, N_HEAD:], cum_ps[:, N_HEAD:2 * N_HEAD], ACT.Copy)\
                .then_inc(S["heads_set"], 1)

            def normalise(n, c, first_tile=False):
                act.wait_ge(S["norm_set"], 2 * (n + 1))
                act.wait_ge(S["u_loaded"], 16 * (n + 1))
                if c == 1:
                    act.wait_ge(S["turned"], n * C + 1)
                elif not first_tile:
                    act.wait_ge(S["turned"], n * C)
                nc.scalar.activation(xn[:, :], u[:, c, :], ACT.Identity, bias=shift[:, c:c + 1],
                                     scale=scale[:, c:c + 1]).then_inc(S["xn_done"], 1)

            def high(n, c):
                act.wait_ge(S["turned"], n * C + c + 1)
                nc.scalar.activation(x_hi[:, :, c * P:(c + 1) * P],
                                     turn_ps[c][:, :].rearrange("p (k t) -> p k t", t=P), ACT.Copy)\
                    .then_inc(S["xhi_done"], 1)

            def conv_in(n, q, first_tile):
                j = ORDER[q]
                act.wait_ge(S["proj_done"], n * NT + q + 1)
                act.wait_ge(S["edge_in"], n * NT + q + 1)
                nc.scalar.activation(raw[:, q % 2, N_TAP - 1:], proj_ps[q % 2][:, 0:T], ACT.Copy)\
                    .then_inc(S["raw_done"], 1)
                if q >= 2 or not first_tile:
                    act.wait_ge(S["conv_done"], n * NT + max(q - 1, 0))
                nc.scalar.activation(acc[:, q % 2, :], proj_ps[q % 2][:, 0:T], ACT.Identity,
                                     bias=tap_bias[:, j:j + 1], scale=taps[:, j, N_TAP - 1:N_TAP])\
                    .then_inc(S["acc_done"], 1)

            def conv_tanh(n, q, first_tile):
                act.wait_ge(S["tap_done"], (n * NT + q + 1) * 3)
                if q >= 4:
                    act.wait_ge(S["pair_done"], n * (XT + 2) + q - 1)
                elif q >= 2:
                    act.wait_ge(S["conv_done"], n * NT + q - 1)
                elif not first_tile:
                    act.wait_ge(S["pair_done"], n * (XT + 2))
                nc.scalar.activation(act_x[:, q % 2, :], acc[:, q % 2, :], ACT.Tanh).then_inc(S["tanh_done"], 1)

            def x_copy(n, j, first_tile):
                act.wait_ge(S["pair_done"], n * (XT + 2) + j + 3)
                if j == 0 and not first_tile:
                    act.wait_ge(S["y_turned"], 4 * n)
                    act.wait_ge(S["sq_done"], C * n)
                nc.scalar.activation(x_tok[:, :, j * P:(j + 1) * P],
                                     pair_ps[j % 2].rearrange("p (c d) -> p c d", d=P), ACT.Copy)\
                    .then_inc(S["pair_copied"], 1)

            def decay_heads(n, first, first_tile):
                for h in (first, first + 1):
                    act.wait_ge(S["cumb_done"], n * N_HEAD + first + 2)
                    if h == 0 and not first_tile:
                        act.wait_ge(S["diag_done"], 4 * n)
                    for c in range(C):
                        nc.scalar.activation(lm[:, h, c, :], cum_ps[:, (h % 2) * T + c * P:(h % 2) * T + (c + 1) * P],
                                             ACT.Relu, bias=cum[:, c, h:h + 1], scale=-1.0)\
                            .then_inc(S["relu_done"], 1)
                act.wait_ge(S["relu_done"], (n * N_HEAD + first + 2) * C)
                v = lm[:, first:first + 2, :, :].rearrange("p h c l -> p (h c l)")
                nc.scalar.activation(v, v, ACT.Exp, scale=-1.0).then_inc(S["exp_done"], 1)

            def z_tanh(n, i, first_tile):
                c, h = CH[i]
                act.wait_ge(S["z_done"], n * 4 + i + 1)
                if not first_tile and i == 0:
                    act.wait_ge(S["y_done"], 4 * n)
                nc.scalar.activation(gz[:, c, h * 512:(h + 1) * 512], z_ps[i][:, :], ACT.Tanh, scale=0.5)\
                    .then_inc(S["tz_done"], 1)

            def squares(n, c):
                act.wait_ge(S["y_done"], n * 4 + 3 + c)
                nc.scalar.activation(xd[:, c, :], x_tok[:, c, :], ACT.Square, accum_out=ssq[:, c:c + 1])\
                    .then_inc(S["sq_done"], 1)

            def y_high(n, c):
                for r in range(2):
                    act.wait_ge(S["y_turned"], n * 4 + 2 * c + r + 1)
                    if c and r == 0:
                        act.wait_ge(S["out_done"], n * C + c)
                    nc.scalar.activation(y_hi[:, 4 * r:4 * r + 4, :],
                                         turn_ps[r][:, :].rearrange("p (j t) -> p j t", t=P), ACT.Copy)\
                        .then_inc(S["yhi_done"], 1)

            def body(n, first_tile, last_tile):
                act.wait_ge(S["dt_done"], n + 1)
                if not first_tile:
                    act.wait_ge(S["cumt_done"], n)
                nc.scalar.activation(dt_raw[:, :], dt_ps, ACT.Identity, bias=dtb[:, 0:1]).then_inc(S["dtraw_done"], 1)
                act.wait_ge(S["dtt_done"], n + 1)
                if not first_tile:
                    act.wait_ge(S["dt_set"], n)
                nc.scalar.activation(sp[:, 0, :], dtt_ps, ACT.Abs).then_inc(S["sp_act"], 1)
                act.wait_ge(S["sp_act"], 2 * n + 1)
                nc.scalar.activation(sp[:, 1, :], sp[:, 0, :], ACT.Exp, scale=-1.0).then_inc(S["sp_act"], 1)
                conv_in(n, 0, first_tile)
                if not first_tile:
                    y_high(n - 1, 0)
                conv_in(n, 1, first_tile)
                if not first_tile:
                    squares(n - 1, 0)
                act.wait_ge(S["cumr_done"], n + 1)
                if not first_tile:
                    act.wait_ge(S["cumb_done"], n * N_HEAD)
                    act.wait_ge(S["cumt_done"], n)
                nc.scalar.activation(cum_parts[:, :], cumr_ps, ACT.Copy).then_inc(S["cumhi_done"], 1)
                nc.scalar.activation(cum_rows[:, :], small[0:N_HEAD, 0:T], ACT.Copy).then_inc(S["cumrows_done"], 1)
                z_tanh(n, 0, first_tile)
                conv_tanh(n, 0, first_tile)
                if not first_tile:
                    squares(n - 1, 1)
                act.wait_ge(S["cumt_done"], n + 1)
                if not first_tile:
                    act.wait_ge(S["relu_done"], n * N_HEAD * C)
                    act.wait_ge(S["tail_set"], 2 * n)
                nc.scalar.activation(cum[:, :, :].rearrange("p c h -> p (c h)"), cumt_ps, ACT.Copy)\
                    .then_inc(S["cum_set"], 1)
                if not first_tile:
                    act.wait_ge(S["part_off"], 4 * n)
                nc.scalar.activation(grow[:, :, :].rearrange("p c h -> p (c h)"), cumt_ps, ACT.Exp)\
                    .then_inc(S["grow_set"], 1)
                conv_tanh(n, 1, first_tile)
                conv_in(n, 2, first_tile)
                act.wait_ge(S["last_done"], n + 1)
                if not first_tile:
                    act.wait_ge(S["decayed"], 4 * n)
                nc.scalar.activation(chunk_decay[:, :, :].rearrange("p c h -> p (c h)"), last_ps, ACT.Exp)\
                    .then_inc(S["chunk_set"], 1)
                act.wait_ge(S["tail_set"], 2 * (n + 1))
                if not first_tile:
                    act.wait_ge(S["xdd_done"], n * XT * C)
                nc.scalar.activation(tail_decay[:, :, :], tail[:, :, :], ACT.Exp, scale=-1.0)\
                    .then_inc(S["taild_set"], 1)
                if not first_tile:
                    y_high(n - 1, 1)
                decay_heads(n, 0, first_tile)
                conv_in(n, 3, first_tile)
                conv_tanh(n, 2, first_tile)
                decay_heads(n, 2, first_tile)
                conv_in(n, 4, first_tile)
                act.wait_ge(S["pair_done"], n * (XT + 2) + 1)
                if not first_tile:
                    act.wait_ge(S["st_done"], 4 * n)
                nc.scalar.activation(b_tok[:, :, :], pair_ps[0].rearrange("p (c d) -> p c d", d=P), ACT.Copy)\
                    .then_inc(S["pair_copied"], 1)
                conv_tanh(n, 3, first_tile)
                for q in range(4, 10):
                    if q > 4:
                        conv_in(n, q, first_tile)
                    decay_heads(n, 2 * q - 4, first_tile)
                    if q == 7:
                        z_tanh(n, 1, first_tile)
                    x_copy(n, q - 4, first_tile)
                    conv_tanh(n, q, first_tile)
                x_copy(n, 6, first_tile)
                z_tanh(n, 2, first_tile)
                x_copy(n, 7, first_tile)
                if not last_tile:
                    normalise(n + 1, 0)
                z_tanh(n, 3, first_tile)
                if not last_tile:
                    normalise(n + 1, 1)
                    high(n + 1, 0)
                    high(n + 1, 1)

            act.wait_ge(S["taps_halved"], 2)
            normalise(0, 0, first_tile=True)
            normalise(0, 1, first_tile=True)
            high(0, 0)
            high(0, 1)
            body(0, True, False)
            with act.Fori(1, N - 1) as n:
                body(n, False, False)
            body(N - 1, False, True)
            for c in range(C):
                squares(N - 1, c)
                y_high(N - 1, c)

        @block.vector
        def _(dve):
            WH = W_ALL // 2
            for q in range(2 * KD):
                k, h = q // 2, q % 2
                dve.wait_ge(S["w_hi_set"], q + 1)
                nc.vector.tensor_tensor(w_lo[:, k, h * WH:(h + 1) * WH], STAGE2[h][:, 0:WH],
                                        w_hi[:, k, h * WH:(h + 1) * WH].bitcast(F32), ALU.subtract)\
                    .then_inc(S["w_lo_set"], 1)
            dve.wait_ge(S["wo_loaded"], 16)
            dve.wait_ge(S["params_loaded"], 16 * 6)
            nc.vector.tensor_scalar(taps[:, :, :], taps[:, :, :], 0.5, None, ALU.mult).then_inc(S["taps_halved"], 1)
            nc.vector.tensor_scalar(tap_bias[:, :], tap_bias[:, :], 0.5, None, ALU.mult).then_inc(S["taps_halved"], 1)
            for j in range(XT):
                w = STAGE[0][:, j * DM:(j + 1) * DM]
                nc.vector.tensor_scalar(w, w, norm_cols[:, j:j + 1], None, ALU.mult).then_inc(S["wo_scaled"], 1)
                dve.wait_ge(S["wo_hi_set"], j + 1)
                nc.vector.tensor_tensor(wo_lo[:, j, :], w, wo_hi[:, j, :].bitcast(F32), ALU.subtract)\
                    .then_inc(S["wo_lo_set"], 1)
            dve.wait_ge(S["heads_exp"], 1)
            nc.vector.tensor_scalar(head_params[:, 0:N_HEAD], head_params[:, 0:N_HEAD], -1.0, None, ALU.mult)\
                .then_inc(S["heads_set"], 1)
            dve.wait_ge(S["heads_set"], 2)
            dve.wait_ge(S["taps_halved"], 2)
            dve.wait_ge(S["consts"], 7 + n_batch)

            def low(n, c):
                dve.wait_ge(S["xhi_done"], n * C + c + 1)
                v = slice(c * P, (c + 1) * P)
                nc.vector.tensor_tensor(x_lo[:, :, v], turn_ps[c][:, :].rearrange("p (k t) -> p k t", t=P),
                                        x_hi[:, :, v].bitcast(F32), ALU.subtract).then_inc(S["xlo_done"], 1)

            def conv_tap(n, q, i):
                t = 2 - i
                j = ORDER[q]
                if i:
                    dve.wait_ge(S["tap_done"], (n * NT + q) * 3 + i)
                else:
                    dve.wait_ge(S["acc_done"], n * NT + q + 1)
                nc.vector.scalar_tensor_tensor(acc[:, q % 2, :], raw[:, q % 2, t:t + T], taps[:, j, t:t + 1],
                                               acc[:, q % 2, :], ALU.mult, ALU.add).then_inc(S["tap_done"], 1)

            def conv_taps(n, q, between=()):
                for i in range(3):
                    conv_tap(n, q, i)
                    if i < len(between):
                        between[i]()

            def conv_out(n, q, first_tile):
                dve.wait_ge(S["tanh_done"], n * NT + q + 1)
                if q < 2 and not first_tile:
                    dve.wait_ge(S["off_done"], 4 * n)
                out = (bt, ct)[q][:, :] if q < 2 else act_x[:, q % 2, :]
                nc.vector.scalar_tensor_tensor(out, act_x[:, q % 2, :], 1.0, acc[:, q % 2, :], ALU.add, ALU.mult)\
                    .then_inc(S["conv_done"], 1)

            def x_dt(n, j, first_tile):
                dve.wait_ge(S["pair_copied"], n * (XT + 1) + j + 2)
                if j == 0 and not first_tile:
                    dve.wait_ge(S["sq_done"], C * n)
                src = x_tok[:, :, j * P:(j + 1) * P].rearrange("p c (h d) -> p c h d", d=HEAD)
                out = xd[:, :, j * P:(j + 1) * P].rearrange("p c (h d) -> p c h d", d=HEAD)
                w = dtv[:, :, 2 * j:2 * j + 2].unsqueeze(-1).to_broadcast([P, C, 2, HEAD])
                nc.vector.tensor_tensor(out, src, w, ALU.mult).then_inc(S["xd_done"], 1)

            def softplus(n, between):
                base = [n * 14]
                count = [0]

                def step(ins):
                    base[0] = base[0] + 1
                    count[0] += 1
                    ins.then_inc(S["sp_step"], 1)
                    for work in between.get(count[0], ()):
                        work()
                    dve.wait_ge(S["sp_step"], base[0])

                e, s, s2, r, q = (sp[:, i, :] for i in (1, 2, 3, 4, 5))
                dve.wait_ge(S["sp_act"], 2 * (n + 1))
                step(nc.vector.tensor_scalar(r, e, 2.0, None, ALU.add))
                step(nc.vector.reciprocal(q, r))
                step(nc.vector.tensor_tensor(s, e, q, ALU.mult))
                step(nc.vector.tensor_tensor(s2, s, s, ALU.mult))
                step(nc.vector.tensor_scalar(q, s2, 1.0 / 17, None, ALU.mult))
                for odd in (15, 13, 11, 9, 7, 5, 3):
                    step(nc.vector.scalar_tensor_tensor(q, q, 1.0 / odd, s2, ALU.add, ALU.mult))
                step(nc.vector.scalar_tensor_tensor(q, q, 1.0, s, ALU.add, ALU.mult))
                step(nc.vector.tensor_scalar(r, dtt_ps, 0.0, None, ALU.max))
                nc.vector.scalar_tensor_tensor(dtv[:, :, :].rearrange("p c h -> p (c h)"), q, 2.0, r, ALU.mult,
                                               ALU.add).then_inc(S["dt_set"], 1)
                dve.wait_ge(S["dt_set"], n + 1)
                for start in (0, LO):
                    nc.vector.tensor_tensor(a_dup[:, :, start:start + N_HEAD], dtv[:, :, :],
                                            head_params[:, 0:N_HEAD].unsqueeze(1).to_broadcast([P, C, N_HEAD]),
                                            ALU.mult).then_inc(S["a_set"], 1)

            def z_gate(n, i):
                c, h = CH[i]
                dve.wait_ge(S["tz_done"], n * 4 + i + 1)
                v = gz[:, c, h * 512:(h + 1) * 512]
                nc.vector.scalar_tensor_tensor(v, v, 1.0, z_ps[i][:, :], ALU.add, ALU.mult)\
                    .then_inc(S["gz_done"], 1)

            def mask(n, i):
                c, h = CH[i]
                dve.wait_ge(S["exp_done"], n * HALF + (h + 1) * HALF // 2)
                v = lm[:, h * HALF:(h + 1) * HALF, c, :]
                nc.vector.tensor_tensor(v, v, gm[:, c:c + 1, :].to_broadcast([P, HALF, P]), ALU.mult)\
                    .then_inc(S["lm_done"], 1)

            def y_low(n, c, r):
                dve.wait_ge(S["yhi_done"], n * 4 + 2 * c + r + 1)
                nc.vector.tensor_tensor(y_lo[:, 4 * r:4 * r + 4, :],
                                        turn_ps[r][:, :].rearrange("p (j t) -> p j t", t=P),
                                        y_hi[:, 4 * r:4 * r + 4, :].bitcast(F32), ALU.subtract)\
                    .then_inc(S["ylo_done"], 1)

            def finish(n, c):
                dve.wait_ge(S["rest_loaded"], 32 * (n + 1))
                dve.wait_ge(S["out_done"], n * C + c + 1)
                dve.wait_ge(S["rms_step"], n * 4 + 2 * c + 2)
                nc.vector.scalar_tensor_tensor(gate[:, c, :], out_ps[c][:, :], rms[:, c, 1:2], gate[:, c, :],
                                               ALU.mult, ALU.mult).then_inc(S["o_mult"], 1)

            def from_before(n, i, first_tile):
                c, h = CH[i]
                dve.wait_ge(S["off_done"], n * 4 + i + 1)
                dve.wait_ge(S["grow_kept"], n + 1)
                if i >= 2 or not first_tile:
                    dve.wait_ge(S["sum_done"], n * 4 + i - 1)
                nc.vector.tensor_tensor(part[:, i % 2, :].rearrange("p (h d) -> p h d", d=HEAD),
                                        off_ps[:, :].rearrange("p (h d) -> p h d", d=HEAD),
                                        heads(grow[:, c, h * HALF:(h + 1) * HALF]), ALU.mult)\
                    .then_inc(S["part_off"], 1)

            def add_state(n, i):
                h = CH[i][1]
                dve.wait_ge(S["st_done"], n * 4 + i + 1)
                dve.wait_ge(S["decayed"], n * 4 + i + 1)
                v = state[:, h * 512:(h + 1) * 512]
                nc.vector.tensor_tensor(v, v, state_ps[:, :], ALU.add).then_inc(S["state_set"], 1)

            def add_within(n, i):
                dve.wait_ge(S["part_off"], n * 4 + i + 1)
                dve.wait_ge(S["diag_done"], n * 4 + i + 1)
                nc.vector.tensor_tensor(part[:, i % 2, :], part[:, i % 2, :], diag_ps[:, :], ALU.add)\
                    .then_inc(S["part_sum"], 1)

            def body(n, first_tile, last_tile):
                def out(q):
                    return lambda: conv_out(n, q, first_tile)

                def xdt(j):
                    return lambda: x_dt(n, j, first_tile)

                between = {}
                if not first_tile:
                    between = {5: [lambda: y_low(n - 1, 0, 0)], 8: [lambda: y_low(n - 1, 0, 1)]}
                    dve.wait_ge(S["xd_done"], n * XT)
                    dve.wait_ge(S["cumr_done"], n)
                softplus(n, between)
                conv_taps(n, 0)
                dve.wait_ge(S["cumhi_done"], n + 1)
                dve.wait_ge(S["cumrows_done"], n + 1)
                nc.vector.tensor_tensor(cum_parts[LO:LO + N_HEAD, :], small[LO:LO + N_HEAD, 0:T],
                                        cum_parts[LO:LO + N_HEAD, :].bitcast(F32), ALU.subtract)\
                    .then_inc(S["cumlo_done"], 1)
                conv_taps(n, 1, [lambda: z_gate(n, 0), out(0)])
                dve.wait_ge(S["chunk_set"], n + 1)
                if not first_tile:
                    dve.wait_ge(S["taild_set"], n)
                flat = tail[:, :, :].rearrange("p c h -> p (c h)")
                nc.vector.tensor_tensor(flat, cum[:, :, :].rearrange("p c h -> p (c h)"), last_ps, ALU.subtract)\
                    .then_inc(S["tail_set"], 1)
                dve.wait_ge(S["tail_set"], 2 * n + 1)
                nc.vector.tensor_scalar(flat, flat, 0.0, None, ALU.max).then_inc(S["tail_set"], 1)
                conv_taps(n, 2, [out(1)])
                if not first_tile:
                    finish(n - 1, 0)
                    y_low(n - 1, 1, 0)
                    y_low(n - 1, 1, 1)
                conv_taps(n, 3, [out(2)])
                dve.wait_ge(S["pair_done"], n * (XT + 2) + 2)
                if not first_tile:
                    dve.wait_ge(S["lm_done"], 4 * n)
                nc.vector.tensor_tensor(gm[:, :, :], pair_ps[1].rearrange("p (c l) -> p c l", l=P),
                                        tri[:, :].unsqueeze(1).to_broadcast([P, C, P]), ALU.mult)\
                    .then_inc(S["gm_done"], 1)
                conv_taps(n, 4, [out(3)])
                conv_taps(n, 5, [xdt(0), out(4)])
                conv_taps(n, 6, [xdt(1), out(5)])
                mask(n, 0)
                conv_taps(n, 7, [xdt(2), out(6)])
                z_gate(n, 1)
                if not first_tile:
                    finish(n - 1, 1)
                conv_taps(n, 8, [xdt(3), out(7)])
                mask(n, 1)
                conv_taps(n, 9, [xdt(4), out(8)])
                from_before(n, 0, first_tile)
                conv_out(n, 9, first_tile)
                add_state(n, 0)
                x_dt(n, 5, first_tile)
                add_within(n, 0)
                x_dt(n, 6, first_tile)
                from_before(n, 1, first_tile)
                z_gate(n, 2)
                x_dt(n, 7, first_tile)
                mask(n, 2)
                add_state(n, 1)
                add_within(n, 1)
                z_gate(n, 3)
                from_before(n, 2, first_tile)
                mask(n, 3)
                add_state(n, 2)
                if not last_tile:
                    low(n + 1, 0)
                add_within(n, 2)
                from_before(n, 3, first_tile)
                if not last_tile:
                    low(n + 1, 1)
                add_state(n, 3)
                add_within(n, 3)

            low(0, 0)
            low(0, 1)
            body(0, True, False)
            with dve.Fori(1, N - 1) as n:
                body(n, False, False)
            body(N - 1, False, True)
            for c in range(C):
                y_low(N - 1, c, 0)
                y_low(N - 1, c, 1)
                finish(N - 1, c)

        @block.tensor
        def _(pe):
            pe.wait_ge(S["params_loaded"], 16 * 6)
            pe.wait_ge(S["consts"], 7 + n_batch)
            nc.tensor.matmul(cum_ps[:, 0:2 * N_HEAD], ones_row[:, :], head_rows[:, :], start=True, stop=True)\
                .then_inc(S["head_ps"], 1)
            pe.wait_ge(S["heads_set"], 2)
            pe.wait_ge(S["w_lo_set"], 2 * KD)
            pe.wait_ge(S["wo_lo_set"], XT)

            def turn(n, c, first_tile=False):
                pe.wait_ge(S["xn_done"], n * C + c + 1)
                if c == 0 and not first_tile:
                    pe.wait_ge(S["pair_copied"], n * (XT + 1))
                for k in range(KD):
                    last = nc.tensor.transpose(turn_ps[c][:, k * P:(k + 1) * P], xn[:, k * P:(k + 1) * P],
                                               ident[:, :])
                last.then_inc(S["turned"], 1)

            def product(out, ks, blocks, lhs_hi, lhs_lo, rhs_hi, rhs_lo):
                pairs = [(lhs_hi, rhs_hi), (lhs_hi, rhs_lo), (lhs_lo, rhs_hi)]
                for k in ks:
                    for j, (a, b) in enumerate(pairs):
                        last = nc.tensor.matmul(out, a(k), b(k), start=(k == 0 and j == 0),
                                                stop=(k == blocks - 1 and j == 2))
                return last

            def by_channel(out, lo, width):
                return product(out, range(KD), KD, lambda k: w_hi[:, k, lo:lo + width], lambda k: w_lo[:, k, lo:lo + width],
                               lambda k: x_hi[:, k, :], lambda k: x_lo[:, k, :])

            def project(n, q, first_tile):
                if q >= 2:
                    pe.wait_ge(S["acc_done"], n * NT + q - 1)
                elif not first_tile:
                    pe.wait_ge(S["gz_done"], 4 * n - 1 + q)
                by_channel(proj_ps[q % 2][:, 0:T], W_X + ORDER[q] * P, P).then_inc(S["proj_done"], 1)

            def pair(i, src):
                for c in range(C):
                    last = nc.tensor.transpose(pair_ps[i][:, c * P:(c + 1) * P], src[:, c * P:(c + 1) * P],
                                               ident[:, :])
                last.then_inc(S["pair_done"], 1)

            def x_pair(n, j):
                pe.wait_ge(S["conv_done"], n * NT + j + 3)
                if j == 1:
                    pe.wait_ge(S["gm_done"], n + 1)
                elif j == 0:
                    pe.wait_ge(S["pair_copied"], n * (XT + 1) + 1)
                else:
                    pe.wait_ge(S["pair_copied"], n * (XT + 1) + j)
                pair(j % 2, act_x[:, j % 2, :])

            def spread(n, first):
                if first:
                    pe.wait_ge(S["relu_done"], (n * N_HEAD + first) * C)
                else:
                    pe.wait_ge(S["chunk_set"], n + 1)
                    pe.wait_ge(S["tail_set"], 2 * n + 1)
                for h in (first, first + 1):
                    nc.tensor.matmul(cum_ps[:, (h % 2) * T:(h % 2 + 1) * T],
                                     pick[:, h:h + 1].to_broadcast([LO + N_HEAD, P]), cum_parts[:, :],
                                     start=True, stop=True).then_inc(S["cumb_done"], 1)

            def z_part(n, i, first_tile):
                c, h = CH[i]
                if i == 0 and not first_tile:
                    pe.wait_ge(S["state_set"], 4 * n)
                elif i == 1 and not first_tile:
                    pe.wait_ge(S["o_mult"], C * n - 1)
                elif i >= 2:
                    pe.wait_ge(S["acc_done"], n * NT + NT - 3 + i)
                v = slice(c * P, (c + 1) * P)
                cols = slice(h * 512, (h + 1) * 512)
                product(z_ps[i][:, :], range(KD), KD, lambda k: x_hi[:, k, v], lambda k: x_lo[:, k, v],
                        lambda k: w_hi[:, k, cols], lambda k: w_lo[:, k, cols]).then_inc(S["z_done"], 1)

            def off(n, i):
                c, h = CH[i]
                if i == 0:
                    pe.wait_ge(S["gz_done"], n * 4 + 2)
                else:
                    pe.wait_ge(S["part_off"], n * 4 + i)
                if c:
                    pe.wait_ge(S["state_set"], n * 4 + i)
                nc.tensor.matmul(off_ps[:, :], ct[:, c * P:(c + 1) * P], state[:, h * 512:(h + 1) * 512],
                                 start=True, stop=True).then_inc(S["off_done"], 1)

            def new_state(n, i):
                c, h = CH[i]
                pe.wait_ge(S["xdd_done"], n * XT * C + (h + 1) * XT)
                if i:
                    pe.wait_ge(S["state_set"], n * 4 + i)
                nc.tensor.matmul(state_ps[:, :], b_tok[:, c, :], xdd[:, c, h * 512:(h + 1) * 512],
                                 start=True, stop=True).then_inc(S["st_done"], 1)

            def diag(n, i, first_tile):
                c, h = CH[i]
                pe.wait_ge(S["lm_done"], n * 4 + i + 1)
                if i:
                    pe.wait_ge(S["part_sum"], n * 4 + i)
                elif not first_tile:
                    pe.wait_ge(S["o_mult"], C * n)
                for m in range(HALF - 1, -1, -1):
                    lead = 32 if m else 0
                    lo = m * HEAD - lead
                    hi = (m + 1) * HEAD
                    last = nc.tensor.matmul(diag_ps[:, lo:hi], lm[:, h * HALF + m, c, :],
                                            xd[:, c, h * 512 + lo:h * 512 + hi], start=True, stop=True)
                last.then_inc(S["diag_done"], 1)

            def y_turn(n, c):
                pe.wait_ge(S["y_done"], n * 4 + 3 + c)
                if c:
                    pe.wait_ge(S["ylo_done"], n * 4 + 2)
                for r in range(2):
                    for j in range(4):
                        lo = (4 * r + j) * P
                        last = nc.tensor.transpose(turn_ps[r][:, j * P:(j + 1) * P], x_tok[:, c, lo:lo + P],
                                                   ident[:, :])
                    last.then_inc(S["y_turned"], 1)

            def output(n, c, blocks):
                if blocks[0] == 0:
                    pe.wait_ge(S["ylo_done"], n * 4 + 2 * c + 2)
                    pe.wait_ge(S["part_sum" if c else "part_off"], 4 * (n + 1))
                last = product(out_ps[c][:, :], blocks, XT, lambda j: y_hi[:, j, :], lambda j: y_lo[:, j, :],
                               lambda j: wo_hi[:, j, :], lambda j: wo_lo[:, j, :])
                if blocks[-1] == XT - 1:
                    last.then_inc(S["out_done"], 1)

            def body(n, first_tile, last_tile):
                pe.wait_ge(S["xlo_done"], (n + 1) * C)
                if not first_tile:
                    pe.wait_ge(S["relu_done"], n * N_HEAD * C)
                by_channel(dt_ps, W_DT, N_HEAD).then_inc(S["dt_done"], 1)
                project(n, 0, first_tile)
                pe.wait_ge(S["dtraw_done"], n + 1)
                apart(pe, S["pe_passed"])
                for c in range(C):
                    last = nc.tensor.transpose(small[:, 256 + c * N_HEAD:256 + (c + 1) * N_HEAD],
                                               dt_raw[:, c * P:(c + 1) * P], ident[0:N_HEAD, 0:N_HEAD])
                last.then_inc(S["dtt_done"], 1)
                if not first_tile:
                    y_turn(n - 1, 0)
                project(n, 1, first_tile)
                z_part(n, 0, first_tile)
                if not first_tile:
                    output(n - 1, 0, range(0, 2))
                pe.wait_ge(S["a_set"], 2 * (n + 1))
                for c in range(C):
                    last = nc.tensor.matmul(small[0:LO + N_HEAD, c * P:(c + 1) * P], a_dup[:, c, :], tri[:, :],
                                            start=True, stop=True)
                last.then_inc(S["cumr_done"], 1)
                if not first_tile:
                    output(n - 1, 0, range(2, 5))
                pe.wait_ge(S["cumrows_done"], n + 1)
                pe.wait_ge(S["cumlo_done"], n + 1)
                apart(pe, S["pe_passed"])
                for c in range(C):
                    last = nc.tensor.transpose(small[:, 288 + c * N_HEAD:288 + (c + 1) * N_HEAD],
                                               cum_rows[:, c * P:(c + 1) * P], ident[0:N_HEAD, 0:N_HEAD])
                last.then_inc(S["cumt_done"], 1)
                project(n, 2, first_tile)
                pe.wait_ge(S["cum_set"], n + 1)
                pe.wait_ge(S["grow_set"], n + 1)
                nc.tensor.matmul(last_ps, ident[:, P - 1:P].to_broadcast([P, P]), cum[:, :, :].rearrange("p c h -> p (c h)"),
                                 start=True, stop=True).then_inc(S["last_done"], 1)
                if not first_tile:
                    y_turn(n - 1, 1)
                    output(n - 1, 0, range(5, XT))
                spread(n, 0)
                project(n, 3, first_tile)
                project(n, 4, first_tile)
                spread(n, 2)
                if not first_tile:
                    pe.wait_ge(S["ylo_done"], 4 * n)
                pe.wait_ge(S["conv_done"], n * NT + 1)
                pair(0, bt)
                pe.wait_ge(S["conv_done"], n * NT + 2)
                for c in range(C):
                    tok = slice(c * P, (c + 1) * P)
                    last = nc.tensor.matmul(pair_ps[1][:, tok], bt[:, tok], ct[:, tok], start=True, stop=True)
                last.then_inc(S["pair_done"], 1)
                if not first_tile:
                    output(n - 1, 1, range(0, 3))
                spread(n, 4)
                x_pair(n, 0)
                project(n, 5, first_tile)
                spread(n, 6)
                if not first_tile:
                    output(n - 1, 1, range(3, 6))
                x_pair(n, 1)
                project(n, 6, first_tile)
                spread(n, 8)
                if not first_tile:
                    output(n - 1, 1, range(6, XT))
                x_pair(n, 2)
                project(n, 7, first_tile)
                spread(n, 10)
                z_part(n, 1, first_tile)
                x_pair(n, 3)
                project(n, 8, first_tile)
                spread(n, 12)
                off(n, 0)
                x_pair(n, 4)
                project(n, 9, first_tile)
                spread(n, 14)
                x_pair(n, 5)
                new_state(n, 0)
                diag(n, 0, first_tile)
                x_pair(n, 6)
                z_part(n, 2, first_tile)
                off(n, 1)
                x_pair(n, 7)
                new_state(n, 1)
                diag(n, 1, first_tile)
                off(n, 2)
                z_part(n, 3, first_tile)
                if not last_tile:
                    turn(n + 1, 0)
                new_state(n, 2)
                diag(n, 2, first_tile)
                off(n, 3)
                if not last_tile:
                    turn(n + 1, 1)
                new_state(n, 3)
                diag(n, 3, first_tile)

            turn(0, 0, first_tile=True)
            turn(0, 1, first_tile=True)
            body(0, True, False)
            with pe.Fori(1, N - 1) as n:
                body(n, False, False)
            body(N - 1, False, True)
            for c in range(C):
                y_turn(N - 1, c)
                output(N - 1, c, range(XT))


def build_program(nc, u, w_in, conv_w, conv_b, dt_bias, a_log, d_skip, norm_w, w_out, w_r, w_k, w_v, mu_r, mu_k, out):
    n_batch, length, _ = u.shape
    n_tok = n_batch * length
    u_rows = u.rearrange("b l d -> (b l) d")
    out_rows = out.rearrange("b l d -> (b l) d")
    gate_rows = nc.dram_tensor("gate_rows", (n_tok, DM), F32, kind="Internal").ap()
    ctx = ExitStack()
    with ctx:
        ident = ctx.enter_context(nc.sbuf_tensor("ident", [P, P], F32))
        ln_scale = ctx.enter_context(nc.sbuf_tensor("ln_scale", [P, n_tok // P], F32))
        ln_shift = ctx.enter_context(nc.sbuf_tensor("ln_shift", [P, n_tok // P], F32))
        ident_step = ctx.enter_context(nc.semaphore("ident_step"))
        with nc.Block() as block:
            @block.gpsimd
            def _(pool):
                pool.memset(ident[:, :], 0.0).then_inc(ident_step, 1)
                pool.wait_ge(ident_step, 1)
                pool.affine_select(out=ident[:, :], in_=ident[:, :], compare_op=ALU.not_equal, fill=1.0, base=0,
                                   pattern=[[-1, P]], channel_multiplier=1).then_inc(ident_step, 1)
                pool.wait_ge(ident_step, 2)
        ffn_phase(nc, u_rows, w_r, w_k, w_v, mu_r, mu_k, gate_rows, ident, ln_scale, ln_shift, n_tok, n_batch)
        ssm_phase(nc, u_rows, w_in, conv_w, conv_b, dt_bias, a_log, d_skip, norm_w, w_out, gate_rows, out_rows,
                  ident, ln_scale, ln_shift, n_tok, n_batch)


INPUTS = ["L0_attn_u", "L0_attn_W_in", "L0_attn_conv_w", "L0_attn_conv_b", "L0_attn_dt_bias", "L0_attn_A_log",
          "L0_attn_D", "L0_attn_norm_w", "L0_attn_W_out", "L0_ffn_W_r", "L0_ffn_W_k", "L0_ffn_W_v", "L0_ffn_mu_r",
          "L0_ffn_mu_k"]


def kernel(**inputs):
    import numpy as np
    import concourse.bacc as bacc
    from concourse.bass_utils import run_bass_kernel_spmd

    nc = bacc.Bacc("TRN2", target_bir_lowering=False, num_devices=1)
    arrays, args = {}, []
    for name in INPUTS:
        a = np.ascontiguousarray(inputs[name])
        arrays[f"in_{name}"] = a
        args.append(nc.dram_tensor(f"in_{name}", a.shape, mybir.dt.from_np(a.dtype), kind="ExternalInput").ap())
    shape = arrays["in_L0_attn_u"].shape
    args.append(nc.dram_tensor("out", shape, F32, kind="ExternalOutput").ap())
    build_program(nc, *args)
    result = run_bass_kernel_spmd(nc, [arrays], core_ids=[0])
    return result.results[0]["out"]
```

```python
import concourse.bass as bass
from concourse import mybir
from contextlib import ExitStack

F32 = mybir.dt.float32
F32R = mybir.dt.float32r
ALU = mybir.AluOpType
ACT = mybir.ActivationFunctionType
P = 128
DM = 512
KD = DM // P
LN_EPS = 1e-5


def apart(eng, passed):
    eng.sem_inc(passed)


def column(ap):
    return ap.rearrange("(k p) -> p k", p=P)


def ffn_phase(nc, u_rows, w_r, w_k, w_v, mu_r, mu_k, gate_rows, x_cols, ident, load_ahead, n_tok, n_batch):
    T = 512
    C = T // P
    N = n_tok // T
    N_PER_BATCH = N // n_batch

    ctx = ExitStack()
    with ctx:
        def sb(name, shape, dt=F32):
            return ctx.enter_context(nc.sbuf_tensor("f_" + name, shape, dt))

        def ps(name):
            return ctx.enter_context(nc.psum_tensor("f_" + name, [P, 512], F32))

        def sem(name):
            return ctx.enter_context(nc.semaphore("f_" + name))

        w_hi = {n: sb(f"w{n}_hi", [P, KD, DM], F32R) for n in "rkv"}
        w_lo = {n: sb(f"w{n}_lo", [P, KD, DM], F32R) for n in "rkv"}
        mu = {"r": sb("mu_r", [P, KD]), "k": sb("mu_k", [P, KD])}
        keep = sb("keep", [P, N])
        keep_now = sb("keep_now", [P, 1])
        minus_half = sb("minus_half", [P, C])
        minus_one = sb("minus_one", [P, C])
        eps = sb("eps", [P, C])

        u = sb("u", [P, C, DM])
        bn = sb("bn", [P, C, 6])
        mv = sb("mv", [P, C, 2])
        ve = sb("ve", [P, C])
        scale = sb("scale", [P, C])
        mean_scaled = sb("mean_scaled", [P, C])
        shift = sb("shift", [P, C])
        xn = sb("xn", [P, C, DM])
        xt = sb("xt", [P, KD, T + 1])
        dt_ = sb("dt", [P, KD, T])
        mixed = sb("mixed", [P, 2 * KD, T])
        x_hi = {n: sb(f"x{n}_hi", [P, KD, T], F32R) for n in "rk"}
        x_lo = {n: sb(f"x{n}_lo", [P, KD, T], F32R) for n in "rk"}
        kr = sb("kr", [P, KD, T])
        ka = kr
        ka_hi = sb("ka_hi", [P, KD, T], F32R)
        ka_lo = sb("ka_lo", [P, KD, T], F32R)
        tr = sb("tr", [P, C, DM])
        f2 = tr
        tg = sb("tg", [P, C, DM])
        g4 = tg

        ps_t = [ps("ps_t0"), ps("ps_t1")]
        ps_k = [ps("ps_k0"), ps("ps_k1")]
        ps_r = [ps("ps_r0"), ps("ps_r1")]
        ps_v = [ps("ps_v0"), ps("ps_v1")]

        w_loaded = {n: sem(f"w{n}_loaded") for n in "rkv"}
        mu_loaded = sem("mu_loaded")
        consts_set = sem("consts_set")
        w_turned = sem("w_turned")
        w_hi_set = sem("w_hi_set")
        w_lo_set = sem("w_lo_set")
        u_loaded = sem("u_loaded")
        bn_done = sem("bn_done")
        mv_done = sem("mv_done")
        pool_step = sem("pool_step")
        ln_done = sem("ln_done")
        xn_done = sem("xn_done")
        turned = sem("turned")
        xt_done = sem("xt_done")
        keep_set = sem("keep_set")
        edge_done = sem("edge_done")
        diff_done = sem("diff_done")
        mixed_done = sem("mixed_done")
        hi_done = sem("hi_done")
        lo_done = sem("lo_done")
        k_done = sem("k_done")
        kr_done = sem("kr_done")
        ka_done = sem("ka_done")
        kahi_done = sem("kahi_done")
        kalo_done = sem("kalo_done")
        r_done = sem("r_done")
        tr_done = sem("tr_done")
        v_done = sem("v_done")
        f2_done = sem("f2_done")
        tg_done = sem("tg_done")
        g4_done = sem("g4_done")
        g_stored = sem("g_stored")
        x_stored = sem("x_stored")
        pool_passed = sem("pool_passed")
        dve_passed = sem("dve_passed")

        w_raw = {"k": kr[:, :, :], "r": tr[:, :, :], "v": tg[:, :, :]}
        W_SRC = {"r": w_r, "k": w_k, "v": w_v}

        def u_tile(n):
            return u_rows[bass.ds(n * T, T), :].rearrange("(c p) d -> p c d", p=P)

        def g_tile(n):
            return gate_rows[bass.ds(n * T, T), :].rearrange("(c p) d -> p c d", p=P)

        def x_tile(n):
            return x_cols.rearrange("(k p) t -> p k t", p=P)[:, :, bass.ds(n * T, T)]

        block = ctx.enter_context(nc.Block())

        @block.sync
        def _(sp):
            sp.dma_start(u[:, :, :], u_tile(0)).then_inc(u_loaded, 16)
            for n in "krv":
                sp.dma_start(w_raw[n], W_SRC[n].rearrange("(o p) c -> p o c", p=P)).then_inc(w_loaded[n], 16)
            sp.dma_start(mu["r"][:, :], column(mu_r), allow_slow_non_contiguous=True).then_inc(mu_loaded, 16)
            sp.dma_start(mu["k"][:, :], column(mu_k), allow_slow_non_contiguous=True).then_inc(mu_loaded, 16)
            sp.wait_ge(xn_done, C)
            sp.dma_start(u[:, :, :], u_tile(1)).then_inc(u_loaded, 16)
            load_ahead(sp)
            sp.wait_ge(xt_done, KD)
            sp.dma_start(x_tile(0), xt[:, :, 1:T + 1]).then_inc(x_stored, 16)
            with sp.Fori(0, N - 2) as n:
                sp.wait_ge(xn_done, (n + 2) * C)
                sp.dma_start(u[:, :, :], u_tile(n + 2)).then_inc(u_loaded, 16)
                sp.wait_ge(xt_done, (n + 2) * KD)
                sp.dma_start(x_tile(n + 1), xt[:, :, 1:T + 1]).then_inc(x_stored, 16)
                sp.wait_ge(g4_done, (n + 1) * C)
                sp.dma_start(g_tile(n), g4[:, :, :]).then_inc(g_stored, 16)
            sp.wait_ge(xt_done, N * KD)
            sp.dma_start(x_tile(N - 1), xt[:, :, 1:T + 1]).then_inc(x_stored, 16)
            sp.wait_ge(g4_done, (N - 1) * C)
            sp.dma_start(g_tile(N - 2), g4[:, :, :]).then_inc(g_stored, 16)
            for c in range(C):
                sp.wait_ge(g4_done, (N - 1) * C + c + 1)
                sp.dma_start(g_tile(N - 1)[:, c, :], g4[:, c, :]).then_inc(g_stored, 16)
            sp.wait_ge(g_stored, 16 * (N - 1 + C))
            sp.wait_ge(x_stored, 16 * N)

        @block.gpsimd
        def _(pool):
            pool.memset(keep[:, :], 1.0).then_inc(pool_step, 1)
            pool.memset(minus_half[:, :], -0.5).then_inc(consts_set, 1)
            pool.memset(minus_one[:, :], -1.0).then_inc(consts_set, 1)
            pool.memset(eps[:, :], LN_EPS).then_inc(consts_set, 1)
            pool.memset(xt[:, :, T:T + 1], 0.0).then_inc(consts_set, 1)
            pool.wait_ge(pool_step, 1)
            for b in range(1, n_batch):
                pool.memset(keep[:, b * N_PER_BATCH:b * N_PER_BATCH + 1], 0.0).then_inc(consts_set, 1)
            pool.wait_ge(consts_set, 3 + n_batch)

            STEPS = 3

            def norm(n, first_tile=False):
                first = 1 + n * STEPS
                pool.wait_ge(mv_done, n + 1)
                nc.gpsimd.tensor_tensor(ve[:, :], mv[:, :, 1], eps[:, :], ALU.add).then_inc(pool_step, 1)
                pool.wait_ge(pool_step, first + 1)
                if not first_tile:
                    pool.wait_ge(xn_done, n * C)
                nc.gpsimd.tensor_tensor(scale[:, :], ve[:, :], minus_half[:, :], ALU.pow).then_inc(pool_step, 1)
                pool.wait_ge(pool_step, first + 2)
                nc.gpsimd.tensor_tensor(mean_scaled[:, :], mv[:, :, 0], scale[:, :], ALU.mult).then_inc(pool_step, 1)
                pool.wait_ge(pool_step, first + 3)
                nc.gpsimd.tensor_tensor(shift[:, :], mean_scaled[:, :], minus_one[:, :], ALU.mult)\
                    .then_inc(ln_done, 1)

            def edge_and_diff(n, first_tile=False):
                if not first_tile:
                    pool.wait_ge(edge_done, n)
                    pool.wait_ge(mixed_done, n * 2 * KD)
                    apart(pool, pool_passed)
                nc.gpsimd.tensor_copy(keep_now[:, :], keep[:, bass.ds(n, 1)]).then_inc(keep_set, 1)
                pool.wait_ge(keep_set, n + 1)
                nc.gpsimd.tensor_tensor(xt[:, :, 0:1], xt[:, :, T:T + 1],
                                        keep_now[:, :].unsqueeze(1).to_broadcast([P, KD, 1]), ALU.mult)\
                    .then_inc(edge_done, 1)
                pool.wait_ge(edge_done, n + 1)
                for k in range(KD):
                    pool.wait_ge(xt_done, n * KD + k + 1)
                    nc.gpsimd.tensor_tensor(dt_[:, k, :], xt[:, k, 1:T + 1], xt[:, k, 0:T], ALU.subtract)\
                        .then_inc(diff_done, 1)

            norm(0, first_tile=True)
            edge_and_diff(0, first_tile=True)
            with pool.Fori(0, N - 1) as n:
                norm(n + 1)
                edge_and_diff(n + 1)

        @block.scalar
        def _(act):
            def weight_high(w):
                for k in range(KD):
                    act.wait_ge(w_turned, "krv".index(w) * KD + k + 1)
                    nc.scalar.activation(w_hi[w][:, k, :], ps_t[k % 2][:, :], ACT.Copy).then_inc(w_hi_set, 1)

            def normalise(n, c, first_tile=False):
                if c == 0:
                    act.wait_ge(ln_done, n + 1)
                    act.wait_ge(u_loaded, 16 * (n + 1))
                    if not first_tile:
                        act.wait_ge(turned, n * KD)
                nc.scalar.activation(xn[:, c, :], u[:, c, :], ACT.Identity, bias=shift[:, c:c + 1],
                                     scale=scale[:, c:c + 1]).then_inc(xn_done, 1)

            def columns(n, first_tile=False):
                act.wait_ge(edge_done, n + 1)
                if not first_tile:
                    act.wait_ge(x_stored, 16 * n)
                for k in range(KD):
                    act.wait_ge(turned, n * KD + k + 1)
                    nc.scalar.activation(xt[:, k, 1:T + 1], ps_t[k % 2][:, :], ACT.Copy).then_inc(xt_done, 1)

            def high(n, w, first_tile=False):
                base = KD * "kr".index(w)
                if not first_tile:
                    act.wait_ge(k_done if w == "k" else r_done, n * KD)
                for k in range(KD):
                    act.wait_ge(mixed_done, n * 2 * KD + base + k + 1)
                    nc.scalar.activation(x_hi[w][:, k, :], mixed[:, base + k, :], ACT.Copy).then_inc(hi_done, 1)

            def tanh_gate(n, c):
                act.wait_ge(f2_done, n * C + c + 1)
                nc.scalar.activation(tg[:, c, :], f2[:, c, :], ACT.Tanh, scale=0.25).then_inc(tg_done, 1)

            def body(n, first_tile, last_tile):
                for m in range(KD + 1):
                    if m < KD:
                        act.wait_ge(k_done, n * KD + m + 1)
                        if not first_tile and m == 0:
                            act.wait_ge(kalo_done, n * KD)
                        nc.scalar.activation(kr[:, m, :], ps_k[m % 2][:, :], ACT.Relu).then_inc(kr_done, 1)
                        if not first_tile and m < 2:
                            tanh_gate(n - 1, 2 + m)
                    if m >= 1:
                        act.wait_ge(ka_done, n * KD + m)
                        if not first_tile and m == 1:
                            act.wait_ge(v_done, n * C)
                        nc.scalar.activation(ka_hi[:, m - 1, :], ka[:, m - 1, :], ACT.Copy).then_inc(kahi_done, 1)
                for c in range(C):
                    if not last_tile:
                        normalise(n + 1, c)
                    act.wait_ge(r_done, n * C + c + 1)
                    if not first_tile and c == 0:
                        act.wait_ge(g4_done, n * C)
                    nc.scalar.activation(tr[:, c, :], ps_r[c % 2][:, :], ACT.Tanh, scale=0.5).then_inc(tr_done, 1)
                if not last_tile:
                    columns(n + 1)
                    high(n + 1, "k")
                if not first_tile:
                    act.wait_ge(g_stored, 16 * n)
                tanh_gate(n, 0)
                tanh_gate(n, 1)
                if not last_tile:
                    high(n + 1, "r")
                else:
                    tanh_gate(n, 2)
                    tanh_gate(n, 3)

            for c in range(C):
                normalise(0, c, first_tile=True)
            columns(0, first_tile=True)
            weight_high("k")
            high(0, "k", first_tile=True)
            weight_high("r")
            weight_high("v")
            high(0, "r", first_tile=True)
            body(0, True, False)
            with act.Fori(1, N - 1) as n:
                body(n, False, False)
            body(N - 1, False, True)

        @block.vector
        def _(dve):
            def weight_low(w):
                for k in range(KD):
                    dve.wait_ge(w_hi_set, "krv".index(w) * KD + k + 1)
                    nc.vector.tensor_tensor(w_lo[w][:, k, :], ps_t[k % 2][:, :], w_hi[w][:, k, :].bitcast(F32),
                                            ALU.subtract).then_inc(w_lo_set, 1)

            def statistics(n, first_tile=False):
                dve.wait_ge(u_loaded, 16 * (n + 1))
                for c in range(C):
                    nc.vector.bn_stats(bn[:, c, :], u[:, c, :]).then_inc(bn_done, 1)
                dve.wait_ge(bn_done, (n + 1) * C)
                if not first_tile:
                    dve.wait_ge(ln_done, n)
                    apart(dve, dve_passed)
                for c in range(C):
                    last = nc.vector.bn_aggr(mv[:, c, :], bn[:, c, :])
                last.then_inc(mv_done, 1)

            def mix(n, w, first_tile=False, between={}):
                base = KD * "kr".index(w)

                def low(k):
                    dve.wait_ge(hi_done, n * 2 * KD + base + k + 1)
                    nc.vector.tensor_tensor(x_lo[w][:, k, :], mixed[:, base + k, :],
                                            x_hi[w][:, k, :].bitcast(F32), ALU.subtract).then_inc(lo_done, 1)

                if not first_tile:
                    dve.wait_ge(lo_done, n * 2 * KD - KD + base)
                    dve.wait_ge(k_done if w == "k" else r_done, n * KD)
                for k in range(KD):
                    dve.wait_ge(diff_done, n * KD + k + 1)
                    nc.vector.scalar_tensor_tensor(mixed[:, base + k, :], dt_[:, k, :], mu[w][:, k:k + 1],
                                                   xt[:, k, 0:T], ALU.mult, ALU.add).then_inc(mixed_done, 1)
                    if k >= 1:
                        low(k - 1)
                    if k in between:
                        between[k]()
                low(KD - 1)

            def squares(n, first_tile):
                def low(m):
                    dve.wait_ge(kahi_done, n * KD + m + 1)
                    nc.vector.tensor_tensor(ka_lo[:, m, :], ka[:, m, :], ka_hi[:, m, :].bitcast(F32),
                                            ALU.subtract).then_inc(kalo_done, 1)
                if not first_tile:
                    dve.wait_ge(kalo_done, n * KD)
                    dve.wait_ge(v_done, n * C)
                for m in range(KD):
                    dve.wait_ge(kr_done, n * KD + m + 1)
                    nc.vector.tensor_tensor(ka[:, m, :], kr[:, m, :], kr[:, m, :], ALU.mult).then_inc(ka_done, 1)
                    if m >= 1:
                        low(m - 1)
                low(KD - 1)

            def gated(n, c):
                dve.wait_ge(v_done, n * C + c + 1)
                dve.wait_ge(tr_done, n * C + c + 1)
                nc.vector.scalar_tensor_tensor(f2[:, c, :], tr[:, c, :], 1.0, ps_v[c % 2][:, :], ALU.add,
                                               ALU.mult).then_inc(f2_done, 1)

            def silu_gate(n, c):
                dve.wait_ge(tg_done, n * C + c + 1)
                nc.vector.scalar_tensor_tensor(g4[:, c, :], tg[:, c, :], 1.0, f2[:, c, :], ALU.add,
                                               ALU.mult).then_inc(g4_done, 1)

            def body(n, first_tile, last_tile):
                if not last_tile:
                    statistics(n + 1)
                if not first_tile:
                    silu_gate(n - 1, 2)
                    silu_gate(n - 1, 3)
                squares(n, first_tile)
                if not last_tile:
                    mix(n + 1, "k", between={2: lambda: gated(n, 0)})
                else:
                    gated(n, 0)
                gated(n, 1)
                silu_gate(n, 0)
                silu_gate(n, 1)
                if not last_tile:
                    mix(n + 1, "r", between={1: lambda: gated(n, 2)})
                else:
                    gated(n, 2)
                gated(n, 3)
                if last_tile:
                    silu_gate(n, 2)
                    silu_gate(n, 3)

            statistics(0, first_tile=True)
            weight_low("k")
            dve.wait_ge(mu_loaded, 32)
            mix(0, "k", first_tile=True)
            weight_low("r")
            weight_low("v")
            mix(0, "r", first_tile=True)
            body(0, True, False)
            with dve.Fori(1, N - 1) as n:
                body(n, False, False)
            body(N - 1, False, True)

        @block.tensor
        def _(pe):
            def turn_weight(w):
                pe.wait_ge(w_loaded[w], 16)
                for k in range(KD):
                    q = "krv".index(w) * KD + k
                    if q < 2:
                        pe.wait_ge(xt_done, KD - 1 + q)
                    else:
                        pe.wait_ge(w_lo_set, q - 1)
                    for o in range(KD):
                        last = nc.tensor.transpose(ps_t[k % 2][:, o * P:(o + 1) * P],
                                                   w_raw[w][:, o, k * P:(k + 1) * P], ident[:, :])
                    last.then_inc(w_turned, 1)

            def turn(n, first_tile=False):
                pe.wait_ge(xn_done, (n + 1) * C)
                for k in range(KD):
                    if not (first_tile and k < 2):
                        pe.wait_ge(xt_done, n * KD + k - 1)
                    for c in range(C):
                        last = nc.tensor.transpose(ps_t[k % 2][:, c * P:(c + 1) * P], xn[:, c, k * P:(k + 1) * P],
                                                   ident[:, :])
                    last.then_inc(turned, 1)

            def product(out, lhs_hi, lhs_lo, rhs_hi, rhs_lo):
                pairs = [(lhs_hi, rhs_hi), (lhs_hi, rhs_lo), (lhs_lo, rhs_hi)]
                for k in range(KD):
                    for j, (a, b) in enumerate(pairs):
                        last = nc.tensor.matmul(out, a(k), b(k), start=(k == 0 and j == 0),
                                                stop=(k == KD - 1 and j == 2))
                return last

            def body(n, first_tile, last_tile):
                pe.wait_ge(lo_done, n * 2 * KD + KD)
                for m in range(KD):
                    if not (first_tile and m < 2):
                        pe.wait_ge(kr_done, n * KD + m - 1)
                    product(ps_k[m % 2][:, :],
                            lambda k: w_hi["k"][:, k, m * P:(m + 1) * P], lambda k: w_lo["k"][:, k, m * P:(m + 1) * P],
                            lambda k: x_hi["k"][:, k, :], lambda k: x_lo["k"][:, k, :]).then_inc(k_done, 1)
                pe.wait_ge(lo_done, (n + 1) * 2 * KD)
                for c in range(C):
                    if not (first_tile and c < 2):
                        pe.wait_ge(tr_done, n * C + c - 1)
                    product(ps_r[c % 2][:, :],
                            lambda k: x_hi["r"][:, k, c * P:(c + 1) * P], lambda k: x_lo["r"][:, k, c * P:(c + 1) * P],
                            lambda k: w_hi["r"][:, k, :], lambda k: w_lo["r"][:, k, :]).then_inc(r_done, 1)
                if not last_tile:
                    turn(n + 1)
                pe.wait_ge(kalo_done, (n + 1) * KD)
                for c in range(C):
                    if not (first_tile and c < 2):
                        pe.wait_ge(f2_done, n * C + c - 1)
                    product(ps_v[c % 2][:, :],
                            lambda k: ka_hi[:, k, c * P:(c + 1) * P], lambda k: ka_lo[:, k, c * P:(c + 1) * P],
                            lambda k: w_hi["v"][:, k, :], lambda k: w_lo["v"][:, k, :]).then_inc(v_done, 1)

            turn(0, first_tile=True)
            for w in "krv":
                turn_weight(w)
            pe.wait_ge(w_lo_set, 3 * KD)
            body(0, True, False)
            with pe.Fori(1, N - 1) as n:
                body(n, False, False)
            body(N - 1, False, True)


D_INNER, D_STATE, N_HEAD, HEAD, N_TAP = 1024, 128, 16, 64, 4
RMS_EPS = 1e-5
W_X = D_INNER
W_DT = 2 * D_INNER + 2 * D_STATE
W_ALL = W_DT + N_HEAD


class Ahead:

    N_SMALL = 7

    def __init__(self, nc, ctx):
        def sb(name, shape):
            return ctx.enter_context(nc.sbuf_tensor("ahead_" + name, shape, F32))

        n_tile = D_INNER // P + 2
        self.w_in_raw = sb("w_in_raw", [P, KD, W_ALL])
        self.taps = sb("taps", [P, n_tile, N_TAP])
        self.tap_bias = sb("tap_bias", [P, n_tile])
        self.norm_cols = sb("norm_cols", [P, D_INNER // P])
        self.dtb = sb("dtb", [2 * N_HEAD, 1])
        self.head_rows = sb("head_rows", [1, 2 * N_HEAD])
        self.w_in_loaded = ctx.enter_context(nc.semaphore("ahead_w_in_loaded"))
        self.params_loaded = ctx.enter_context(nc.semaphore("ahead_params_loaded"))

    def load(self, sync, w_in, conv_w, conv_b, dt_bias, a_log, d_skip, norm_w):
        for k in range(KD):
            sync.dma_start(self.w_in_raw[:, k, :], w_in[k * P:(k + 1) * P, :]).then_inc(self.w_in_loaded, 16)
        slow = dict(allow_slow_non_contiguous=True)
        small = [(self.taps[:, :, :], conv_w.rearrange("(j p) t -> p j t", p=P), {}),
                 (self.tap_bias[:, :], column(conv_b), slow),
                 (self.norm_cols[:, :], column(norm_w), slow),
                 (self.dtb[0:N_HEAD, :], dt_bias.rearrange("(h a) -> h a", a=1), {}),
                 (self.dtb[N_HEAD:, :], dt_bias.rearrange("(h a) -> h a", a=1), {}),
                 (self.head_rows[:, 0:N_HEAD], a_log.rearrange("(a h) -> a h", a=1), {}),
                 (self.head_rows[:, N_HEAD:], d_skip.rearrange("(a h) -> a h", a=1), {})]
        for to, source, options in small:
            sync.dma_start(to, source, **options).then_inc(self.params_loaded, 16)


def ssm_phase(nc, u_rows, x_cols, ahead, w_out, gate_rows, out_rows, ident, n_tok, n_batch):
    C = 2
    T = C * P
    N = n_tok // T
    N_PER_BATCH = N // n_batch
    XT = D_INNER // P
    NT = XT + 2
    B_TILE, C_TILE = XT, XT + 1
    ORDER = [B_TILE, C_TILE] + list(range(XT))
    HALF = N_HEAD // 2
    LO = 32

    ctx = ExitStack()
    with ctx:
        def sb(name, shape, dt=F32):
            return ctx.enter_context(nc.sbuf_tensor("s_" + name, shape, dt))

        def ps(name):
            return ctx.enter_context(nc.psum_tensor("s_" + name, [P, 512], F32))

        def sem(name):
            return ctx.enter_context(nc.semaphore("s_" + name))

        w_hi = sb("w_hi", [P, KD, W_DT], F32R)
        w_lo = sb("w_lo", [P, KD, W_DT], F32R)
        w_dt = sb("w_dt", [P, KD, 2 * N_HEAD], F32R)
        wo_hi = sb("wo_hi", [P, XT, DM], F32R)
        wo_lo = sb("wo_lo", [P, XT, DM], F32R)
        tri = sb("tri", [P, P])
        pick = sb("pick", [LO + N_HEAD, N_HEAD], F32R)
        both = sb("both", [2 * N_HEAD, N_HEAD])
        ones_row = sb("ones_row", [1, P])
        w_in_raw, taps, tap_bias, norm_cols = ahead.w_in_raw, ahead.taps, ahead.tap_bias, ahead.norm_cols
        dtb, head_rows = ahead.dtb, ahead.head_rows
        head_params = sb("head_params", [P, 2 * N_HEAD])
        keep = sb("keep", [P, N])
        keep_now = sb("keep_now", [P, 1])
        minus_half = sb("minus_half", [P, 1])
        ones = sb("ones", [P, 1])

        x = sb("x", [P, KD, T])
        residual = sb("residual", [P, C, DM])
        gate = sb("gate", [P, C, DM])
        x_hi = sb("x_hi", [P, KD, T], F32R)
        x_lo = sb("x_lo", [P, KD, T], F32R)
        raw = sb("raw", [P, 2, T + N_TAP - 1])
        edges = sb("edges", [P, NT, N_TAP - 1])
        place = w_in_raw[:, :, :].rearrange("p k n -> p (k n)")
        sizes = [N_HEAD * C * P, C * D_INNER, C * D_INNER, 2 * T, 2 * T]
        starts = [sum(sizes[:i]) for i in range(len(sizes))]
        places = [place[:, a:a + b] for a, b in zip(starts, sizes)]
        lm = places[0].rearrange("p (h c l) -> p h c l", h=N_HEAD, c=C)
        xd = places[1].rearrange("p (c d) -> p c d", c=C)
        xdd = places[2].rearrange("p (c d) -> p c d", c=C)
        acc = places[3].rearrange("p (b t) -> p b t", b=2)
        act_x = places[4].rearrange("p (b t) -> p b t", b=2)
        bt = sb("bt", [P, T])
        ct = sb("ct", [P, T])
        b_tok = sb("b_tok", [P, C, D_STATE])
        x_tok = sb("x_tok", [P, C, D_INNER])
        sp = sb("sp", [P, 6, C * N_HEAD])
        dtv = sb("dtv", [P, C, N_HEAD])
        a_dup = sb("a_dup", [P, C, LO + N_HEAD])
        cum_rows = sb("cum_rows", [2 * N_HEAD, T])
        dt_raw = cum_rows
        cum_parts = sb("cum_parts", [LO + N_HEAD, T], F32R)
        cum = sb("cum", [P, C, N_HEAD])
        grow = sb("grow", [P, C, N_HEAD])
        chunk_decay = sb("chunk_decay", [P, C, N_HEAD])
        tail = sb("tail", [P, C, N_HEAD])
        tail_decay = sb("tail_decay", [P, C, N_HEAD])
        gm = sb("gm", [P, C, P])
        gz = sb("gz", [P, C, D_INNER])
        part = sb("part", [P, 2, 512])
        state = sb("state", [P, D_INNER])
        ssq = sb("ssq", [P, C])
        rms = sb("rms", [P, C, 2])
        y_hi = sb("y_hi", [P, XT, P], F32R)
        y_lo = sb("y_lo", [P, XT, P], F32R)

        turn_ps = [ps("turn0"), ps("turn1")]
        proj_ps = [ps("proj0"), ps("proj1")]
        cum_ps = ps("cum_ps")
        off_ps = ps("off_ps")
        diag_ps = ps("diag_ps")
        state_ps = ps("state_ps")
        small = cum_ps
        dt_ps = small[0:2 * N_HEAD, 0:T]
        dtt_ps = small[:, 256:288]
        cumr_ps = small[0:LO + N_HEAD, 0:T]
        cumt_ps = small[:, 288:320]
        last_ps = small[:, 320:352]
        pair_ps = [turn_ps[0][:, 0:T], turn_ps[1][:, 0:T]]
        z_ps = [state_ps, off_ps, proj_ps[0], proj_ps[1]]
        out_ps = [off_ps, diag_ps]
        CH = [(0, 0), (1, 0), (0, 1), (1, 1)]

        names = """grow_kept chunk_kept keep_set w_hi_set w_lo_set wo_hi_set taps_halved wo_lo_set wo_loaded consts pool_step head_ps heads_exp heads_set
            x_loaded rest_loaded out_stored xhi_done xlo_done
            dt_done dtraw_done dtt_done sp_act sp_step dt_set a_set cumr_done cumrows_done cumhi_done cumlo_done
            cumt_done cum_set grow_set last_done chunk_set tail_set taild_set
            proj_done edge_in raw_done edge_out acc_done tap_done tanh_done conv_done
            pair_done pair_copied xd_done xdd_done skip_done gm_done
            cumb_done relu_done exp_done lm_done z_done tz_done gz_done
            off_done st_done diag_done decayed state_set part_off part_sum sum_done y_done sq_done rms_step
            y_turned yhi_done ylo_done out_done o_mult o_done
            pool_passed pe_passed""".split()
        S = {n: sem(n) for n in names}

        def rows(t, n):
            return t[bass.ds(n * T, T), :].rearrange("(c p) d -> p c d", p=P)

        def x_tile(n):
            return x_cols.rearrange("(k p) t -> p k t", p=P)[:, :, bass.ds(n * T, T)]

        def heads(ap):
            return ap.unsqueeze(-1).to_broadcast([P, ap.shape[-1], HEAD])

        wo_raw = [t[:, :, :].rearrange("p c d -> p (c d)").rearrange("p (j d) -> p j d", d=DM) for t in (x_tok, gz)]

        block = ctx.enter_context(nc.Block())

        @block.sync
        def _(sp_):
            sp_.dma_start(x[:, :, :], x_tile(0)).then_inc(S["x_loaded"], 16)
            wov = w_out.rearrange("(j p) d -> p j d", p=P)
            for i in range(2):
                sp_.dma_start(wo_raw[i], wov[:, i * XT // 2:(i + 1) * XT // 2, :]).then_inc(S["wo_loaded"], 16)

            def body(n, first_tile, last_tile):
                if not last_tile:
                    sp_.wait_ge(S["xlo_done"], (n + 1) * C)
                    sp_.dma_start(x[:, :, :], x_tile(n + 1)).then_inc(S["x_loaded"], 16)
                if not first_tile:
                    sp_.wait_ge(S["o_done"], C * n)
                    sp_.dma_start(rows(out_rows, n - 1), gate[:, :, :]).then_inc(S["out_stored"], 16)
                    sp_.wait_ge(S["out_stored"], 16 * n)
                sp_.dma_start(gate[:, :, :], rows(gate_rows, n)).then_inc(S["rest_loaded"], 16)
                sp_.dma_start(residual[:, :, :], rows(u_rows, n)).then_inc(S["rest_loaded"], 16)

            body(0, True, False)
            with sp_.Fori(1, N - 1) as n:
                body(n, False, False)
            body(N - 1, False, True)
            for c in range(C):
                sp_.wait_ge(S["o_done"], C * (N - 1) + c + 1)
                sp_.dma_start(rows(out_rows, N - 1)[:, c, :], gate[:, c, :]).then_inc(S["out_stored"], 16)
            sp_.wait_ge(S["out_stored"], 16 * (N - 1 + C))

        @block.gpsimd
        def _(pool):
            pool.memset(tri[:, :], 1.0).then_inc(S["pool_step"], 1)
            pool.memset(part[0:LO + N_HEAD, 0, 0:N_HEAD], 0.0).then_inc(S["pool_step"], 1)
            pool.memset(keep[:, :], 1.0).then_inc(S["pool_step"], 1)
            pool.memset(both[:, :], 0.0).then_inc(S["pool_step"], 1)
            pool.memset(ones_row[:, :], 1.0).then_inc(S["consts"], 1)
            pool.memset(minus_half[:, :], -0.5).then_inc(S["consts"], 1)
            pool.memset(ones[:, :], 1.0).then_inc(S["consts"], 1)
            pool.memset(a_dup[:, :, :], 0.0).then_inc(S["consts"], 1)
            pool.memset(state[:, :], 0.0).then_inc(S["consts"], 1)
            pool.memset(edges[:, :, :], 0.0).then_inc(S["consts"], 1)
            pool.wait_ge(S["pool_step"], 4)
            pool.affine_select(out=tri[:, :], in_=tri[:, :], compare_op=ALU.is_ge, fill=0.0, base=0,
                               pattern=[[1, P]], channel_multiplier=-1).then_inc(S["consts"], 1)
            select = part[0:LO + N_HEAD, 0, 0:N_HEAD]
            for i, start in enumerate((0, LO)):
                pool.affine_select(out=select, in_=select, compare_op=ALU.not_equal, fill=1.0, base=-start,
                                   pattern=[[-1, N_HEAD]], channel_multiplier=1).then_inc(S["pool_step"], 1)
                pool.wait_ge(S["pool_step"], 5 + i)
            nc.gpsimd.tensor_copy(pick[:, :], select).then_inc(S["consts"], 1)
            for i, start in enumerate((0, N_HEAD)):
                pool.affine_select(out=both[:, :], in_=both[:, :], compare_op=ALU.not_equal, fill=1.0, base=-start,
                                   pattern=[[-1, N_HEAD]], channel_multiplier=1).then_inc(S["pool_step"], 1)
                pool.wait_ge(S["pool_step"], 7 + i)
            for b in range(1, n_batch):
                pool.memset(keep[:, b * N_PER_BATCH:b * N_PER_BATCH + 1], 0.0).then_inc(S["consts"], 1)
            pool.wait_ge(S["consts"], 7 + n_batch)

            def edge_before(n, q, first_tile):
                j = ORDER[q]
                if q >= 2:
                    pool.wait_ge(S["tap_done"], (n * NT + q - 1) * 3)
                    pool.wait_ge(S["edge_out"], n * NT + q - 1)
                elif not first_tile:
                    pool.wait_ge(S["tap_done"], n * NT * 3)
                    pool.wait_ge(S["edge_out"], n * NT)
                nc.gpsimd.tensor_tensor(raw[:, q % 2, 0:N_TAP - 1], edges[:, j, :],
                                        keep_now[:, :].to_broadcast([P, N_TAP - 1]), ALU.mult)\
                    .then_inc(S["edge_in"], 1)

            def edge_after(n, q):
                pool.wait_ge(S["raw_done"], n * NT + q + 1)
                pool.wait_ge(S["edge_in"], n * NT + q + 1)
                nc.gpsimd.tensor_tensor(edges[:, ORDER[q], :], raw[:, q % 2, T:T + N_TAP - 1],
                                        ones[:, :].to_broadcast([P, N_TAP - 1]), ALU.mult)\
                    .then_inc(S["edge_out"], 1)

            def to_end(n, j, first_tile):
                cols = slice(j * P, (j + 1) * P)
                pool.wait_ge(S["xd_done"], n * XT + j + 1)
                if j == 0:
                    pool.wait_ge(S["taild_set"], n + 1)
                    if not first_tile:
                        pool.wait_ge(S["st_done"], 4 * n)
                for c in range(C):
                    nc.gpsimd.tensor_tensor(xdd[:, c, cols].rearrange("p (h d) -> p h d", d=HEAD),
                                            xd[:, c, cols].rearrange("p (h d) -> p h d", d=HEAD),
                                            heads(tail_decay[:, c, 2 * j:2 * j + 2]), ALU.mult)\
                        .then_inc(S["xdd_done"], 1)

            def skip(n, j):
                pool.wait_ge(S["xd_done"], n * XT + j + 1)
                for c in range(C):
                    v = x_tok[:, c, j * P:(j + 1) * P].rearrange("p (h d) -> p h d", d=HEAD)
                    nc.gpsimd.tensor_tensor(v, v, heads(head_params[:, N_HEAD + 2 * j:N_HEAD + 2 * j + 2]),
                                            ALU.mult).then_inc(S["skip_done"], 1)

            def keep_decays(n):
                pool.wait_ge(S["keep_set"], n + 1)
                pool.wait_ge(S["grow_set"], n + 1)
                k = keep_now[:, :].to_broadcast([P, N_HEAD])
                nc.gpsimd.tensor_tensor(grow[:, 0, :], grow[:, 0, :], k, ALU.mult).then_inc(S["grow_kept"], 1)
                pool.wait_ge(S["chunk_set"], n + 1)
                nc.gpsimd.tensor_tensor(chunk_decay[:, 0, :], chunk_decay[:, 0, :], k, ALU.mult)\
                    .then_inc(S["chunk_kept"], 1)

            def decay_state(n, i):
                c, h = CH[i]
                pool.wait_ge(S["off_done"], n * 4 + i + 1)
                if c:
                    pool.wait_ge(S["state_set"], n * 4 + i)
                else:
                    pool.wait_ge(S["chunk_kept"], n + 1)
                v = state[:, h * 512:(h + 1) * 512].rearrange("p (h d) -> p h d", d=HEAD)
                nc.gpsimd.tensor_tensor(v, v, heads(chunk_decay[:, c, h * HALF:(h + 1) * HALF]), ALU.mult)\
                    .then_inc(S["decayed"], 1)

            def add_skip(n, i):
                c, h = CH[i]
                cols = slice(h * 512, (h + 1) * 512)
                pool.wait_ge(S["skip_done"], n * XT * C + (h + 1) * XT)
                pool.wait_ge(S["part_sum"], n * 4 + i + 1)
                nc.gpsimd.tensor_tensor(x_tok[:, c, cols], x_tok[:, c, cols], part[:, i % 2, :], ALU.add)\
                    .then_inc(S["sum_done"], 1)

            def gate_y(n, i):
                c, h = CH[i]
                cols = slice(h * 512, (h + 1) * 512)
                pool.wait_ge(S["sum_done"], n * 4 + i + 1)
                pool.wait_ge(S["gz_done"], n * 4 + i + 1)
                nc.gpsimd.tensor_tensor(x_tok[:, c, cols], x_tok[:, c, cols], gz[:, c, cols], ALU.mult)\
                    .then_inc(S["y_done"], 1)

            def add_and_gate(n, i):
                add_skip(n, i)
                gate_y(n, i)

            def rms_factor(n, c):
                pool.wait_ge(S["sq_done"], n * C + c + 1)
                apart(pool, S["pool_passed"])
                nc.gpsimd.tensor_scalar(rms[:, c, 0:1], ssq[:, c:c + 1], 64.0 / (4 * D_INNER), 64 * RMS_EPS,
                                        ALU.mult, ALU.add).then_inc(S["rms_step"], 1)
                pool.wait_ge(S["rms_step"], n * 4 + c * 2 + 1)
                nc.gpsimd.tensor_tensor(rms[:, c, 1:2], rms[:, c, 0:1], minus_half[:, :], ALU.pow)\
                    .then_inc(S["rms_step"], 1)

            def add_residual(n, c):
                pool.wait_ge(S["o_mult"], n * C + c + 1)
                nc.gpsimd.tensor_tensor(gate[:, c, :], gate[:, c, :], residual[:, c, :], ALU.add)\
                    .then_inc(S["o_done"], 1)

            def body(n, first_tile, last_tile):
                if not first_tile:
                    pool.wait_ge(S["edge_in"], n * NT)
                    pool.wait_ge(S["chunk_kept"], n)
                    apart(pool, S["pool_passed"])
                nc.gpsimd.tensor_copy(keep_now[:, :], keep[:, bass.ds(n, 1)]).then_inc(S["keep_set"], 1)
                pool.wait_ge(S["keep_set"], n + 1)

                def edge(q):
                    if q < NT:
                        edge_before(n, q, first_tile)

                edge(0)
                edge(1)
                if not first_tile:
                    add_and_gate(n - 1, 3)
                edge_after(n, 0)
                edge(2)
                if not first_tile:
                    rms_factor(n - 1, 0)
                edge_after(n, 1)
                edge(3)
                if not first_tile:
                    rms_factor(n - 1, 1)
                keep_decays(n)
                edge_after(n, 2)
                edge(4)
                if not first_tile:
                    add_residual(n - 1, 0)
                edge_after(n, 3)
                edge(5)
                edge_after(n, 4)
                edge(6)
                for q in range(5, 10):
                    edge_after(n, q)
                    edge(q + 2)
                    to_end(n, q - 5, first_tile)
                    if q == 8:
                        decay_state(n, 0)
                    if q < 9:
                        skip(n, q - 5)
                    if q == 7 and not first_tile:
                        add_residual(n - 1, 1)
                to_end(n, 5, first_tile)
                decay_state(n, 1)
                to_end(n, 6, first_tile)
                to_end(n, 7, first_tile)
                add_skip(n, 0)
                decay_state(n, 2)
                gate_y(n, 0)
                skip(n, 4)
                skip(n, 5)
                add_and_gate(n, 1)
                skip(n, 6)
                skip(n, 7)
                add_and_gate(n, 2)
                decay_state(n, 3)

            body(0, True, False)
            with pool.Fori(1, N - 1) as n:
                body(n, False, False)
            body(N - 1, False, True)
            add_and_gate(N - 1, 3)
            for c in range(C):
                rms_factor(N - 1, c)
                add_residual(N - 1, c)

        @block.scalar
        def _(act):
            def weight_high(k):
                nc.scalar.activation(w_hi[:, k, :], w_in_raw[:, k, 0:W_DT], ACT.Copy).then_inc(S["w_hi_set"], 1)

            def head_values():
                act.wait_ge(S["head_ps"], 1)
                nc.scalar.activation(head_params[:, 0:N_HEAD], cum_ps[:, 0:N_HEAD], ACT.Exp)\
                    .then_inc(S["heads_exp"], 1)
                nc.scalar.activation(head_params[:, N_HEAD:], cum_ps[:, N_HEAD:2 * N_HEAD], ACT.Copy)\
                    .then_inc(S["heads_set"], 1)

            def high(n, c, first_tile=False):
                if c == 0:
                    act.wait_ge(S["x_loaded"], 16 * (n + 1))
                    if not first_tile:
                        act.wait_ge(S["z_done"], 4 * n)
                v = slice(c * P, (c + 1) * P)
                nc.scalar.activation(x_hi[:, :, v], x[:, :, v], ACT.Copy).then_inc(S["xhi_done"], 1)

            def conv_in(n, q, first_tile):
                j = ORDER[q]
                act.wait_ge(S["proj_done"], n * NT + q + 1)
                act.wait_ge(S["edge_in"], n * NT + q + 1)
                nc.scalar.activation(raw[:, q % 2, N_TAP - 1:], proj_ps[q % 2][:, 0:T], ACT.Copy)\
                    .then_inc(S["raw_done"], 1)
                if q >= 2 or not first_tile:
                    act.wait_ge(S["conv_done"], n * NT + max(q - 1, 0))
                nc.scalar.activation(acc[:, q % 2, :], proj_ps[q % 2][:, 0:T], ACT.Identity,
                                     bias=tap_bias[:, j:j + 1], scale=taps[:, j, N_TAP - 1:N_TAP])\
                    .then_inc(S["acc_done"], 1)

            def conv_tanh(n, q, first_tile):
                act.wait_ge(S["tap_done"], (n * NT + q + 1) * 3)
                if q >= 4:
                    act.wait_ge(S["pair_done"], n * (XT + 2) + q - 1)
                elif q >= 2:
                    act.wait_ge(S["conv_done"], n * NT + q - 1)
                elif not first_tile:
                    act.wait_ge(S["pair_done"], n * (XT + 2))
                nc.scalar.activation(act_x[:, q % 2, :], acc[:, q % 2, :], ACT.Tanh).then_inc(S["tanh_done"], 1)

            def x_copy(n, j, first_tile):
                act.wait_ge(S["pair_done"], n * (XT + 2) + j + 3)
                if j == 0 and not first_tile:
                    act.wait_ge(S["y_turned"], 4 * n)
                    act.wait_ge(S["sq_done"], C * n)
                nc.scalar.activation(x_tok[:, :, j * P:(j + 1) * P],
                                     pair_ps[j % 2].rearrange("p (c d) -> p c d", d=P), ACT.Copy)\
                    .then_inc(S["pair_copied"], 1)

            def decay_heads(n, first, first_tile):
                for h in (first, first + 1):
                    act.wait_ge(S["cumb_done"], n * N_HEAD + first + 2)
                    if h == 0 and not first_tile:
                        act.wait_ge(S["diag_done"], 4 * n)
                    for c in range(C):
                        nc.scalar.activation(lm[:, h, c, :], cum_ps[:, (h % 2) * T + c * P:(h % 2) * T + (c + 1) * P],
                                             ACT.Relu, bias=cum[:, c, h:h + 1], scale=-1.0)\
                            .then_inc(S["relu_done"], 1)
                act.wait_ge(S["relu_done"], (n * N_HEAD + first + 2) * C)
                v = lm[:, first:first + 2, :, :].rearrange("p h c l -> p (h c l)")
                nc.scalar.activation(v, v, ACT.Exp, scale=-1.0).then_inc(S["exp_done"], 1)

            def z_tanh(n, i, first_tile):
                c, h = CH[i]
                act.wait_ge(S["z_done"], n * 4 + i + 1)
                if i == 0 and first_tile:
                    act.wait_ge(S["wo_lo_set"], XT)
                elif i == 0:
                    act.wait_ge(S["y_done"], 4 * n)
                nc.scalar.activation(gz[:, c, h * 512:(h + 1) * 512], z_ps[i][:, :], ACT.Tanh, scale=0.5)\
                    .then_inc(S["tz_done"], 1)

            def squares(n, c):
                act.wait_ge(S["y_done"], n * 4 + 3 + c)
                nc.scalar.activation(xd[:, c, :], x_tok[:, c, :], ACT.Square, accum_out=ssq[:, c:c + 1])\
                    .then_inc(S["sq_done"], 1)

            def y_high(n, c):
                for r in range(2):
                    act.wait_ge(S["y_turned"], n * 4 + 2 * c + r + 1)
                    if c and r == 0:
                        act.wait_ge(S["out_done"], n * C + c)
                    nc.scalar.activation(y_hi[:, 4 * r:4 * r + 4, :],
                                         turn_ps[r][:, :].rearrange("p (j t) -> p j t", t=P), ACT.Copy)\
                        .then_inc(S["yhi_done"], 1)

            def body(n, first_tile, last_tile):
                act.wait_ge(S["dt_done"], n + 1)
                if not first_tile:
                    act.wait_ge(S["cumt_done"], n)
                nc.scalar.activation(dt_raw[:, :], dt_ps, ACT.Identity, bias=dtb[:, 0:1]).then_inc(S["dtraw_done"], 1)
                act.wait_ge(S["dtt_done"], n + 1)
                if not first_tile:
                    act.wait_ge(S["dt_set"], n)
                nc.scalar.activation(sp[:, 0, :], dtt_ps, ACT.Abs).then_inc(S["sp_act"], 1)
                act.wait_ge(S["sp_act"], 2 * n + 1)
                nc.scalar.activation(sp[:, 1, :], sp[:, 0, :], ACT.Exp, scale=-1.0).then_inc(S["sp_act"], 1)
                conv_in(n, 0, first_tile)
                if not first_tile:
                    y_high(n - 1, 0)
                conv_in(n, 1, first_tile)
                if not first_tile:
                    squares(n - 1, 0)
                act.wait_ge(S["cumr_done"], n + 1)
                if not first_tile:
                    act.wait_ge(S["cumb_done"], n * N_HEAD)
                    act.wait_ge(S["cumt_done"], n)
                nc.scalar.activation(cum_parts[:, :], cumr_ps, ACT.Copy).then_inc(S["cumhi_done"], 1)
                nc.scalar.activation(cum_rows[0:N_HEAD, :], small[0:N_HEAD, 0:T], ACT.Copy).then_inc(S["cumrows_done"], 1)
                z_tanh(n, 0, first_tile)
                conv_tanh(n, 0, first_tile)
                if not first_tile:
                    squares(n - 1, 1)
                act.wait_ge(S["cumt_done"], n + 1)
                if not first_tile:
                    act.wait_ge(S["relu_done"], n * N_HEAD * C)
                    act.wait_ge(S["tail_set"], 2 * n)
                nc.scalar.activation(cum[:, :, :].rearrange("p c h -> p (c h)"), cumt_ps, ACT.Copy)\
                    .then_inc(S["cum_set"], 1)
                if not first_tile:
                    act.wait_ge(S["part_off"], 4 * n)
                nc.scalar.activation(grow[:, :, :].rearrange("p c h -> p (c h)"), cumt_ps, ACT.Exp)\
                    .then_inc(S["grow_set"], 1)
                conv_tanh(n, 1, first_tile)
                conv_in(n, 2, first_tile)
                act.wait_ge(S["last_done"], n + 1)
                if not first_tile:
                    act.wait_ge(S["decayed"], 4 * n)
                nc.scalar.activation(chunk_decay[:, :, :].rearrange("p c h -> p (c h)"), last_ps, ACT.Exp)\
                    .then_inc(S["chunk_set"], 1)
                act.wait_ge(S["tail_set"], 2 * (n + 1))
                if not first_tile:
                    act.wait_ge(S["xdd_done"], n * XT * C)
                nc.scalar.activation(tail_decay[:, :, :], tail[:, :, :], ACT.Exp, scale=-1.0)\
                    .then_inc(S["taild_set"], 1)
                if not first_tile:
                    y_high(n - 1, 1)
                decay_heads(n, 0, first_tile)
                conv_in(n, 3, first_tile)
                conv_tanh(n, 2, first_tile)
                act.wait_ge(S["pair_done"], n * (XT + 2) + 1)
                if not first_tile:
                    act.wait_ge(S["st_done"], 4 * n)
                nc.scalar.activation(b_tok[:, :, :], pair_ps[0].rearrange("p (c d) -> p c d", d=P), ACT.Copy)\
                    .then_inc(S["pair_copied"], 1)
                decay_heads(n, 2, first_tile)
                conv_in(n, 4, first_tile)
                conv_tanh(n, 3, first_tile)
                for q in range(4, 10):
                    if q > 4:
                        conv_in(n, q, first_tile)
                    decay_heads(n, 2 * q - 4, first_tile)
                    if q == 7:
                        z_tanh(n, 1, first_tile)
                    x_copy(n, q - 4, first_tile)
                    conv_tanh(n, q, first_tile)
                x_copy(n, 6, first_tile)
                z_tanh(n, 2, first_tile)
                x_copy(n, 7, first_tile)
                z_tanh(n, 3, first_tile)
                if not last_tile:
                    high(n + 1, 0)
                    high(n + 1, 1)

            act.wait_ge(ahead.w_in_loaded, 16 * KD)
            for k in range(KD):
                weight_high(k)
            nc.scalar.activation(w_dt[:, :, 0:N_HEAD], w_in_raw[:, :, W_DT:], ACT.Copy).then_inc(S["w_hi_set"], 1)
            high(0, 0, first_tile=True)
            high(0, 1)
            head_values()
            act.wait_ge(S["taps_halved"], 3)
            act.wait_ge(S["wo_loaded"], 32)
            for j in range(XT):
                nc.scalar.activation(wo_hi[:, j, :], wo_raw[j // 4][:, j % 4, :], ACT.Copy,
                                     scale=norm_cols[:, j:j + 1]).then_inc(S["wo_hi_set"], 1)
            body(0, True, False)
            with act.Fori(1, N - 1) as n:
                body(n, False, False)
            body(N - 1, False, True)
            for c in range(C):
                squares(N - 1, c)
                y_high(N - 1, c)

        @block.vector
        def _(dve):
            def split_low(j):
                dve.wait_ge(S["wo_hi_set"], j + 1)
                nc.vector.scalar_tensor_tensor(wo_lo[:, j, :], wo_raw[j // 4][:, j % 4, :], norm_cols[:, j:j + 1],
                                               wo_hi[:, j, :].bitcast(F32), ALU.mult, ALU.subtract)\
                    .then_inc(S["wo_lo_set"], 1)

            def low(n, c):
                dve.wait_ge(S["xhi_done"], n * C + c + 1)
                v = slice(c * P, (c + 1) * P)
                nc.vector.tensor_tensor(x_lo[:, :, v], x[:, :, v], x_hi[:, :, v].bitcast(F32), ALU.subtract)\
                    .then_inc(S["xlo_done"], 1)

            def conv_tap(n, q, i):
                t = 2 - i
                j = ORDER[q]
                if i:
                    dve.wait_ge(S["tap_done"], (n * NT + q) * 3 + i)
                else:
                    dve.wait_ge(S["acc_done"], n * NT + q + 1)
                nc.vector.scalar_tensor_tensor(acc[:, q % 2, :], raw[:, q % 2, t:t + T], taps[:, j, t:t + 1],
                                               acc[:, q % 2, :], ALU.mult, ALU.add).then_inc(S["tap_done"], 1)

            def conv_taps(n, q, between=()):
                for i in range(3):
                    conv_tap(n, q, i)
                    if i < len(between):
                        between[i]()

            def conv_out(n, q, first_tile):
                dve.wait_ge(S["tanh_done"], n * NT + q + 1)
                if q < 2 and not first_tile:
                    dve.wait_ge(S["off_done"], 4 * n)
                out = (bt, ct)[q][:, :] if q < 2 else act_x[:, q % 2, :]
                nc.vector.scalar_tensor_tensor(out, act_x[:, q % 2, :], 1.0, acc[:, q % 2, :], ALU.add, ALU.mult)\
                    .then_inc(S["conv_done"], 1)

            def x_dt(n, j, first_tile):
                dve.wait_ge(S["pair_copied"], n * (XT + 1) + j + 2)
                if j == 0 and not first_tile:
                    dve.wait_ge(S["sq_done"], C * n)
                src = x_tok[:, :, j * P:(j + 1) * P].rearrange("p c (h d) -> p c h d", d=HEAD)
                out = xd[:, :, j * P:(j + 1) * P].rearrange("p c (h d) -> p c h d", d=HEAD)
                w = dtv[:, :, 2 * j:2 * j + 2].unsqueeze(-1).to_broadcast([P, C, 2, HEAD])
                nc.vector.tensor_tensor(out, src, w, ALU.mult).then_inc(S["xd_done"], 1)

            def weight_low(k):
                dve.wait_ge(S["w_hi_set"], k + 1)
                nc.vector.tensor_tensor(w_lo[:, k, :], w_in_raw[:, k, 0:W_DT], w_hi[:, k, :].bitcast(F32), ALU.subtract)\
                    .then_inc(S["w_lo_set"], 1)

            def softplus(n, between):
                base = [n * 14]
                count = [0]

                def step(ins):
                    base[0] = base[0] + 1
                    count[0] += 1
                    ins.then_inc(S["sp_step"], 1)
                    for work in between.get(count[0], ()):
                        work()
                    dve.wait_ge(S["sp_step"], base[0])

                e, s, s2, r, q = (sp[:, i, :] for i in (1, 2, 3, 4, 5))
                dve.wait_ge(S["sp_act"], 2 * (n + 1))
                step(nc.vector.tensor_scalar(r, e, 2.0, None, ALU.add))
                step(nc.vector.reciprocal(q, r))
                step(nc.vector.tensor_tensor(s, e, q, ALU.mult))
                step(nc.vector.tensor_tensor(s2, s, s, ALU.mult))
                step(nc.vector.tensor_scalar(q, s2, 1.0 / 17, None, ALU.mult))
                for odd in (15, 13, 11, 9, 7, 5, 3):
                    step(nc.vector.scalar_tensor_tensor(q, q, 1.0 / odd, s2, ALU.add, ALU.mult))
                step(nc.vector.scalar_tensor_tensor(q, q, 1.0, s, ALU.add, ALU.mult))
                step(nc.vector.tensor_scalar(r, dtt_ps, 0.0, None, ALU.max))
                nc.vector.scalar_tensor_tensor(dtv[:, :, :].rearrange("p c h -> p (c h)"), q, 2.0, r, ALU.mult,
                                               ALU.add).then_inc(S["dt_set"], 1)
                dve.wait_ge(S["dt_set"], n + 1)
                for start in (0, LO):
                    nc.vector.tensor_tensor(a_dup[:, :, start:start + N_HEAD], dtv[:, :, :],
                                            head_params[:, 0:N_HEAD].unsqueeze(1).to_broadcast([P, C, N_HEAD]),
                                            ALU.mult).then_inc(S["a_set"], 1)

            def z_gate(n, i):
                c, h = CH[i]
                dve.wait_ge(S["tz_done"], n * 4 + i + 1)
                v = gz[:, c, h * 512:(h + 1) * 512]
                nc.vector.scalar_tensor_tensor(v, v, 1.0, z_ps[i][:, :], ALU.add, ALU.mult)\
                    .then_inc(S["gz_done"], 1)

            def mask(n, i):
                c, h = CH[i]
                dve.wait_ge(S["exp_done"], n * HALF + (h + 1) * HALF // 2)
                v = lm[:, h * HALF:(h + 1) * HALF, c, :]
                nc.vector.tensor_tensor(v, v, gm[:, c:c + 1, :].to_broadcast([P, HALF, P]), ALU.mult)\
                    .then_inc(S["lm_done"], 1)

            def y_low(n, c, r):
                dve.wait_ge(S["yhi_done"], n * 4 + 2 * c + r + 1)
                nc.vector.tensor_tensor(y_lo[:, 4 * r:4 * r + 4, :],
                                        turn_ps[r][:, :].rearrange("p (j t) -> p j t", t=P),
                                        y_hi[:, 4 * r:4 * r + 4, :].bitcast(F32), ALU.subtract)\
                    .then_inc(S["ylo_done"], 1)

            def finish(n, c):
                dve.wait_ge(S["rest_loaded"], 32 * (n + 1))
                dve.wait_ge(S["out_done"], n * C + c + 1)
                dve.wait_ge(S["rms_step"], n * 4 + 2 * c + 2)
                nc.vector.scalar_tensor_tensor(gate[:, c, :], out_ps[c][:, :], rms[:, c, 1:2], gate[:, c, :],
                                               ALU.mult, ALU.mult).then_inc(S["o_mult"], 1)

            def from_before(n, i, first_tile):
                c, h = CH[i]
                dve.wait_ge(S["off_done"], n * 4 + i + 1)
                dve.wait_ge(S["grow_kept"], n + 1)
                if i >= 2 or not first_tile:
                    dve.wait_ge(S["sum_done"], n * 4 + i - 1)
                nc.vector.tensor_tensor(part[:, i % 2, :].rearrange("p (h d) -> p h d", d=HEAD),
                                        off_ps[:, :].rearrange("p (h d) -> p h d", d=HEAD),
                                        heads(grow[:, c, h * HALF:(h + 1) * HALF]), ALU.mult)\
                    .then_inc(S["part_off"], 1)

            def add_state(n, i):
                h = CH[i][1]
                dve.wait_ge(S["st_done"], n * 4 + i + 1)
                dve.wait_ge(S["decayed"], n * 4 + i + 1)
                v = state[:, h * 512:(h + 1) * 512]
                nc.vector.tensor_tensor(v, v, state_ps[:, :], ALU.add).then_inc(S["state_set"], 1)

            def add_within(n, i):
                dve.wait_ge(S["part_off"], n * 4 + i + 1)
                dve.wait_ge(S["diag_done"], n * 4 + i + 1)
                nc.vector.tensor_tensor(part[:, i % 2, :], part[:, i % 2, :], diag_ps[:, :], ALU.add)\
                    .then_inc(S["part_sum"], 1)

            def body(n, first_tile, last_tile):
                def out(q):
                    return lambda: conv_out(n, q, first_tile)

                def xdt(j):
                    return lambda: x_dt(n, j, first_tile)

                between = {}
                if not first_tile:
                    between = {5: [lambda: y_low(n - 1, 0, 0)], 8: [lambda: y_low(n - 1, 0, 1)]}
                    dve.wait_ge(S["xd_done"], n * XT)
                    dve.wait_ge(S["cumr_done"], n)
                softplus(n, between)
                conv_taps(n, 0)
                dve.wait_ge(S["cumhi_done"], n + 1)
                dve.wait_ge(S["cumrows_done"], n + 1)
                nc.vector.tensor_tensor(cum_parts[LO:LO + N_HEAD, :], small[LO:LO + N_HEAD, 0:T],
                                        cum_parts[LO:LO + N_HEAD, :].bitcast(F32), ALU.subtract)\
                    .then_inc(S["cumlo_done"], 1)
                conv_taps(n, 1, [lambda: z_gate(n, 0), out(0)])
                dve.wait_ge(S["chunk_set"], n + 1)
                if not first_tile:
                    dve.wait_ge(S["taild_set"], n)
                flat = tail[:, :, :].rearrange("p c h -> p (c h)")
                nc.vector.tensor_tensor(flat, cum[:, :, :].rearrange("p c h -> p (c h)"), last_ps, ALU.subtract)\
                    .then_inc(S["tail_set"], 1)
                dve.wait_ge(S["tail_set"], 2 * n + 1)
                nc.vector.tensor_scalar(flat, flat, 0.0, None, ALU.max).then_inc(S["tail_set"], 1)
                conv_taps(n, 2, [out(1)])
                if not first_tile:
                    finish(n - 1, 0)
                    y_low(n - 1, 1, 0)
                    y_low(n - 1, 1, 1)
                conv_taps(n, 3, [out(2)])
                dve.wait_ge(S["pair_done"], n * (XT + 2) + 2)
                if not first_tile:
                    dve.wait_ge(S["lm_done"], 4 * n)
                nc.vector.tensor_tensor(gm[:, :, :], pair_ps[1].rearrange("p (c l) -> p c l", l=P),
                                        tri[:, :].unsqueeze(1).to_broadcast([P, C, P]), ALU.mult)\
                    .then_inc(S["gm_done"], 1)
                conv_taps(n, 4, [out(3)])
                conv_taps(n, 5, [xdt(0), out(4)])
                conv_taps(n, 6, [xdt(1), out(5)])
                mask(n, 0)
                conv_taps(n, 7, [xdt(2), out(6)])
                z_gate(n, 1)
                if not first_tile:
                    finish(n - 1, 1)
                conv_taps(n, 8, [xdt(3), out(7)])
                mask(n, 1)
                conv_taps(n, 9, [xdt(4), out(8)])
                from_before(n, 0, first_tile)
                conv_out(n, 9, first_tile)
                add_state(n, 0)
                x_dt(n, 5, first_tile)
                add_within(n, 0)
                x_dt(n, 6, first_tile)
                from_before(n, 1, first_tile)
                z_gate(n, 2)
                x_dt(n, 7, first_tile)
                mask(n, 2)
                add_state(n, 1)
                add_within(n, 1)
                from_before(n, 2, first_tile)
                add_state(n, 2)
                mask(n, 3)
                z_gate(n, 3)
                if not last_tile:
                    low(n + 1, 0)
                add_within(n, 2)
                from_before(n, 3, first_tile)
                if not last_tile:
                    low(n + 1, 1)
                add_state(n, 3)
                add_within(n, 3)

            dve.wait_ge(ahead.params_loaded, 16 * ahead.N_SMALL)
            nc.vector.tensor_scalar(taps[:, :, :], taps[:, :, :], 0.5, None, ALU.mult).then_inc(S["taps_halved"], 1)
            nc.vector.tensor_scalar(tap_bias[:, :], tap_bias[:, :], 0.5, None, ALU.mult).then_inc(S["taps_halved"], 1)
            nc.vector.tensor_scalar(dtb[:, :], dtb[:, :], 0.5, None, ALU.mult).then_inc(S["taps_halved"], 1)
            for k in range(KD):
                weight_low(k)
            dve.wait_ge(S["w_hi_set"], KD + 1)
            nc.vector.tensor_tensor(w_dt[:, :, N_HEAD:], w_in_raw[:, :, W_DT:], w_dt[:, :, 0:N_HEAD].bitcast(F32),
                                    ALU.subtract).then_inc(S["w_lo_set"], 1)
            low(0, 0)
            low(0, 1)
            dve.wait_ge(S["heads_exp"], 1)
            nc.vector.tensor_scalar(head_params[:, 0:N_HEAD], head_params[:, 0:N_HEAD], -1.0, None, ALU.mult)\
                .then_inc(S["heads_set"], 1)
            dve.wait_ge(S["heads_set"], 2)
            dve.wait_ge(S["taps_halved"], 3)
            dve.wait_ge(S["consts"], 7 + n_batch)
            for j in range(XT):
                split_low(j)
            body(0, True, False)
            with dve.Fori(1, N - 1) as n:
                body(n, False, False)
            body(N - 1, False, True)
            for c in range(C):
                y_low(N - 1, c, 0)
                y_low(N - 1, c, 1)
                finish(N - 1, c)

        @block.tensor
        def _(pe):
            def product(out, ks, blocks, lhs_hi, lhs_lo, rhs_hi, rhs_lo):
                pairs = [(lhs_hi, rhs_hi), (lhs_hi, rhs_lo), (lhs_lo, rhs_hi)]
                for k in ks:
                    for j, (a, b) in enumerate(pairs):
                        last = nc.tensor.matmul(out, a(k), b(k), start=(k == 0 and j == 0),
                                                stop=(k == blocks - 1 and j == 2))
                return last

            def by_channel(out, lo, width):
                return product(out, range(KD), KD, lambda k: w_hi[:, k, lo:lo + width], lambda k: w_lo[:, k, lo:lo + width],
                               lambda k: x_hi[:, k, :], lambda k: x_lo[:, k, :])

            def project(n, q, first_tile):
                if q >= 2:
                    pe.wait_ge(S["acc_done"], n * NT + q - 1)
                elif not first_tile:
                    pe.wait_ge(S["gz_done"], 4 * n - 1 + q)
                by_channel(proj_ps[q % 2][:, 0:T], W_X + ORDER[q] * P, P).then_inc(S["proj_done"], 1)

            def pair(i, src):
                for c in range(C):
                    last = nc.tensor.transpose(pair_ps[i][:, c * P:(c + 1) * P], src[:, c * P:(c + 1) * P],
                                               ident[:, :])
                last.then_inc(S["pair_done"], 1)

            def x_pair(n, j):
                pe.wait_ge(S["conv_done"], n * NT + j + 3)
                if j == 1:
                    pe.wait_ge(S["gm_done"], n + 1)
                elif j == 0:
                    pe.wait_ge(S["pair_copied"], n * (XT + 1) + 1)
                else:
                    pe.wait_ge(S["pair_copied"], n * (XT + 1) + j)
                pair(j % 2, act_x[:, j % 2, :])

            def spread(n, first):
                if first:
                    pe.wait_ge(S["relu_done"], (n * N_HEAD + first) * C)
                else:
                    pe.wait_ge(S["chunk_set"], n + 1)
                    pe.wait_ge(S["tail_set"], 2 * n + 1)
                for h in (first, first + 1):
                    nc.tensor.matmul(cum_ps[:, (h % 2) * T:(h % 2 + 1) * T],
                                     pick[:, h:h + 1].to_broadcast([LO + N_HEAD, P]), cum_parts[:, :],
                                     start=True, stop=True).then_inc(S["cumb_done"], 1)

            def z_part(n, i, first_tile):
                c, h = CH[i]
                if i == 0 and not first_tile:
                    pe.wait_ge(S["state_set"], 4 * n)
                elif i == 1 and not first_tile:
                    pe.wait_ge(S["o_mult"], C * n - 1)
                elif i >= 2:
                    pe.wait_ge(S["acc_done"], n * NT + NT - 3 + i)
                v = slice(c * P, (c + 1) * P)
                cols = slice(h * 512, (h + 1) * 512)
                product(z_ps[i][:, :], range(KD), KD, lambda k: x_hi[:, k, v], lambda k: x_lo[:, k, v],
                        lambda k: w_hi[:, k, cols], lambda k: w_lo[:, k, cols]).then_inc(S["z_done"], 1)

            def off(n, i):
                c, h = CH[i]
                if i == 0:
                    pe.wait_ge(S["gz_done"], n * 4 + 2)
                else:
                    pe.wait_ge(S["part_off"], n * 4 + i)
                if c:
                    pe.wait_ge(S["state_set"], n * 4 + i)
                nc.tensor.matmul(off_ps[:, :], ct[:, c * P:(c + 1) * P], state[:, h * 512:(h + 1) * 512],
                                 start=True, stop=True).then_inc(S["off_done"], 1)

            def new_state(n, i):
                c, h = CH[i]
                pe.wait_ge(S["xdd_done"], n * XT * C + (h + 1) * XT)
                if i:
                    pe.wait_ge(S["state_set"], n * 4 + i)
                nc.tensor.matmul(state_ps[:, :], b_tok[:, c, :], xdd[:, c, h * 512:(h + 1) * 512],
                                 start=True, stop=True).then_inc(S["st_done"], 1)

            def diag(n, i, first_tile):
                c, h = CH[i]
                pe.wait_ge(S["lm_done"], n * 4 + i + 1)
                if i:
                    pe.wait_ge(S["part_sum"], n * 4 + i)
                elif not first_tile:
                    pe.wait_ge(S["o_mult"], C * n)
                for m in range(HALF - 1, -1, -1):
                    lead = 32 if m else 0
                    lo = m * HEAD - lead
                    hi = (m + 1) * HEAD
                    last = nc.tensor.matmul(diag_ps[:, lo:hi], lm[:, h * HALF + m, c, :],
                                            xd[:, c, h * 512 + lo:h * 512 + hi], start=True, stop=True)
                last.then_inc(S["diag_done"], 1)

            def y_turn(n, c):
                pe.wait_ge(S["y_done"], n * 4 + 3 + c)
                if c:
                    pe.wait_ge(S["ylo_done"], n * 4 + 2)
                else:
                    pe.wait_ge(S["pair_copied"], (n + 1) * (XT + 1))
                for r in range(2):
                    for j in range(4):
                        lo = (4 * r + j) * P
                        last = nc.tensor.transpose(turn_ps[r][:, j * P:(j + 1) * P], x_tok[:, c, lo:lo + P],
                                                   ident[:, :])
                    last.then_inc(S["y_turned"], 1)

            def output(n, c, blocks):
                if blocks[0] == 0:
                    pe.wait_ge(S["ylo_done"], n * 4 + 2 * c + 2)
                    pe.wait_ge(S["part_sum" if c else "part_off"], 4 * (n + 1))
                last = product(out_ps[c][:, :], blocks, XT, lambda j: y_hi[:, j, :], lambda j: y_lo[:, j, :],
                               lambda j: wo_hi[:, j, :], lambda j: wo_lo[:, j, :])
                if blocks[-1] == XT - 1:
                    last.then_inc(S["out_done"], 1)

            def body(n, first_tile, last_tile):
                pe.wait_ge(S["xlo_done"], (n + 1) * C)
                if not first_tile:
                    pe.wait_ge(S["relu_done"], n * N_HEAD * C)
                for k in range(KD):
                    nc.tensor.matmul(dt_ps, w_dt[:, k, :], x_hi[:, k, :], start=(k == 0), stop=False)
                    last = nc.tensor.matmul(small[0:N_HEAD, 0:T], w_dt[:, k, 0:N_HEAD], x_lo[:, k, :], start=False,
                                            stop=(k == KD - 1))
                last.then_inc(S["dt_done"], 1)
                project(n, 0, first_tile)
                pe.wait_ge(S["dtraw_done"], n + 1)
                apart(pe, S["pe_passed"])
                for c in range(C):
                    last = nc.tensor.matmul(small[:, 256 + c * N_HEAD:256 + (c + 1) * N_HEAD],
                                            dt_raw[:, c * P:(c + 1) * P], both[:, :], start=True, stop=True)
                last.then_inc(S["dtt_done"], 1)
                if not first_tile:
                    y_turn(n - 1, 0)
                project(n, 1, first_tile)
                z_part(n, 0, first_tile)
                if not first_tile:
                    output(n - 1, 0, range(0, 3))
                pe.wait_ge(S["a_set"], 2 * (n + 1))
                for c in range(C):
                    last = nc.tensor.matmul(small[0:LO + N_HEAD, c * P:(c + 1) * P], a_dup[:, c, :], tri[:, :],
                                            start=True, stop=True)
                last.then_inc(S["cumr_done"], 1)
                if not first_tile:
                    output(n - 1, 0, range(3, 5))
                project(n, 2, first_tile)
                pe.wait_ge(S["cumrows_done"], n + 1)
                pe.wait_ge(S["cumlo_done"], n + 1)
                apart(pe, S["pe_passed"])
                for c in range(C):
                    last = nc.tensor.transpose(small[:, 288 + c * N_HEAD:288 + (c + 1) * N_HEAD],
                                               cum_rows[0:N_HEAD, c * P:(c + 1) * P], ident[0:N_HEAD, 0:N_HEAD])
                last.then_inc(S["cumt_done"], 1)
                if not first_tile:
                    y_turn(n - 1, 1)
                pe.wait_ge(S["cum_set"], n + 1)
                pe.wait_ge(S["grow_set"], n + 1)
                nc.tensor.matmul(last_ps, ident[:, P - 1:P].to_broadcast([P, P]), cum[:, :, :].rearrange("p c h -> p (c h)"),
                                 start=True, stop=True).then_inc(S["last_done"], 1)
                if not first_tile:
                    output(n - 1, 0, range(5, XT))
                spread(n, 0)
                project(n, 3, first_tile)
                project(n, 4, first_tile)
                spread(n, 2)
                if not first_tile:
                    pe.wait_ge(S["ylo_done"], 4 * n)
                pe.wait_ge(S["conv_done"], n * NT + 1)
                pair(0, bt)
                pe.wait_ge(S["conv_done"], n * NT + 2)
                for c in range(C):
                    tok = slice(c * P, (c + 1) * P)
                    last = nc.tensor.matmul(pair_ps[1][:, tok], bt[:, tok], ct[:, tok], start=True, stop=True)
                last.then_inc(S["pair_done"], 1)
                if not first_tile:
                    output(n - 1, 1, range(0, 3))
                spread(n, 4)
                x_pair(n, 0)
                project(n, 5, first_tile)
                if not first_tile:
                    output(n - 1, 1, range(3, 6))
                spread(n, 6)
                x_pair(n, 1)
                project(n, 6, first_tile)
                if not first_tile:
                    output(n - 1, 1, range(6, XT))
                spread(n, 8)
                x_pair(n, 2)
                project(n, 7, first_tile)
                spread(n, 10)
                z_part(n, 1, first_tile)
                x_pair(n, 3)
                project(n, 8, first_tile)
                spread(n, 12)
                off(n, 0)
                x_pair(n, 4)
                project(n, 9, first_tile)
                spread(n, 14)
                x_pair(n, 5)
                new_state(n, 0)
                diag(n, 0, first_tile)
                x_pair(n, 6)
                z_part(n, 2, first_tile)
                off(n, 1)
                x_pair(n, 7)
                new_state(n, 1)
                diag(n, 1, first_tile)
                off(n, 2)
                new_state(n, 2)
                z_part(n, 3, first_tile)
                diag(n, 2, first_tile)
                off(n, 3)
                new_state(n, 3)
                diag(n, 3, first_tile)

            pe.wait_ge(ahead.params_loaded, 16 * ahead.N_SMALL)
            pe.wait_ge(S["consts"], 7 + n_batch)
            pe.wait_ge(S["pool_step"], 8)
            nc.tensor.matmul(cum_ps[:, 0:2 * N_HEAD], ones_row[:, :], head_rows[:, :], start=True, stop=True)\
                .then_inc(S["head_ps"], 1)
            pe.wait_ge(S["w_lo_set"], KD + 1)
            pe.wait_ge(S["heads_set"], 2)
            body(0, True, False)
            pe.wait_ge(S["wo_lo_set"], XT)
            with pe.Fori(1, N - 1) as n:
                body(n, False, False)
            body(N - 1, False, True)
            for c in range(C):
                y_turn(N - 1, c)
                output(N - 1, c, range(XT))


def build_program(nc, u, w_in, conv_w, conv_b, dt_bias, a_log, d_skip, norm_w, w_out, w_r, w_k, w_v, mu_r, mu_k, out):
    n_batch, length, _ = u.shape
    n_tok = n_batch * length
    u_rows = u.rearrange("b l d -> (b l) d")
    out_rows = out.rearrange("b l d -> (b l) d")
    gate_rows = nc.dram_tensor("gate_rows", (n_tok, DM), F32, kind="Internal").ap()
    x_cols = nc.dram_tensor("x_cols", (DM, n_tok), F32, kind="Internal").ap()
    ctx = ExitStack()
    with ctx:
        ident = ctx.enter_context(nc.sbuf_tensor("ident", [P, P], F32))
        ahead = Ahead(nc, ctx)
        ident_step = ctx.enter_context(nc.semaphore("ident_step"))
        with nc.Block() as block:
            @block.gpsimd
            def _(pool):
                pool.memset(ident[:, :], 0.0).then_inc(ident_step, 1)
                pool.wait_ge(ident_step, 1)
                pool.affine_select(out=ident[:, :], in_=ident[:, :], compare_op=ALU.not_equal, fill=1.0, base=0,
                                   pattern=[[-1, P]], channel_multiplier=1).then_inc(ident_step, 1)
                pool.wait_ge(ident_step, 2)
        ffn_phase(nc, u_rows, w_r, w_k, w_v, mu_r, mu_k, gate_rows, x_cols, ident,
                  lambda sync: ahead.load(sync, w_in, conv_w, conv_b, dt_bias, a_log, d_skip, norm_w), n_tok, n_batch)
        ssm_phase(nc, u_rows, x_cols, ahead, w_out, gate_rows, out_rows, ident, n_tok, n_batch)


INPUTS = ["L0_attn_u", "L0_attn_W_in", "L0_attn_conv_w", "L0_attn_conv_b", "L0_attn_dt_bias", "L0_attn_A_log",
          "L0_attn_D", "L0_attn_norm_w", "L0_attn_W_out", "L0_ffn_W_r", "L0_ffn_W_k", "L0_ffn_W_v", "L0_ffn_mu_r",
          "L0_ffn_mu_k"]


def kernel(**inputs):
    import numpy as np
    import concourse.bacc as bacc
    from concourse.bass_utils import run_bass_kernel_spmd

    nc = bacc.Bacc("TRN2", target_bir_lowering=False, num_devices=1)
    arrays, args = {}, []
    for name in INPUTS:
        a = np.ascontiguousarray(inputs[name])
        arrays[f"in_{name}"] = a
        args.append(nc.dram_tensor(f"in_{name}", a.shape, mybir.dt.from_np(a.dtype), kind="ExternalInput").ap())
    shape = arrays["in_L0_attn_u"].shape
    args.append(nc.dram_tensor("out", shape, F32, kind="ExternalOutput").ap())
    build_program(nc, *args)
    result = run_bass_kernel_spmd(nc, [arrays], core_ids=[0])
    return result.results[0]["out"]
```
